# Optimizing a Trainium2 kernel written in Bass

```python
import numpy as np
import jax
import jax.numpy as jnp

def _softmax(x, axis=-1):
    return jax.nn.softmax(x, axis=axis)

def _gelu(x):
    return jax.nn.gelu(x, approximate=True)

def _silu(x):
    return jax.nn.silu(x)

def _sigmoid(x):
    return jax.nn.sigmoid(x)

def _layernorm(x, axis=-1, eps=1e-05):
    m = jnp.mean(x, axis=axis, keepdims=True)
    v = jnp.var(x, axis=axis, keepdims=True)
    return (x - m) / jnp.sqrt(v + eps)

def _scatter_add(tgt, idx, src, axis=0):
    return tgt.at[idx].add(src)

def _segment_sum(src, seg, n):
    return jax.ops.segment_sum(src, seg, n)
kernel_name = 'mk_gnn_preln_d4_gnn_r16_a6de11'

def setup_inputs(seed: int=0):
    np.random.seed(seed)
    _w = jnp.asarray

    def _rec_inputs():
        import jax
        import jax.numpy as jnp
        _gk = jax.random.key(seed)
        x = -0.000202 + 1 * jax.random.normal(jax.random.fold_in(_gk, 1), (3125, 160), jnp.float32)
        _s = jax.random.randint(jax.random.fold_in(_gk, 2), (50000,), 0, 3125, jnp.int32)
        _d = jax.random.randint(jax.random.fold_in(_gk, 3), (50000,), 0, 3125, jnp.int32)
        _loop = jnp.arange(3125, dtype=jnp.int32)
        src = jnp.concatenate([_s, _d, _loop])
        dst = jnp.concatenate([_d, _s, _loop])
        _o = jnp.argsort(dst, stable=True)
        src = src[_o]
        dst = dst[_o]
        edge_attr_16 = -0.000191324 + 0.999809 * jax.random.normal(jax.random.fold_in(_gk, 12), (103125, 16), jnp.float32)
        edge_attr_3 = 0.00262751 + 0.999568 * jax.random.normal(jax.random.fold_in(_gk, 13), (103125, 3), jnp.float32)
        edge_attr_4 = 0.0012443 + 1.0001 * jax.random.normal(jax.random.fold_in(_gk, 14), (103125, 4), jnp.float32)
        edge_attr_64 = 0.000127647 + 1.00004 * jax.random.normal(jax.random.fold_in(_gk, 15), (103125, 64), jnp.float32)
        node_vec1 = jax.random.uniform(jax.random.fold_in(_gk, 17), (3125, 1), jnp.float32, 0.0, 1)
        return (x, src, dst, edge_attr_16, edge_attr_3, edge_attr_4, edge_attr_64, node_vec1)
    x, src, dst, edge_attr_16, edge_attr_3, edge_attr_4, edge_attr_64, node_vec1 = _rec_inputs()

    def _L0_gnn_setup():
        import jax, jax.numpy as jnp
        import numpy as np
        N, E = (2500, 40000)
        S_IN, V_IN = (64, 32)
        S_MID, V_MID = (96, 128)
        S_OUT, V_OUT = (96, 32)
        R = 64
        FC_HID = 64
        W_NUMEL = 64 + 64 + 32 + 32 + 32
        NUM_NEIGHBORS = 16.0

        def _inv(d):
            return 1.0 / jnp.sqrt(jnp.float32(d))

        def _forward(node_features, node_attr, edge_attr, edge_scalars, lin1_ws, lin1_wv, fc_w1, fc_w2, sc_ws, sc_wv, lin2_ws, lin2_wv, edge_src, edge_dst):
            n = node_features.shape[0]
            s = node_features[:, :S_IN]
            v = node_features[:, S_IN:].reshape(n, V_IN, 3)
            a = node_attr
            sc_s = s @ sc_ws * a * _inv(S_IN)
            sc_v = jnp.einsum('nci,cd->ndi', v, sc_wv) * a[:, :, None] * _inv(V_IN)
            h_s = s @ lin1_ws * a * _inv(S_IN)
            h_v = jnp.einsum('nci,cd->ndi', v, lin1_wv) * a[:, :, None] * _inv(V_IN)
            hid = jax.nn.silu(edge_scalars @ fc_w1 * _inv(R))
            w = hid @ fc_w2 * _inv(FC_HID)
            w1, w2, w3, w4, w5 = jnp.split(w, [64, 128, 160, 192], axis=-1)
            es = h_s[edge_src]
            ev = h_v[edge_src]
            e0 = edge_attr[:, :1]
            e1 = edge_attr[:, 1:4]
            m_s1 = w1 * es * e0
            m_s2 = w4 * jnp.einsum('eci,ei->ec', ev, e1) * _inv(3)
            m_v1 = (w2 * es)[:, :, None] * e1[:, None, :]
            m_v2 = w3[:, :, None] * ev * e0[:, :, None]
            m_v3 = w5[:, :, None] * jnp.cross(ev, e1[:, None, :]) * _inv(2)
            mid_s = jnp.concatenate([m_s1, m_s2], axis=-1)
            mid_v = jnp.concatenate([m_v1, m_v2, m_v3], axis=1)
            inv_nn = 1.0 / jnp.sqrt(jnp.float32(NUM_NEIGHBORS))
            agg_s = jax.ops.segment_sum(mid_s, edge_dst, num_segments=n) * inv_nn
            agg_v = jax.ops.segment_sum(mid_v, edge_dst, num_segments=n) * inv_nn
            o_s = agg_s @ lin2_ws * a * _inv(S_MID)
            o_v = jnp.einsum('nci,cd->ndi', agg_v, lin2_wv) * a[:, :, None] * _inv(V_MID)
            pre_s = sc_s + o_s
            pre_v = sc_v + o_v
            scalars = jax.nn.silu(pre_s[:, :64])
            gates = jax.nn.sigmoid(pre_s[:, 64:96])
            gated = gates[:, :, None] * pre_v
            return jnp.concatenate([scalars, gated.reshape(n, 3 * V_OUT)], axis=-1)
        key = jax.random.key(seed)
        ks = jax.random.split(key, 13)
        return {'node_features': jax.random.normal(ks[0], (N, S_IN + 3 * V_IN), jnp.float32), 'node_attr': jnp.ones((N, 1), jnp.float32), 'edge_src': jax.random.randint(ks[1], (E,), 0, N), 'edge_dst': jax.random.randint(ks[2], (E,), 0, N), 'edge_attr': jax.random.normal(ks[3], (E, 4), jnp.float32), 'edge_scalars': jax.random.normal(ks[4], (E, R), jnp.float32), 'lin1_ws': jax.random.normal(ks[5], (S_IN, S_IN), jnp.float32), 'lin1_wv': jax.random.normal(ks[6], (V_IN, V_IN), jnp.float32), 'fc_w1': jax.random.normal(ks[7], (R, FC_HID), jnp.float32), 'fc_w2': jax.random.normal(ks[8], (FC_HID, W_NUMEL), jnp.float32), 'sc_ws': jax.random.normal(ks[9], (S_IN, S_OUT), jnp.float32), 'sc_wv': jax.random.normal(ks[10], (V_IN, V_OUT), jnp.float32), 'lin2_ws': jax.random.normal(ks[11], (S_MID, S_OUT), jnp.float32), 'lin2_wv': jax.random.normal(ks[12], (V_MID, V_OUT), jnp.float32)}
    _L0_gnn_all = _L0_gnn_setup()
    _L0_gnn_in = {k: v for k, v in _L0_gnn_all.items() if k in ('lin1_ws', 'lin1_wv', 'fc_w1', 'fc_w2', 'sc_ws', 'sc_wv', 'lin2_ws', 'lin2_wv')}
    del _L0_gnn_all

    def _L1_gnn_setup():
        import jax, jax.numpy as jnp
        import numpy as np
        N = 1250
        E = 20000
        MUL0 = 64
        MUL1 = 32
        FC_IN = 16
        FC_H = 64
        WNUM = 192
        key = jax.random.key(seed)
        ks = jax.random.split(key, 16)
        return {'x': jax.random.normal(ks[0], (N, MUL0 + 3 * MUL1), jnp.float32), 'node_attr': jnp.ones((N, 1), jnp.float32), 'edge_scalars': jax.random.normal(ks[1], (E, FC_IN), jnp.float32), 'edge_attr_sh': jax.random.normal(ks[2], (E, 4), jnp.float32), 'edge_src': jax.random.randint(ks[3], (E,), 0, N), 'edge_dst': jax.random.randint(ks[4], (E,), 0, N), 'Wfc1': jax.random.normal(ks[5], (FC_IN, FC_H), jnp.float32), 'Wfc2': jax.random.normal(ks[6], (FC_H, WNUM), jnp.float32), 'Wsc0': jax.random.normal(ks[7], (MUL0, MUL0), jnp.float32), 'Wsc1': jax.random.normal(ks[8], (MUL1, MUL1), jnp.float32), 'Wl1_0': jax.random.normal(ks[9], (MUL0, MUL0), jnp.float32), 'Wl1_1': jax.random.normal(ks[10], (MUL1, MUL1), jnp.float32), 'Wl2_s': jax.random.normal(ks[11], (MUL0 + MUL1, MUL0), jnp.float32), 'Wl2_v': jax.random.normal(ks[12], (MUL0 + MUL1, MUL1), jnp.float32), 'Wa': 0.1 * jax.random.normal(ks[13], (MUL0 + MUL1, 1), jnp.float32)}
    _L1_gnn_all = _L1_gnn_setup()
    _L1_gnn_in = {k: v for k, v in _L1_gnn_all.items() if k in ('Wfc1', 'Wfc2', 'Wsc0', 'Wsc1', 'Wl1_0', 'Wl1_1', 'Wl2_s', 'Wl2_v', 'Wa')}
    del _L1_gnn_all

    def _L2_gnn_setup():
        import jax, jax.numpy as jnp
        import numpy as np
        N, E = (625, 10000)
        C0, C1 = (64, 32)
        H, A = (8, 8)
        H0, H1 = (8, 4)
        M0, M1 = (128, 64)
        NG, RH = (64, 64)
        WN = C0 + C0 + C1 + C1 + C1
        DS, DV = (C0 + C1, C0 + 2 * C1)
        EPS = 1e-05
        SQ3 = np.float32(np.sqrt(3.0))
        SQ2 = np.float32(np.sqrt(2.0))

        def _split(x):
            return (x[:, :C0], x[:, C0:].reshape(x.shape[0], C1, 3))

        def _merge(s, v):
            return jnp.concatenate([s, v.reshape(v.shape[0], -1)], axis=1)

        def _eq_ln(x, w0, b0, w1):
            s, v = _split(x)
            s = s - s.mean(axis=1, keepdims=True)
            s = s * jax.lax.rsqrt(jnp.square(s).mean(axis=1, keepdims=True) + EPS) * w0 + b0
            v = v * jax.lax.rsqrt(jnp.square(v).mean(axis=(1, 2), keepdims=True) + EPS) * w1[None, :, None]
            return (s, v)

        def _eq_lin(s, v, ws, bs, wv):
            return (s @ ws + bs, jnp.einsum('nud,uk->nkd', v, wv))

        def _ln(x, g, b):
            xc = x - x.mean(-1, keepdims=True)
            return xc * jax.lax.rsqrt(jnp.square(xc).mean(-1, keepdims=True) + EPS) * g + b

        def _smooth_leaky(x, alpha=0.2):
            return 0.5 * (1 + alpha) * x + 0.5 * (1 - alpha) * x * (2.0 * jax.nn.sigmoid(x) - 1.0)

        def _forward(node_input, node_attr, edge_vec, edge_scalars, edge_src, edge_dst, ln1_w0, ln1_b0, ln1_w1, ln2_w0, ln2_b0, ln2_w1, msrc_ws, msrc_wv, mdst_ws, mdst_bs, mdst_wv, rw1, rb1, rg1, rbe1, rw2, rb2, rg2, rbe2, rw3, roff, lin_ws, lin_bs, lin_wv, alpha_dot, proj_ws, proj_bs, proj_wv, f1_ws, f1_bs, f1_wv, f2_ws, f2_bs, f2_wv):
            n = node_input.shape[0]
            s, v = _eq_ln(node_input, ln1_w0, ln1_b0, ln1_w1)
            src_s = s @ msrc_ws
            src_v = jnp.einsum('nud,uk->nkd', v, msrc_wv)
            dst_s = s @ mdst_ws + mdst_bs
            dst_v = jnp.einsum('nud,uk->nkd', v, mdst_wv)
            ms = src_s[edge_src] + dst_s[edge_dst]
            mv = src_v[edge_src] + dst_v[edge_dst]
            h = jax.nn.silu(_ln(edge_scalars @ rw1 + rb1, rg1, rbe1))
            h = jax.nn.silu(_ln(h @ rw2 + rb2, rg2, rbe2))
            w = h @ rw3 + roff
            rhat = edge_vec * jax.lax.rsqrt(jnp.sum(jnp.square(edge_vec), -1, keepdims=True) + 1e-12)
            Y1 = SQ3 * rhat
            w1, w2, w3, w4, w5 = jnp.split(w, [C0, 2 * C0, 2 * C0 + C1, 2 * C0 + 2 * C1], axis=1)
            o0a = w1 * ms
            o0b = w4 * (jnp.einsum('eud,ed->eu', mv, Y1) / SQ3)
            o1a = (w2 * ms)[:, :, None] * Y1[:, None, :]
            o1b = w3[:, :, None] * mv
            o1c = w5[:, :, None] * (jnp.cross(mv, Y1[:, None, :]) / SQ2)
            ds = jnp.concatenate([o0a, o0b], axis=1)
            dv = jnp.concatenate([o1a, o1b, o1c], axis=1)
            ls, lv = _eq_lin(ds, dv, lin_ws, lin_bs, lin_wv)
            e = ls.shape[0]
            alpha = ls[:, :H * A].reshape(e, H, A)
            vs = ls[:, H * A:].reshape(e, H, H0)
            vv = lv.reshape(e, H, H1, 3)
            a = jnp.einsum('ehk,hk->eh', _smooth_leaky(alpha), alpha_dot)
            amax = jax.lax.stop_gradient(jax.ops.segment_max(a, edge_dst, num_segments=n))
            a = jnp.exp(a - amax[edge_dst])
            a = a / (jax.ops.segment_sum(a, edge_dst, num_segments=n)[edge_dst] + 1e-12)
            ns = jax.ops.segment_sum(vs * a[..., None], edge_dst, num_segments=n).reshape(n, H * H0)
            nv = jax.ops.segment_sum(vv * a[..., None, None], edge_dst, num_segments=n).reshape(n, H * H1, 3)
            ps, pv = _eq_lin(ns, nv, proj_ws, proj_bs, proj_wv)
            x = node_input + _merge(ps, pv)
            s2, v2 = _eq_ln(x, ln2_w0, ln2_b0, ln2_w1)
            a0 = node_attr[:, :1]
            fs, fv = _eq_lin(s2, v2, f1_ws, f1_bs, f1_wv)
            fs = fs * a0
            fv = fv * a0[:, :, None]
            sc = jax.nn.silu(fs[:, :M0])
            fv = fv * jax.nn.sigmoid(fs[:, M0:])[:, :, None]
            os_, ov = _eq_lin(sc, fv, f2_ws, f2_bs, f2_wv)
            os_ = os_ * a0
            ov = ov * a0[:, :, None]
            return x + _merge(os_, ov)
        key = jax.random.key(seed)
        ks = iter(jax.random.split(key, 24))

        def nrm(shape, fan):
            return jax.random.normal(next(ks), shape, jnp.float32) / np.float32(np.sqrt(fan))
        inp = {}
        inp['node_input'] = jax.random.normal(next(ks), (N, C0 + 3 * C1), jnp.float32)
        inp['node_attr'] = jnp.ones((N, 1), jnp.float32)
        inp['edge_vec'] = jax.random.normal(next(ks), (E, 3), jnp.float32)
        inp['edge_scalars'] = jax.random.uniform(next(ks), (E, NG), dtype=jnp.float32)
        inp['edge_src'] = jax.random.randint(next(ks), (E,), 0, N)
        inp['edge_dst'] = jax.random.randint(next(ks), (E,), 0, N)
        inp['ln1_w0'] = jnp.ones((C0,), jnp.float32)
        inp['ln1_b0'] = jnp.zeros((C0,), jnp.float32)
        inp['ln1_w1'] = jnp.ones((C1,), jnp.float32)
        inp['ln2_w0'] = jnp.ones((C0,), jnp.float32)
        inp['ln2_b0'] = jnp.zeros((C0,), jnp.float32)
        inp['ln2_w1'] = jnp.ones((C1,), jnp.float32)
        inp['msrc_ws'] = nrm((C0, C0), C0)
        inp['msrc_wv'] = nrm((C1, C1), C1)
        inp['mdst_ws'] = nrm((C0, C0), C0)
        inp['mdst_bs'] = jnp.zeros((C0,), jnp.float32)
        inp['mdst_wv'] = nrm((C1, C1), C1)
        inp['rw1'] = nrm((NG, RH), NG)
        inp['rb1'] = jnp.zeros((RH,), jnp.float32)
        inp['rg1'] = jnp.ones((RH,), jnp.float32)
        inp['rbe1'] = jnp.zeros((RH,), jnp.float32)
        inp['rw2'] = nrm((RH, RH), RH)
        inp['rb2'] = jnp.zeros((RH,), jnp.float32)
        inp['rg2'] = jnp.ones((RH,), jnp.float32)
        inp['rbe2'] = jnp.zeros((RH,), jnp.float32)
        inp['rw3'] = nrm((RH, WN), RH)
        inp['roff'] = 0.1 * jax.random.normal(next(ks), (WN,), jnp.float32)
        inp['lin_ws'] = nrm((DS, H * A + H * H0), DS)
        inp['lin_bs'] = jnp.zeros((H * A + H * H0,), jnp.float32)
        inp['lin_wv'] = nrm((DV, H * H1), DV)
        inp['alpha_dot'] = nrm((H, A), A)
        inp['proj_ws'] = nrm((H * H0, C0), H * H0)
        inp['proj_bs'] = jnp.zeros((C0,), jnp.float32)
        inp['proj_wv'] = nrm((H * H1, C1), H * H1)
        inp['f1_ws'] = nrm((C0, M0 + M1), C0)
        inp['f1_bs'] = jnp.zeros((M0 + M1,), jnp.float32)
        inp['f1_wv'] = nrm((C1, M1), C1)
        inp['f2_ws'] = nrm((M0, C0), M0)
        inp['f2_bs'] = jnp.zeros((C0,), jnp.float32)
        inp['f2_wv'] = nrm((M1, C1), M1)
        return inp
    _L2_gnn_all = _L2_gnn_setup()
    _L2_gnn_in = {k: v for k, v in _L2_gnn_all.items() if k in ('ln1_w0', 'ln1_b0', 'ln1_w1', 'ln2_w0', 'ln2_b0', 'ln2_w1', 'msrc_ws', 'msrc_wv', 'mdst_ws', 'mdst_bs', 'mdst_wv', 'rw1', 'rb1', 'rg1', 'rbe1', 'rw2', 'rb2', 'rg2', 'rbe2', 'rw3', 'roff', 'lin_ws', 'lin_bs', 'lin_wv', 'alpha_dot', 'proj_ws', 'proj_bs', 'proj_wv', 'f1_ws', 'f1_bs', 'f1_wv', 'f2_ws', 'f2_bs', 'f2_wv')}
    del _L2_gnn_all

    def _L3_gnn_setup():
        import jax, jax.numpy as jnp
        import numpy as np
        N_NODES = 625
        N_EDGES = 20000
        MUL0, MUL1 = (64, 32)
        EDGE_DIM = 64
        W_NUMEL = 224
        DENOM = 32.0
        SQRT3 = 3.0 ** 0.5
        INV_SQRT3 = 1.0 / SQRT3
        INV_SQRT2 = 2.0 ** (-0.5)

        def _forward(node_feature, edge_attr, edge_feature, W_skip0, W_skip1, W_nl0, W_nl1, W_fc1, W_fc2, W_out_s, W_out_v, edge_index):
            N = node_feature.shape[0]
            E = edge_attr.shape[0]
            s = node_feature[:, :MUL0]
            v = node_feature[:, MUL0:].reshape(N, MUL1, 3)
            skip_s = s @ W_skip0
            skip_v = jnp.einsum('nmi,mk->nki', v, W_skip1)
            s = s @ W_nl0
            v = jnp.einsum('nmi,mk->nki', v, W_nl1)
            rhat = edge_attr / jnp.linalg.norm(edge_attr, axis=-1, keepdims=True)
            sh1 = SQRT3 * rhat
            w = jax.nn.relu(edge_feature @ W_fc1) @ W_fc2
            w0, w1, w2, w3, w4 = jnp.split(w, [64, 128, 160, 192], axis=-1)
            src, dst = (edge_index[0], edge_index[1])
            xs = s[dst]
            xv = v[dst]
            out0a = w0 * xs
            out0b = w3 * (jnp.einsum('emi,ei->em', xv, sh1) * INV_SQRT3)
            out1a = (w1 * xs)[:, :, None] * sh1[:, None, :]
            out1b = w2[:, :, None] * xv
            out1c = w4[:, :, None] * (jnp.cross(xv, sh1[:, None, :]) * INV_SQRT2)
            tp = jnp.concatenate([out0a, out0b, out1a.reshape(E, -1), out1b.reshape(E, -1), out1c.reshape(E, -1)], axis=-1)
            agg = jax.ops.segment_sum(tp, src, num_segments=N) / DENOM
            agg_s = agg[:, :96]
            agg_v = agg[:, 96:].reshape(N, 128, 3)
            out_s = agg_s @ W_out_s + skip_s
            out_v = jnp.einsum('nmi,mk->nki', agg_v, W_out_v) + skip_v
            fs = jax.nn.silu(out_s[:, :MUL0])
            gate = jax.nn.sigmoid(out_s[:, MUL0:MUL0 + 32])
            gv = gate[:, :, None] * out_v
            return jnp.concatenate([fs, gv.reshape(N, -1)], axis=-1)
        key = jax.random.key(seed)
        ks = jax.random.split(key, 12)

        def lin(k, fi, fo):
            return jax.random.normal(k, (fi, fo), jnp.float32) / np.float32(np.sqrt(fi))
        return {'node_feature': jax.random.normal(ks[0], (N_NODES, MUL0 + 3 * MUL1), jnp.float32), 'edge_attr': jax.random.normal(ks[1], (N_EDGES, 3), jnp.float32), 'edge_feature': jax.random.normal(ks[2], (N_EDGES, EDGE_DIM), jnp.float32), 'W_skip0': lin(ks[3], MUL0, 96), 'W_skip1': lin(ks[4], MUL1, 32), 'W_nl0': lin(ks[5], MUL0, MUL0), 'W_nl1': lin(ks[6], MUL1, MUL1), 'W_fc1': lin(ks[7], EDGE_DIM, 64), 'W_fc2': lin(ks[8], 64, W_NUMEL), 'W_out_s': lin(ks[9], 96, 96), 'W_out_v': lin(ks[10], 128, 32), 'edge_index': jax.random.randint(ks[11], (2, N_EDGES), 0, N_NODES)}
    _L3_gnn_all = _L3_gnn_setup()
    _L3_gnn_in = {k: v for k, v in _L3_gnn_all.items() if k in ('W_skip0', 'W_skip1', 'W_nl0', 'W_nl1', 'W_fc1', 'W_fc2', 'W_out_s', 'W_out_v')}
    del _L3_gnn_all
    return {'x': x, 'src': src, 'dst': dst, 'edge_attr_16': edge_attr_16, 'edge_attr_3': edge_attr_3, 'edge_attr_4': edge_attr_4, 'edge_attr_64': edge_attr_64, 'node_vec1': node_vec1, 'L0_gnn_lin1_ws': _L0_gnn_in['lin1_ws'], 'L0_gnn_lin1_wv': _L0_gnn_in['lin1_wv'], 'L0_gnn_fc_w1': _L0_gnn_in['fc_w1'], 'L0_gnn_fc_w2': _L0_gnn_in['fc_w2'], 'L0_gnn_sc_ws': _L0_gnn_in['sc_ws'], 'L0_gnn_sc_wv': _L0_gnn_in['sc_wv'], 'L0_gnn_lin2_ws': _L0_gnn_in['lin2_ws'], 'L0_gnn_lin2_wv': _L0_gnn_in['lin2_wv'], 'L1_gnn_Wfc1': _L1_gnn_in['Wfc1'], 'L1_gnn_Wfc2': _L1_gnn_in['Wfc2'], 'L1_gnn_Wsc0': _L1_gnn_in['Wsc0'], 'L1_gnn_Wsc1': _L1_gnn_in['Wsc1'], 'L1_gnn_Wl1_0': _L1_gnn_in['Wl1_0'], 'L1_gnn_Wl1_1': _L1_gnn_in['Wl1_1'], 'L1_gnn_Wl2_s': _L1_gnn_in['Wl2_s'], 'L1_gnn_Wl2_v': _L1_gnn_in['Wl2_v'], 'L1_gnn_Wa': _L1_gnn_in['Wa'], 'L2_gnn_ln1_w0': _L2_gnn_in['ln1_w0'], 'L2_gnn_ln1_b0': _L2_gnn_in['ln1_b0'], 'L2_gnn_ln1_w1': _L2_gnn_in['ln1_w1'], 'L2_gnn_ln2_w0': _L2_gnn_in['ln2_w0'], 'L2_gnn_ln2_b0': _L2_gnn_in['ln2_b0'], 'L2_gnn_ln2_w1': _L2_gnn_in['ln2_w1'], 'L2_gnn_msrc_ws': _L2_gnn_in['msrc_ws'], 'L2_gnn_msrc_wv': _L2_gnn_in['msrc_wv'], 'L2_gnn_mdst_ws': _L2_gnn_in['mdst_ws'], 'L2_gnn_mdst_bs': _L2_gnn_in['mdst_bs'], 'L2_gnn_mdst_wv': _L2_gnn_in['mdst_wv'], 'L2_gnn_rw1': _L2_gnn_in['rw1'], 'L2_gnn_rb1': _L2_gnn_in['rb1'], 'L2_gnn_rg1': _L2_gnn_in['rg1'], 'L2_gnn_rbe1': _L2_gnn_in['rbe1'], 'L2_gnn_rw2': _L2_gnn_in['rw2'], 'L2_gnn_rb2': _L2_gnn_in['rb2'], 'L2_gnn_rg2': _L2_gnn_in['rg2'], 'L2_gnn_rbe2': _L2_gnn_in['rbe2'], 'L2_gnn_rw3': _L2_gnn_in['rw3'], 'L2_gnn_roff': _L2_gnn_in['roff'], 'L2_gnn_lin_ws': _L2_gnn_in['lin_ws'], 'L2_gnn_lin_bs': _L2_gnn_in['lin_bs'], 'L2_gnn_lin_wv': _L2_gnn_in['lin_wv'], 'L2_gnn_alpha_dot': _L2_gnn_in['alpha_dot'], 'L2_gnn_proj_ws': _L2_gnn_in['proj_ws'], 'L2_gnn_proj_bs': _L2_gnn_in['proj_bs'], 'L2_gnn_proj_wv': _L2_gnn_in['proj_wv'], 'L2_gnn_f1_ws': _L2_gnn_in['f1_ws'], 'L2_gnn_f1_bs': _L2_gnn_in['f1_bs'], 'L2_gnn_f1_wv': _L2_gnn_in['f1_wv'], 'L2_gnn_f2_ws': _L2_gnn_in['f2_ws'], 'L2_gnn_f2_bs': _L2_gnn_in['f2_bs'], 'L2_gnn_f2_wv': _L2_gnn_in['f2_wv'], 'L3_gnn_W_skip0': _L3_gnn_in['W_skip0'], 'L3_gnn_W_skip1': _L3_gnn_in['W_skip1'], 'L3_gnn_W_nl0': _L3_gnn_in['W_nl0'], 'L3_gnn_W_nl1': _L3_gnn_in['W_nl1'], 'L3_gnn_W_fc1': _L3_gnn_in['W_fc1'], 'L3_gnn_W_fc2': _L3_gnn_in['W_fc2'], 'L3_gnn_W_out_s': _L3_gnn_in['W_out_s'], 'L3_gnn_W_out_v': _L3_gnn_in['W_out_v']}

def reference(x, src, dst, edge_attr_16, edge_attr_3, edge_attr_4, edge_attr_64, node_vec1, L0_gnn_lin1_ws, L0_gnn_lin1_wv, L0_gnn_fc_w1, L0_gnn_fc_w2, L0_gnn_sc_ws, L0_gnn_sc_wv, L0_gnn_lin2_ws, L0_gnn_lin2_wv, L1_gnn_Wfc1, L1_gnn_Wfc2, L1_gnn_Wsc0, L1_gnn_Wsc1, L1_gnn_Wl1_0, L1_gnn_Wl1_1, L1_gnn_Wl2_s, L1_gnn_Wl2_v, L1_gnn_Wa, L2_gnn_ln1_w0, L2_gnn_ln1_b0, L2_gnn_ln1_w1, L2_gnn_ln2_w0, L2_gnn_ln2_b0, L2_gnn_ln2_w1, L2_gnn_msrc_ws, L2_gnn_msrc_wv, L2_gnn_mdst_ws, L2_gnn_mdst_bs, L2_gnn_mdst_wv, L2_gnn_rw1, L2_gnn_rb1, L2_gnn_rg1, L2_gnn_rbe1, L2_gnn_rw2, L2_gnn_rb2, L2_gnn_rg2, L2_gnn_rbe2, L2_gnn_rw3, L2_gnn_roff, L2_gnn_lin_ws, L2_gnn_lin_bs, L2_gnn_lin_wv, L2_gnn_alpha_dot, L2_gnn_proj_ws, L2_gnn_proj_bs, L2_gnn_proj_wv, L2_gnn_f1_ws, L2_gnn_f1_bs, L2_gnn_f1_wv, L2_gnn_f2_ws, L2_gnn_f2_bs, L2_gnn_f2_wv, L3_gnn_W_skip0, L3_gnn_W_skip1, L3_gnn_W_nl0, L3_gnn_W_nl1, L3_gnn_W_fc1, L3_gnn_W_fc2, L3_gnn_W_out_s, L3_gnn_W_out_v):
    import jax
    import jax.numpy as jnp

    def _L0_gnn_ref(node_features, node_attr, edge_src, edge_dst, edge_attr, edge_scalars, lin1_ws, lin1_wv, fc_w1, fc_w2, sc_ws, sc_wv, lin2_ws, lin2_wv):
        import jax, jax.numpy as jnp
        import numpy as np
        N, E = (2500, 40000)
        S_IN, V_IN = (64, 32)
        S_MID, V_MID = (96, 128)
        S_OUT, V_OUT = (96, 32)
        R = 64
        FC_HID = 64
        W_NUMEL = 64 + 64 + 32 + 32 + 32
        NUM_NEIGHBORS = 16.0

        def _inv(d):
            return 1.0 / jnp.sqrt(jnp.float32(d))

        def _forward(node_features, node_attr, edge_attr, edge_scalars, lin1_ws, lin1_wv, fc_w1, fc_w2, sc_ws, sc_wv, lin2_ws, lin2_wv, edge_src, edge_dst):
            n = node_features.shape[0]
            s = node_features[:, :S_IN]
            v = node_features[:, S_IN:].reshape(n, V_IN, 3)
            a = node_attr
            sc_s = s @ sc_ws * a * _inv(S_IN)
            sc_v = jnp.einsum('nci,cd->ndi', v, sc_wv) * a[:, :, None] * _inv(V_IN)
            h_s = s @ lin1_ws * a * _inv(S_IN)
            h_v = jnp.einsum('nci,cd->ndi', v, lin1_wv) * a[:, :, None] * _inv(V_IN)
            hid = jax.nn.silu(edge_scalars @ fc_w1 * _inv(R))
            w = hid @ fc_w2 * _inv(FC_HID)
            w1, w2, w3, w4, w5 = jnp.split(w, [64, 128, 160, 192], axis=-1)
            es = h_s[edge_src]
            ev = h_v[edge_src]
            e0 = edge_attr[:, :1]
            e1 = edge_attr[:, 1:4]
            m_s1 = w1 * es * e0
            m_s2 = w4 * jnp.einsum('eci,ei->ec', ev, e1) * _inv(3)
            m_v1 = (w2 * es)[:, :, None] * e1[:, None, :]
            m_v2 = w3[:, :, None] * ev * e0[:, :, None]
            m_v3 = w5[:, :, None] * jnp.cross(ev, e1[:, None, :]) * _inv(2)
            mid_s = jnp.concatenate([m_s1, m_s2], axis=-1)
            mid_v = jnp.concatenate([m_v1, m_v2, m_v3], axis=1)
            inv_nn = 1.0 / jnp.sqrt(jnp.float32(NUM_NEIGHBORS))
            agg_s = jax.ops.segment_sum(mid_s, edge_dst, num_segments=n) * inv_nn
            agg_v = jax.ops.segment_sum(mid_v, edge_dst, num_segments=n) * inv_nn
            o_s = agg_s @ lin2_ws * a * _inv(S_MID)
            o_v = jnp.einsum('nci,cd->ndi', agg_v, lin2_wv) * a[:, :, None] * _inv(V_MID)
            pre_s = sc_s + o_s
            pre_v = sc_v + o_v
            scalars = jax.nn.silu(pre_s[:, :64])
            gates = jax.nn.sigmoid(pre_s[:, 64:96])
            gated = gates[:, :, None] * pre_v
            return jnp.concatenate([scalars, gated.reshape(n, 3 * V_OUT)], axis=-1)
        return _forward(node_features, node_attr, edge_attr, edge_scalars, lin1_ws, lin1_wv, fc_w1, fc_w2, sc_ws, sc_wv, lin2_ws, lin2_wv, edge_src, edge_dst)

    def _L1_gnn_ref(x, node_attr, edge_scalars, edge_attr_sh, edge_src, edge_dst, Wfc1, Wfc2, Wsc0, Wsc1, Wl1_0, Wl1_1, Wl2_s, Wl2_v, Wa):
        import jax, jax.numpy as jnp
        import numpy as np
        N = 1250
        E = 20000
        MUL0 = 64
        MUL1 = 32
        FC_IN = 16
        FC_H = 64
        WNUM = 192
        n = x.shape[0]
        x0 = x[:, :MUL0]
        x1 = x[:, MUL0:].reshape(n, MUL1, 3)
        a = node_attr
        h = jax.nn.silu(edge_scalars @ (Wfc1 / jnp.sqrt(jnp.float32(FC_IN))))
        w = h @ (Wfc2 / jnp.sqrt(jnp.float32(FC_H)))
        w0 = w[:, :64]
        w1 = w[:, 64:128]
        w2 = w[:, 128:160]
        w3 = w[:, 160:192]
        inv8 = 1.0 / jnp.sqrt(jnp.float32(MUL0))
        inv32 = 1.0 / jnp.sqrt(jnp.float32(MUL1))
        sc = jnp.concatenate([x0 @ Wsc0 * a * inv8, (jnp.einsum('num,uv->nvm', x1, Wsc1) * a[..., None] * inv32).reshape(n, 3 * MUL1)], axis=1)
        f0 = x0 @ Wl1_0 * a * inv8
        f1 = jnp.einsum('num,uv->nvm', x1, Wl1_1) * a[..., None] * inv32
        e0 = f0[edge_src]
        e1 = f1[edge_src]
        sh0 = edge_attr_sh[:, :1]
        sh1 = edge_attr_sh[:, 1:4]
        mid0 = w0 * e0 * sh0
        mid1 = w3 * jnp.einsum('eum,em->eu', e1, sh1) / jnp.sqrt(3.0)
        mid2 = w1[:, :, None] * e0[:, :, None] * sh1[:, None, :]
        mid3 = w2[:, :, None] * e1 * sh0[:, :, None]
        cnt = jnp.clip(jax.ops.segment_sum(jnp.ones(edge_dst.shape, x.dtype), edge_dst, num_segments=n), 1.0)

        def smean(v):
            s = jax.ops.segment_sum(v, edge_dst, num_segments=n)
            return s / cnt.reshape((n,) + (1,) * (v.ndim - 1))
        n0, n1 = (smean(mid0), smean(mid1))
        n2, n3 = (smean(mid2), smean(mid3))
        scal = jnp.concatenate([n0, n1], axis=1)
        vec = jnp.concatenate([n2, n3], axis=1)
        inv96 = 1.0 / jnp.sqrt(jnp.float32(MUL0 + MUL1))
        alpha = scal @ Wa * a * inv96
        out_s = scal @ Wl2_s * a * inv96
        out_v = jnp.einsum('num,uv->nvm', vec, Wl2_v) * a[..., None] * inv96
        conv = jnp.concatenate([out_s, out_v.reshape(n, 3 * MUL1)], axis=1)
        return sc + alpha * conv

    def _L2_gnn_ref(node_input, node_attr, edge_vec, edge_scalars, edge_src, edge_dst, ln1_w0, ln1_b0, ln1_w1, ln2_w0, ln2_b0, ln2_w1, msrc_ws, msrc_wv, mdst_ws, mdst_bs, mdst_wv, rw1, rb1, rg1, rbe1, rw2, rb2, rg2, rbe2, rw3, roff, lin_ws, lin_bs, lin_wv, alpha_dot, proj_ws, proj_bs, proj_wv, f1_ws, f1_bs, f1_wv, f2_ws, f2_bs, f2_wv):
        import jax, jax.numpy as jnp
        import numpy as np
        N, E = (625, 10000)
        C0, C1 = (64, 32)
        H, A = (8, 8)
        H0, H1 = (8, 4)
        M0, M1 = (128, 64)
        NG, RH = (64, 64)
        WN = C0 + C0 + C1 + C1 + C1
        DS, DV = (C0 + C1, C0 + 2 * C1)
        EPS = 1e-05
        SQ3 = np.float32(np.sqrt(3.0))
        SQ2 = np.float32(np.sqrt(2.0))

        def _split(x):
            return (x[:, :C0], x[:, C0:].reshape(x.shape[0], C1, 3))

        def _merge(s, v):
            return jnp.concatenate([s, v.reshape(v.shape[0], -1)], axis=1)

        def _eq_ln(x, w0, b0, w1):
            s, v = _split(x)
            s = s - s.mean(axis=1, keepdims=True)
            s = s * jax.lax.rsqrt(jnp.square(s).mean(axis=1, keepdims=True) + EPS) * w0 + b0
            v = v * jax.lax.rsqrt(jnp.square(v).mean(axis=(1, 2), keepdims=True) + EPS) * w1[None, :, None]
            return (s, v)

        def _eq_lin(s, v, ws, bs, wv):
            return (s @ ws + bs, jnp.einsum('nud,uk->nkd', v, wv))

        def _ln(x, g, b):
            xc = x - x.mean(-1, keepdims=True)
            return xc * jax.lax.rsqrt(jnp.square(xc).mean(-1, keepdims=True) + EPS) * g + b

        def _smooth_leaky(x, alpha=0.2):
            return 0.5 * (1 + alpha) * x + 0.5 * (1 - alpha) * x * (2.0 * jax.nn.sigmoid(x) - 1.0)

        def _forward(node_input, node_attr, edge_vec, edge_scalars, edge_src, edge_dst, ln1_w0, ln1_b0, ln1_w1, ln2_w0, ln2_b0, ln2_w1, msrc_ws, msrc_wv, mdst_ws, mdst_bs, mdst_wv, rw1, rb1, rg1, rbe1, rw2, rb2, rg2, rbe2, rw3, roff, lin_ws, lin_bs, lin_wv, alpha_dot, proj_ws, proj_bs, proj_wv, f1_ws, f1_bs, f1_wv, f2_ws, f2_bs, f2_wv):
            n = node_input.shape[0]
            s, v = _eq_ln(node_input, ln1_w0, ln1_b0, ln1_w1)
            src_s = s @ msrc_ws
            src_v = jnp.einsum('nud,uk->nkd', v, msrc_wv)
            dst_s = s @ mdst_ws + mdst_bs
            dst_v = jnp.einsum('nud,uk->nkd', v, mdst_wv)
            ms = src_s[edge_src] + dst_s[edge_dst]
            mv = src_v[edge_src] + dst_v[edge_dst]
            h = jax.nn.silu(_ln(edge_scalars @ rw1 + rb1, rg1, rbe1))
            h = jax.nn.silu(_ln(h @ rw2 + rb2, rg2, rbe2))
            w = h @ rw3 + roff
            rhat = edge_vec * jax.lax.rsqrt(jnp.sum(jnp.square(edge_vec), -1, keepdims=True) + 1e-12)
            Y1 = SQ3 * rhat
            w1, w2, w3, w4, w5 = jnp.split(w, [C0, 2 * C0, 2 * C0 + C1, 2 * C0 + 2 * C1], axis=1)
            o0a = w1 * ms
            o0b = w4 * (jnp.einsum('eud,ed->eu', mv, Y1) / SQ3)
            o1a = (w2 * ms)[:, :, None] * Y1[:, None, :]
            o1b = w3[:, :, None] * mv
            o1c = w5[:, :, None] * (jnp.cross(mv, Y1[:, None, :]) / SQ2)
            ds = jnp.concatenate([o0a, o0b], axis=1)
            dv = jnp.concatenate([o1a, o1b, o1c], axis=1)
            ls, lv = _eq_lin(ds, dv, lin_ws, lin_bs, lin_wv)
            e = ls.shape[0]
            alpha = ls[:, :H * A].reshape(e, H, A)
            vs = ls[:, H * A:].reshape(e, H, H0)
            vv = lv.reshape(e, H, H1, 3)
            a = jnp.einsum('ehk,hk->eh', _smooth_leaky(alpha), alpha_dot)
            amax = jax.lax.stop_gradient(jax.ops.segment_max(a, edge_dst, num_segments=n))
            a = jnp.exp(a - amax[edge_dst])
            a = a / (jax.ops.segment_sum(a, edge_dst, num_segments=n)[edge_dst] + 1e-12)
            ns = jax.ops.segment_sum(vs * a[..., None], edge_dst, num_segments=n).reshape(n, H * H0)
            nv = jax.ops.segment_sum(vv * a[..., None, None], edge_dst, num_segments=n).reshape(n, H * H1, 3)
            ps, pv = _eq_lin(ns, nv, proj_ws, proj_bs, proj_wv)
            x = node_input + _merge(ps, pv)
            s2, v2 = _eq_ln(x, ln2_w0, ln2_b0, ln2_w1)
            a0 = node_attr[:, :1]
            fs, fv = _eq_lin(s2, v2, f1_ws, f1_bs, f1_wv)
            fs = fs * a0
            fv = fv * a0[:, :, None]
            sc = jax.nn.silu(fs[:, :M0])
            fv = fv * jax.nn.sigmoid(fs[:, M0:])[:, :, None]
            os_, ov = _eq_lin(sc, fv, f2_ws, f2_bs, f2_wv)
            os_ = os_ * a0
            ov = ov * a0[:, :, None]
            return x + _merge(os_, ov)
        return _forward(node_input, node_attr, edge_vec, edge_scalars, edge_src, edge_dst, ln1_w0, ln1_b0, ln1_w1, ln2_w0, ln2_b0, ln2_w1, msrc_ws, msrc_wv, mdst_ws, mdst_bs, mdst_wv, rw1, rb1, rg1, rbe1, rw2, rb2, rg2, rbe2, rw3, roff, lin_ws, lin_bs, lin_wv, alpha_dot, proj_ws, proj_bs, proj_wv, f1_ws, f1_bs, f1_wv, f2_ws, f2_bs, f2_wv)

    def _L3_gnn_ref(node_feature, edge_attr, edge_feature, W_skip0, W_skip1, W_nl0, W_nl1, W_fc1, W_fc2, W_out_s, W_out_v, edge_index):
        import jax, jax.numpy as jnp
        import numpy as np
        N_NODES = 625
        N_EDGES = 20000
        MUL0, MUL1 = (64, 32)
        EDGE_DIM = 64
        W_NUMEL = 224
        DENOM = 32.0
        SQRT3 = 3.0 ** 0.5
        INV_SQRT3 = 1.0 / SQRT3
        INV_SQRT2 = 2.0 ** (-0.5)

        def _forward(node_feature, edge_attr, edge_feature, W_skip0, W_skip1, W_nl0, W_nl1, W_fc1, W_fc2, W_out_s, W_out_v, edge_index):
            N = node_feature.shape[0]
            E = edge_attr.shape[0]
            s = node_feature[:, :MUL0]
            v = node_feature[:, MUL0:].reshape(N, MUL1, 3)
            skip_s = s @ W_skip0
            skip_v = jnp.einsum('nmi,mk->nki', v, W_skip1)
            s = s @ W_nl0
            v = jnp.einsum('nmi,mk->nki', v, W_nl1)
            rhat = edge_attr / jnp.linalg.norm(edge_attr, axis=-1, keepdims=True)
            sh1 = SQRT3 * rhat
            w = jax.nn.relu(edge_feature @ W_fc1) @ W_fc2
            w0, w1, w2, w3, w4 = jnp.split(w, [64, 128, 160, 192], axis=-1)
            src, dst = (edge_index[0], edge_index[1])
            xs = s[dst]
            xv = v[dst]
            out0a = w0 * xs
            out0b = w3 * (jnp.einsum('emi,ei->em', xv, sh1) * INV_SQRT3)
            out1a = (w1 * xs)[:, :, None] * sh1[:, None, :]
            out1b = w2[:, :, None] * xv
            out1c = w4[:, :, None] * (jnp.cross(xv, sh1[:, None, :]) * INV_SQRT2)
            tp = jnp.concatenate([out0a, out0b, out1a.reshape(E, -1), out1b.reshape(E, -1), out1c.reshape(E, -1)], axis=-1)
            agg = jax.ops.segment_sum(tp, src, num_segments=N) / DENOM
            agg_s = agg[:, :96]
            agg_v = agg[:, 96:].reshape(N, 128, 3)
            out_s = agg_s @ W_out_s + skip_s
            out_v = jnp.einsum('nmi,mk->nki', agg_v, W_out_v) + skip_v
            fs = jax.nn.silu(out_s[:, :MUL0])
            gate = jax.nn.sigmoid(out_s[:, MUL0:MUL0 + 32])
            gv = gate[:, :, None] * out_v
            return jnp.concatenate([fs, gv.reshape(N, -1)], axis=-1)
        return _forward(node_feature, edge_attr, edge_feature, W_skip0, W_skip1, W_nl0, W_nl1, W_fc1, W_fc2, W_out_s, W_out_v, edge_index)
    edge_index = jnp.stack([src, dst])
    h = jnp.maximum(_layernorm(x, axis=-1), 0.0)
    x = x + _L0_gnn_ref(h, node_vec1, src, dst, edge_attr_4, edge_attr_64, L0_gnn_lin1_ws, L0_gnn_lin1_wv, L0_gnn_fc_w1, L0_gnn_fc_w2, L0_gnn_sc_ws, L0_gnn_sc_wv, L0_gnn_lin2_ws, L0_gnn_lin2_wv)
    h = jnp.maximum(_layernorm(x, axis=-1), 0.0)
    x = x + _L1_gnn_ref(h, node_vec1, edge_attr_16, edge_attr_4, src, dst, L1_gnn_Wfc1, L1_gnn_Wfc2, L1_gnn_Wsc0, L1_gnn_Wsc1, L1_gnn_Wl1_0, L1_gnn_Wl1_1, L1_gnn_Wl2_s, L1_gnn_Wl2_v, L1_gnn_Wa)
    h = jnp.maximum(_layernorm(x, axis=-1), 0.0)
    x = x + _L2_gnn_ref(h, node_vec1, edge_attr_3, edge_attr_64, src, dst, L2_gnn_ln1_w0, L2_gnn_ln1_b0, L2_gnn_ln1_w1, L2_gnn_ln2_w0, L2_gnn_ln2_b0, L2_gnn_ln2_w1, L2_gnn_msrc_ws, L2_gnn_msrc_wv, L2_gnn_mdst_ws, L2_gnn_mdst_bs, L2_gnn_mdst_wv, L2_gnn_rw1, L2_gnn_rb1, L2_gnn_rg1, L2_gnn_rbe1, L2_gnn_rw2, L2_gnn_rb2, L2_gnn_rg2, L2_gnn_rbe2, L2_gnn_rw3, L2_gnn_roff, L2_gnn_lin_ws, L2_gnn_lin_bs, L2_gnn_lin_wv, L2_gnn_alpha_dot, L2_gnn_proj_ws, L2_gnn_proj_bs, L2_gnn_proj_wv, L2_gnn_f1_ws, L2_gnn_f1_bs, L2_gnn_f1_wv, L2_gnn_f2_ws, L2_gnn_f2_bs, L2_gnn_f2_wv)
    h = jnp.maximum(_layernorm(x, axis=-1), 0.0)
    x = x + _L3_gnn_ref(h, edge_attr_3, edge_attr_64, L3_gnn_W_skip0, L3_gnn_W_skip1, L3_gnn_W_nl0, L3_gnn_W_nl1, L3_gnn_W_fc1, L3_gnn_W_fc2, L3_gnn_W_out_s, L3_gnn_W_out_v, edge_index)
    return x

_drawn_inputs = setup_inputs


def setup_inputs(seed=0):
    import zlib

    import numpy as np

    out = dict(_drawn_inputs(seed))
    spreads = {'L2_gnn_ln1_w0': (1.0, 0.2),
     'L2_gnn_ln1_b0': (0.0, 0.1),
     'L2_gnn_ln1_w1': (1.0, 0.2),
     'L2_gnn_ln2_w0': (1.0, 0.2),
     'L2_gnn_ln2_b0': (0.0, 0.1),
     'L2_gnn_ln2_w1': (1.0, 0.2),
     'L2_gnn_mdst_bs': (0.0, 0.1),
     'L2_gnn_rb1': (0.0, 0.1),
     'L2_gnn_rg1': (1.0, 0.2),
     'L2_gnn_rbe1': (0.0, 0.1),
     'L2_gnn_rb2': (0.0, 0.1),
     'L2_gnn_rg2': (1.0, 0.2),
     'L2_gnn_rbe2': (0.0, 0.1),
     'L2_gnn_lin_bs': (0.0, 0.1),
     'L2_gnn_proj_bs': (0.0, 0.1),
     'L2_gnn_f1_bs': (0.0, 0.1),
     'L2_gnn_f2_bs': (0.0, 0.1)}
    factors = {}
    for name, (base, spread) in spreads.items():
        noise = np.random.default_rng([zlib.crc32(name.encode()), seed]).standard_normal(out[name].shape)
        drawn = base * np.exp(spread * noise) if base else spread * noise
        out[name] = jnp.asarray(drawn.astype(out[name].dtype))
    for name, factor in factors.items():
        out[name] = (out[name] * factor).astype(out[name].dtype)
    return out
```

```python
import numpy as np
import concourse.bass as bass
from concourse import mybir
from contextlib import ExitStack, contextmanager

F32 = mybir.dt.float32
I32 = mybir.dt.int32
ALU = mybir.AluOpType
ACT = mybir.ActivationFunctionType
AX = mybir.AxisListType

P = 128
TG = 4
GE = TG * P
NB = 5
NS, NV = 64, 32
FEAT = NS + 3 * NV
COPIES = TG
MSG = 480
EPS = 1e-5
A0, C0, D0, X0, B0 = 0, 64, 160, 192, 288
PA, PC, PD, PE_, PN, PB = 0, 64, 160, 256, 352, 448


class Shapes:

    def __init__(self, nodes, edges):
        self.nodes, self.edges = nodes, edges
        self.node_groups = -(-nodes // (NB * P))
        self.node_tiles = self.node_groups * NB
        self.node_rows = self.node_tiles * P
        assert nodes < self.node_rows, "the last row takes the padding edges"
        self.agg_rows = self.node_rows + P
        self.pairs = -(-edges // (2 * GE))
        self.groups = 2 * self.pairs
        self.tiles = self.groups * TG
        self.edge_rows = self.tiles * P


class Chain:

    def __init__(self, engine, sem, per_iteration=0, iteration=0):
        self.engine, self.sem, self.per, self.it, self.n = engine, sem, per_iteration, iteration, 0

    def link(self, instruction):
        self.n += 1
        instruction.then_inc(self.sem, 1)
        self.engine.wait_ge(self.sem, self.it * self.per + self.n)

    def end(self):
        assert self.n == self.per, f"links of an iteration: {self.n}"


@contextmanager
def phase(nc, names):
    with ExitStack() as stack:
        sems = {n: stack.enter_context(nc.semaphore(n)) for n in names}
        stack.enter_context(nc.allow_non_contiguous_dma(reason="small strided loads"))
        yield sems
        for s in sems.values():
            nc.gpsimd.sem_clear(s)
        nc.all_engine_barrier()


def load_constants(nc, T, D):
    with phase(nc, ["const_loaded", "mask_step"]) as s:
        with nc.Block() as block:
            @block.sync
            def _(sp):
                sp.dma_start(T["x"][:, :, :], D["x"].rearrange("(t p) f -> p t f", p=P)).then_inc(s["const_loaded"], 16)
                sp.dma_start(T["a"][:, :], D["node_vec1"].rearrange("(t p) o -> p (t o)", p=P)).then_inc(s["const_loaded"], 16)
                sp.wait_ge(s["const_loaded"], 32)

            @block.gpsimd
            def _(pool):
                pool.memset(T["ident"][:, :], 0.0).then_inc(s["mask_step"], 1)
                pool.memset(T["lower"][:, :], 1.0).then_inc(s["mask_step"], 1)
                pool.memset(T["zero"][:, :], 0.0).then_inc(s["mask_step"], 1)
                pool.memset(T["ones"][:, :], 1.0).then_inc(s["mask_step"], 1)
                pool.iota(T["spare_i"][:, :], pattern=[[0, TG]], base=D["shapes"].node_rows, channel_multiplier=1).then_inc(s["mask_step"], 1)
                pool.wait_ge(s["mask_step"], 5)
                pool.affine_select(out=T["ident"][:, :], in_=T["ident"][:, :], compare_op=ALU.not_equal, fill=1.0,
                                   base=0, pattern=[[-1, P]], channel_multiplier=1).then_inc(s["mask_step"], 1)
                pool.affine_select(out=T["lower"][:, :], in_=T["lower"][:, :], compare_op=ALU.is_gt, fill=0.0,
                                   base=0, pattern=[[-1, P]], channel_multiplier=1).then_inc(s["mask_step"], 1)
                pool.tensor_copy(T["spare"][:, :], T["spare_i"][:, :]).then_inc(s["mask_step"], 1)
                pool.wait_ge(s["mask_step"], 8)


def zero_phase(nc, T, tables, width):
    with phase(nc, ["zeroed"]) as s:
        with nc.Block() as block:
            @block.sync
            def _(sp):
                for table in tables:
                    rows = table.shape[0] // P
                    zeros = T["zero"][:, 0:width].unsqueeze(1).to_broadcast([P, rows, width])
                    sp.dma_start(table.rearrange("(t p) f -> p t f", p=P), zeros).then_inc(s["zeroed"], 16)
                sp.wait_ge(s["zeroed"], 16 * len(tables))


def norm_steps(nc, T, dve, c, s, src, h, stats, mv, g):
    for t in range(NB):
        ins = nc.vector.bn_stats(stats[:, t, :], src(t))
        ins.then_inc(s["dve_step"], 1)
    c.n += NB
    dve.wait_ge(s["dve_step"], c.it * c.per + c.n)
    dve.sem_inc(T["past"], 1)
    for t in range(NB):
        nc.vector.bn_aggr(mv[:, t, 0:2], stats[:, t, :]).then_inc(s["dve_step"], 1)
    c.n += NB
    dve.wait_ge(s["dve_step"], c.it * c.per + c.n)
    nc.vector.tensor_scalar(mv[:, :, 2], mv[:, :, 1], EPS, None, ALU.add).then_inc(s["var_ready"], 1)


NORM_LINKS = 2 * NB + 1 + NB + 1


def norm_finish(nc, dve, c, s, src, h, mv, roots):
    dve.wait_ge(s["root_ready"], roots)
    c.link(nc.vector.reciprocal(mv[:, :, 4], mv[:, :, 3]))
    for t in range(NB):
        nc.vector.tensor_scalar(h[:, t, :], src(t), mv[:, t, 0:1], mv[:, t, 4:5], ALU.subtract, ALU.mult).then_inc(s["dve_step"], 1)
    c.n += NB
    dve.wait_ge(s["dve_step"], c.it * c.per + c.n)
    c.link(nc.vector.tensor_scalar(h[:, :, :], h[:, :, :], 0.0, None, ALU.max))


def node_pre(nc, T, D, S, L, w_dram, scale_dram, tables, width, skip, attr, eq=None):
    M = w_dram.shape[1]
    skipw = M - width
    names = ["w_loaded", "w_scaled", "dve_step", "var_ready", "root_ready", "h_ready", "tr_ready", "tr_copied",
             "out_ready", "out_copied", "table_ready", "stored", "act_step"]
    with phase(nc, names) as s, ExitStack() as st:
        def sb(n, sh, dt=F32):
            return st.enter_context(nc.sbuf_tensor(f"{L}pre_{n}", sh, dt))
        w1, w2 = sb("w1", [P, M]), sb("w2", [NV, M])
        rs1, rs2 = sb("rs1", [P, 1]), sb("rs2", [NV, 1])
        stats, mv = sb("stats", [P, NB, 6]), sb("mv", [P, NB, 5])
        h = sb("h", [P, NB, FEAT])
        hT = sb("hT", [P, 2, 2 * P])
        tab = sb("tab", [P, NB, width])
        TR = [T["bank"][6], T["bank"][7]]
        OUT = [T["bank"][4], T["bank"][5]]
        loads = 4
        if eq:
            sq = sb("sq", [P, NB, FEAT])
            ev = sb("ev", [P, NB, 8])
            pr = sb("pr", [P, 2 * FEAT])
            bias = sb("bias", [P, width])
            loads = 6
        per = NORM_LINKS + (11 + 2 * NB if eq else 0)
        with nc.Block() as block:
            @block.sync
            def _(sp):
                sp.dma_start(w1[:, :], w_dram[0:P, :]).then_inc(s["w_loaded"], 16)
                sp.dma_start(w2[:, :], w_dram[P:FEAT, :]).then_inc(s["w_loaded"], 16)
                sp.dma_start(rs1[:, :], scale_dram[0:P, :]).then_inc(s["w_loaded"], 16)
                sp.dma_start(rs2[:, :], scale_dram[P:FEAT, :]).then_inc(s["w_loaded"], 16)
                if eq:
                    sp.dma_start(pr[:, :], eq[0].partition_broadcast(P)).then_inc(s["w_loaded"], 16)
                    sp.dma_start(bias[:, :], eq[1].partition_broadcast(P)).then_inc(s["w_loaded"], 16)
                with sp.Fori(0, S.node_groups) as g:
                    sp.wait_ge(s["table_ready"], g + 1)
                    sp.sem_inc(T["past"], 1)
                    for n, table in enumerate(tables):
                        rows = table.rearrange("(t p) f -> p t f", p=P)
                        part = width // len(tables)
                        sp.dma_start(rows[:, bass.ds(g * NB, NB), :], tab[:, :, n * part:(n + 1) * part]).then_inc(s["stored"], 16)
                    sp.wait_ge(s["stored"], 16 * len(tables) * (g + 1))
                    sp.sem_inc(T["past"], 1)

            @block.vector
            def _(dve):
                dve.wait_ge(s["w_loaded"], 16 * loads)
                nc.vector.tensor_scalar(w1[:, :], w1[:, :], rs1[:, 0:1], None, ALU.mult).then_inc(s["w_scaled"], 1)
                nc.vector.tensor_scalar(w2[:, :], w2[:, :], rs2[:, 0:1], None, ALU.mult).then_inc(s["w_scaled"], 1)
                with dve.Fori(0, S.node_groups) as g:
                    c = Chain(dve, s["dve_step"], per, g)
                    x = T["x"][:, bass.ds(g * NB, NB), :]
                    dve.wait_ge(s["tr_ready"], g * NB)
                    norm_steps(nc, T, dve, c, s, lambda t: x[:, t, :], h, stats, mv, g)
                    norm_finish(nc, dve, c, s, lambda t: x[:, t, :], h, mv, (2 if eq else 1) * g + 1)
                    if eq:
                        c.link(nc.vector.tensor_copy(skip[:, bass.ds(g * NB, NB), 0:FEAT], h[:, :, :]))
                        c.link(nc.vector.reduce_sum(ev[:, :, 0], h[:, :, 0:NS], AX.X))
                        c.link(nc.vector.tensor_scalar(ev[:, :, 0], ev[:, :, 0], 1.0 / NS, None, ALU.mult))
                        c.link(nc.vector.tensor_tensor(h[:, :, 0:NS], h[:, :, 0:NS],
                                                       ev[:, :, 0:1].to_broadcast([P, NB, NS]), ALU.subtract))
                        c.link(nc.vector.tensor_tensor(sq[:, :, :], h[:, :, :], h[:, :, :], ALU.mult))
                        c.link(nc.vector.reduce_sum(ev[:, :, 1], sq[:, :, 0:NS], AX.X))
                        c.link(nc.vector.reduce_sum(ev[:, :, 2], sq[:, :, NS:FEAT], AX.X))
                        c.link(nc.vector.tensor_scalar(ev[:, :, 1], ev[:, :, 1], 1.0 / NS, EPS, ALU.mult, ALU.add))
                        nc.vector.tensor_scalar(ev[:, :, 2], ev[:, :, 2], 1.0 / (3 * NV), EPS, ALU.mult, ALU.add).then_inc(s["var_ready"], 1)
                        dve.wait_ge(s["root_ready"], 2 * g + 2)
                        c.link(nc.vector.reciprocal(ev[:, :, 5:7], ev[:, :, 3:5]))
                        for t in range(NB):
                            c.link(nc.vector.tensor_scalar(h[:, t, 0:NS], h[:, t, 0:NS], ev[:, t, 5:6], None, ALU.mult))
                            c.link(nc.vector.tensor_scalar(h[:, t, NS:FEAT], h[:, t, NS:FEAT], ev[:, t, 6:7], None, ALU.mult))
                        c.link(nc.vector.tensor_tensor(h[:, :, :], h[:, :, :], pr[:, 0:FEAT].unsqueeze(1).to_broadcast([P, NB, FEAT]), ALU.mult))
                        c.link(nc.vector.tensor_tensor(h[:, :, :], h[:, :, :], pr[:, FEAT:2 * FEAT].unsqueeze(1).to_broadcast([P, NB, FEAT]), ALU.add))
                    c.end()
                    dve.sem_inc(s["h_ready"], 1)
                    dve.wait_ge(s["stored"], 16 * len(tables) * g)
                    for t in range(NB):
                        dve.wait_ge(s["out_ready"], g * NB + t + 1)
                        o = OUT[t % 2]
                        if eq:
                            nc.vector.tensor_tensor(tab[:, t, :], o[:, 0:width], bias[:, :], ALU.add).then_inc(s["out_copied"], 1)
                        else:
                            at = T["a"][:, bass.ds(g * NB + t, 1)] if attr else 1.0
                            nc.vector.tensor_scalar(tab[:, t, :], o[:, 0:width], at, None, ALU.mult).then_inc(s["act_step"], 1)
                        if skipw:
                            sk = skip[:, bass.ds(g * NB + t, 1), 0:skipw]
                            nc.vector.tensor_scalar(sk, o[:, width:M].unsqueeze(1), at, None, ALU.mult).then_inc(s["out_copied"], 1)
                    dve.wait_ge(s["out_copied"], g * NB + NB)
                    if not eq:
                        dve.wait_ge(s["act_step"], g * NB + NB)
                    dve.sem_inc(s["table_ready"], 1)

            @block.scalar
            def _(act):
                with act.Fori(0, S.node_groups) as g:
                    act.wait_ge(s["var_ready"], (2 if eq else 1) * g + 1)
                    nc.scalar.activation(mv[:, :, 3], mv[:, :, 2], ACT.Sqrt).then_inc(s["root_ready"], 1)
                    if eq:
                        act.wait_ge(s["var_ready"], 2 * g + 2)
                        nc.scalar.activation(ev[:, :, 3:5], ev[:, :, 1:3], ACT.Sqrt).then_inc(s["root_ready"], 1)
                    for t in range(NB):
                        act.wait_ge(s["tr_ready"], g * NB + t + 1)
                        if t >= 2:
                            act.wait_ge(s["out_ready"], g * NB + t - 1)
                        else:
                            act.wait_ge(s["out_ready"], g * NB)
                        nc.scalar.activation(hT[:, t % 2, 0:P], TR[t % 2][:, 0:P], ACT.Copy)
                        nc.scalar.activation(hT[0:NV, t % 2, P:2 * P], TR[t % 2][0:NV, P:2 * P], ACT.Copy).then_inc(s["tr_copied"], 1)

            @block.tensor
            def _(pe):
                pe.wait_ge(s["w_scaled"], 2)
                with pe.Fori(0, S.node_groups) as g:
                    pe.wait_ge(s["h_ready"], g + 1)
                    for t in range(NB):
                        if t >= 2:
                            pe.wait_ge(s["tr_copied"], g * NB + t - 1)
                            pe.wait_ge(s["out_copied"], g * NB + t - 1)
                        else:
                            pe.wait_ge(s["tr_copied"], g * NB)
                            pe.wait_ge(s["out_copied"], g * NB)
                        if not eq:
                            pe.wait_ge(s["act_step"], g * NB + max(t - 1, 0))
                        tr, o = TR[t % 2], OUT[t % 2]
                        nc.tensor.transpose(tr[:, 0:P], h[:, t, 0:P], T["ident"][:, :])
                        nc.tensor.transpose(tr[0:NV, P:2 * P], h[:, t, P:FEAT], T["ident"][:, :]).then_inc(s["tr_ready"], 1)
                        pe.wait_ge(s["tr_copied"], g * NB + t + 1)
                        nc.tensor.matmul(o[:, 0:M], hT[:, t % 2, 0:P], w1[:, :], start=True, stop=False)
                        nc.tensor.matmul(o[:, 0:M], hT[0:NV, t % 2, P:2 * P], w2[:, :], start=False, stop=True).then_inc(s["out_ready"], 1)


def edge_pass(nc, T, D, S, L, meta_i, meta_f, keys, attrT, wA_dram, wB_dram, table, agg, hid_func, hid_scale,
              cross, count):
    K = attrT.shape[0]
    H = wA_dram.shape[1]
    blocks = 3 if cross else 2
    W = 2 * NS + (4 if cross else 2) * NV
    names = ["w_loaded", "neg_ready", "in_free0", "in_free1", "in_loaded0", "in_loaded1",
             "hid_ready", "hid_done", "hid_read", "w_ready", "dve_step", "p_ready", "agg_ready", "msg_ready",
             "idx_ready"]
    with phase(nc, names) as s, ExitStack() as st:
        def sb(n, sh, dt=F32):
            return st.enter_context(nc.sbuf_tensor(f"{L}e_{n}", sh, dt))
        in_free = [s["in_free0"], s["in_free1"]]
        in_loaded = [s["in_loaded0"], s["in_loaded1"]]
        gathered, fetched = T["gathered"], T["gathered_count"]
        added, summed = T["added"], T["added_count"]
        wA, wB = sb("wA", [K, H]), sb("wB", [H, W])
        at = [sb(f"at{b}", [K, GE]) for b in range(2)]
        row = [sb(f"row{b}", [P, GE], I32) for b in range(2)]
        mi = [sb(f"mi{b}", [P, 2 * TG], I32) for b in range(2)]
        mf = [sb(f"mf{b}", [P, TG, 4]) for b in range(2)]
        G = [[sb(f"G{b}{t}", [P, FEAT]) for t in range(TG)] for b in range(2)]
        hidT = [sb(f"hidT{b}", [H, GE]) for b in range(2)]
        keyf = [sb(f"keyf{b}", [P, TG]) for b in range(2)]
        cnt = [sb(f"cnt{b}", [P, 2, TG]) for b in range(2)]
        idx = [[sb(f"idx{b}{t}", [P, 1], I32) for t in range(TG)] for b in range(2)]
        Sk = [sb(f"S{q}", [P, 5 if count else 4, P]) for q in range(2)]
        junk = sb("junk", [P, P])
        prod = [sb(f"prod{q}", [P, 512]) for q in range(2)]
        msg = [sb(f"msg{t}", [P, MSG]) for t in range(TG)]
        HID = [T["bank"][0], T["bank"][1]]
        WPS = [T["bank"][n][:, 0:W] for n in (2, 3, 6, 7)]
        AGG = [T["bank"][4], T["bank"][5]]
        last = S.pairs - 1
        msg_w = MSG
        steps = 2 + 2 * TG

        def tile(g, t):
            return g * TG + t

        with nc.Block() as block:
            @block.sync
            def _(sp):
                sp.dma_start(wA[:, :], wA_dram).then_inc(s["w_loaded"], 16)
                sp.dma_start(wB[:, :], wB_dram).then_inc(s["w_loaded"], 16)
                with sp.Fori(0, S.pairs) as i:
                    for b in range(2):
                        g = i * 2 + b
                        sp.wait_ge(in_free[b], i)
                        sp.sem_inc(T["past"], 1)
                        sp.dma_start(at[b][:, :], attrT[:, bass.ds(g * GE, GE)]).then_inc(in_loaded[b], 16)
                        sp.dma_start(mi[b][:, :], meta_i[bass.ds(g * P, P), :]).then_inc(in_loaded[b], 16)
                        sp.dma_start(mf[b][:, :, :], meta_f[bass.ds(g * P, P), :].rearrange("p (t k) -> p t k", k=4)).then_inc(in_loaded[b], 16)
                        sp.dma_start(row[b][:, :], keys[:, bass.ds(g * GE, GE)].partition_broadcast(P)).then_inc(in_loaded[b], 16)

            @block.gpsimd
            def _(pool):
                def gather(i, b):
                    pool.wait_ge(in_loaded[b], 64 * i + 64)
                    pool.wait_ge(in_free[b], i)
                    pool.sem_inc(T["past"], 1)
                    for t in range(TG):
                        pool.indirect_dma_start(G[b][t][:, :], None, table, bass.IndirectOffsetOnAxis(mi[b][:, t:t + 1], 0)).then_inc(gathered[b], 16)

                def scatter(i, b):
                    g = i * 2 + b
                    pool.wait_ge(s["idx_ready"], g + 1)
                    for t in range(TG):
                        pool.wait_ge(s["msg_ready"], tile(g, t) + 1)
                        pool.wait_ge(added[t], summed + 16 * g)
                        pool.sem_inc(T["past"], 1)
                        pool.indirect_dma_start(agg[t], bass.IndirectOffsetOnAxis(idx[b][t][:, 0:1], 0), msg[t][:, 0:msg_w],
                                                None, compute_op=ALU.add).then_inc(added[t], 16)
                gather(0, 0)
                with pool.Fori(0, last) as i:
                    gather(i, 1)
                    scatter(i, 0)
                    gather(i + 1, 0)
                    scatter(i, 1)
                gather(last, 1)
                scatter(last, 0)
                scatter(last, 1)
                for t in range(TG):
                    pool.wait_ge(added[t], summed + 16 * S.groups)

            @block.vector
            def _(dve):
                dve.wait_ge(s["w_loaded"], 32)
                if cross:
                    nc.vector.tensor_scalar(wB[:, W - NV:W], wB[:, W - 2 * NV:W - NV], -1.0, None, ALU.mult).then_inc(s["neg_ready"], 1)
                with dve.Fori(0, S.pairs) as i:
                    c = Chain(dve, s["dve_step"], 2 * steps, i)
                    for b in range(2):
                        g = i * 2 + b
                        dve.wait_ge(in_loaded[b], 64 * i + 64)
                        c.link(nc.vector.tensor_copy(keyf[b][:, :], mi[b][:, TG:2 * TG]))
                        for t in range(TG):
                            if t >= 2:
                                dve.wait_ge(s["agg_ready"], tile(g, t) - 1)
                            else:
                                dve.wait_ge(s["agg_ready"], tile(g, 0))
                            q = t % 2
                            r = row[b][:, t * P:(t + 1) * P]
                            for k in range(4):
                                nc.vector.tensor_scalar(Sk[q][:, k, :], r, keyf[b][:, t:t + 1], mf[b][:, t, k:k + 1], ALU.is_equal, ALU.mult)
                            if count:
                                nc.vector.tensor_scalar(Sk[q][:, 4, :], r, keyf[b][:, t:t + 1], None, ALU.is_equal)
                            c.link(nc.vector.scalar_tensor_tensor(junk[:, :], r, keyf[b][:, t:t + 1], T["lower"][:, :], ALU.is_equal, ALU.mult,
                                                                  accum_out=cnt[b][:, 0, t:t + 1]))
                            if t == 0:
                                dve.wait_ge(gathered[b], fetched + 16 * TG * i + 16 * TG)
                            dve.wait_ge(s["w_ready"], tile(g, t) + 1)
                            w, gt, p = WPS[t], G[b][t], prod[q]
                            pab = p[:, 0:512].rearrange("p (m c) -> p m c", c=NS)[:, 0:8:7, :]
                            nc.vector.tensor_tensor(pab, w[:, 0:2 * NS].rearrange("p (m c) -> p m c", c=NS),
                                                    gt[:, 0:NS].unsqueeze(1).to_broadcast([P, 2, NS]), ALU.mult)
                            m = (W - 2 * NS) // NV
                            nc.vector.tensor_tensor(p[:, PC:PC + 96 * m].rearrange("p (m k c) -> p m k c", k=3, c=NV),
                                                    w[:, 2 * NS:W].rearrange("p (m c) -> p m c", c=NV).unsqueeze(2).to_broadcast([P, m, 3, NV]),
                                                    gt[:, NS:FEAT].rearrange("p (k c) -> p k c", c=NV).unsqueeze(1).to_broadcast([P, m, 3, NV]),
                                                    ALU.mult).then_inc(s["p_ready"], 1)
                        c.link(nc.vector.tensor_tensor(cnt[b][:, 1, :], T["spare"][:, :], keyf[b][:, :], ALU.subtract))
                        dve.wait_ge(s["p_ready"], tile(g, TG))
                        nc.vector.tensor_scalar(cnt[b][:, 0, :], cnt[b][:, 0, :], 0.5, None, ALU.is_gt).then_inc(in_free[b], 1)
                        dve.wait_ge(in_free[b], i + 1)
                        for t in range(TG):
                            dve.wait_ge(added[t], summed + 32 * i)
                            c.link(nc.vector.scalar_tensor_tensor(idx[b][t][:, :], cnt[b][:, 0, t:t + 1], cnt[b][:, 1, t:t + 1], keyf[b][:, t:t + 1],
                                                                  ALU.mult, ALU.add))
                        dve.sem_inc(s["idx_ready"], 1)
                    c.end()

            @block.scalar
            def _(act):
                def hidden(g, b):
                    act.wait_ge(s["hid_ready"], g + 1)
                    nc.scalar.activation(hidT[b][:, :], HID[b][0:H, :], hid_func, scale=hid_scale).then_inc(s["hid_done"], 1)

                def evacuate(g):
                    for t in range(TG):
                        act.wait_ge(s["agg_ready"], tile(g, t) + 1)
                        act.wait_ge(added[t], summed + 16 * g)
                        nc.scalar.activation(msg[t][:, :], AGG[t % 2][:, 0:MSG], ACT.Copy).then_inc(s["msg_ready"], 1)
                hidden(0, 0)
                with act.Fori(0, last) as i:
                    hidden(i * 2 + 1, 1)
                    evacuate(i * 2)
                    hidden(i * 2 + 2, 0)
                    evacuate(i * 2 + 1)
                hidden(2 * last + 1, 1)
                evacuate(2 * last)
                evacuate(2 * last + 1)

            @block.tensor
            def _(pe):
                def hidden(i, b):
                    g = i * 2 + b
                    pe.wait_ge(in_loaded[b], 64 * i + 64)
                    pe.sem_inc(T["past"], 1)
                    nc.tensor.matmul(HID[b][0:H, :], wA[:, :], at[b][:, :], start=True, stop=True).then_inc(s["hid_ready"], 1)

                def weights(g, b, t):
                    pe.wait_ge(s["hid_done"], g + 1)
                    nc.tensor.matmul(WPS[t], hidT[b][:, t * P:(t + 1) * P], wB[:, :], start=True, stop=True).then_inc(s["w_ready"], 1)

                def sums(g, t):
                    q = t % 2
                    pe.wait_ge(s["p_ready"], tile(g, t) + 1)
                    if t >= 2:
                        pe.wait_ge(s["msg_ready"], tile(g, t) - 1)
                    else:
                        pe.wait_ge(s["msg_ready"], tile(g, 0))
                    o, p, sk = AGG[q], prod[q], Sk[q]
                    nc.tensor.matmul(o[:, A0:D0], sk[:, 0, :], p[:, 0:PD], start=True, stop=False)
                    if count:
                        nc.tensor.matmul(o[:, X0:B0], sk[:, 4, :], T["ones"][:, 0:96], start=False, stop=False)
                    for k in range(3):
                        nc.tensor.matmul(o[:, B0 + NS * k:B0 + NS * (k + 1)], sk[:, k + 1, :], p[:, PB:PB + NS], start=False, stop=False)
                        if cross:
                            j, n = (k + 2) % 3, (k + 1) % 3
                            nc.tensor.matmul(o[:, X0 + NV * n:X0 + NV * (n + 1)], sk[:, k + 1, :], p[:, PE_ + NV * j:PE_ + NV * (j + 1)], start=False, stop=False)
                            nc.tensor.matmul(o[:, X0 + NV * j:X0 + NV * (j + 1)], sk[:, k + 1, :], p[:, PN + NV * n:PN + NV * (n + 1)], start=False, stop=False)
                        ins = nc.tensor.matmul(o[:, D0:X0], sk[:, k + 1, :], p[:, PD + NV * k:PD + NV * (k + 1)], start=False, stop=(k == 2))
                    ins.then_inc(s["agg_ready"], 1)

                pe.wait_ge(s["w_loaded"], 32)
                if cross:
                    pe.wait_ge(s["neg_ready"], 1)
                hidden(0, 0)
                for t in range(TG):
                    weights(0, 0, t)
                with pe.Fori(0, last) as i:
                    hidden(i, 1)
                    for t in range(TG):
                        sums(i * 2, t)
                        weights(i * 2 + 1, 1, t)
                    hidden(i + 1, 0)
                    for t in range(TG):
                        sums(i * 2 + 1, t)
                        weights(i * 2 + 2, 0, t)
                hidden(last, 1)
                for t in range(TG):
                    sums(2 * last, t)
                    weights(2 * last + 1, 1, t)
                for t in range(TG):
                    sums(2 * last + 1, t)
        T["gathered_count"] += 16 * TG * S.pairs
        T["added_count"] += 16 * S.groups


def node_post(nc, T, D, S, L, agg, w_dram, scale_dram, skip, gated, attr):
    M = w_dram.shape[1]
    KC = MSG // 4
    names = ["w_loaded", "w_scaled", "in_free", "in_loaded", "sum_ready", "dve_step", "tr_ready", "tr_copied", "out_ready",
             "out_copied", "pre_ready", "sig_ready"]
    with phase(nc, names) as s, ExitStack() as st:
        def sb(n, sh, dt=F32):
            return st.enter_context(nc.sbuf_tensor(f"{L}post_{n}", sh, dt))
        w = sb("w", [KC, 4, M])
        rs = sb("rs", [KC, 4])
        part = [sb(f"part{q}", [P, NB, MSG]) for q in range(COPIES)]
        mT = [sb(f"mT{q}", [KC, 4, P]) for q in range(2)]
        o = sb("o", [P, NB, M])
        sg = sb("sg", [P, NB, 96])
        TR = [T["bank"][6], T["bank"][7]]
        OUT = [T["bank"][4], T["bank"][5]]
        per = (6 if attr else 5) if gated else 11
        with nc.Block() as block:
            @block.sync
            def _(sp):
                sp.dma_start(w[:, :, :], w_dram.rearrange("(q k) m -> k q m", k=KC)).then_inc(s["w_loaded"], 16)
                sp.dma_start(rs[:, :], scale_dram.rearrange("(q k) o -> k (q o)", k=KC)).then_inc(s["w_loaded"], 16)
                with sp.Fori(0, S.node_groups) as g:
                    sp.wait_ge(s["in_free"], g)
                    sp.sem_inc(T["past"], 1)
                    for q in range(COPIES):
                        rows = agg[q][0:S.node_rows, :].rearrange("(t p) f -> p t f", p=P)
                        sp.dma_start(part[q][:, :, :], rows[:, bass.ds(g * NB, NB), :]).then_inc(s["in_loaded"], 16)

            @block.vector
            def _(dve):
                dve.wait_ge(s["w_loaded"], 32)
                for q in range(4):
                    nc.vector.tensor_scalar(w[:, q, :], w[:, q, :], rs[:, q:q + 1], None, ALU.mult).then_inc(s["w_scaled"], 1)
                with dve.Fori(0, S.node_groups) as g:
                    c = Chain(dve, s["dve_step"], per, g)
                    dve.wait_ge(s["in_loaded"], 64 * g + 64)
                    c.link(nc.vector.tensor_tensor(part[0][:, :, :], part[0][:, :, :], part[1][:, :, :], ALU.add))
                    c.link(nc.vector.tensor_tensor(part[2][:, :, :], part[2][:, :, :], part[3][:, :, :], ALU.add))
                    c.link(nc.vector.tensor_tensor(part[0][:, :, :], part[0][:, :, :], part[2][:, :, :], ALU.add))
                    if not gated:
                        c.link(nc.vector.tensor_scalar(sg[:, :, 0:1], part[0][:, :, X0:X0 + 1], 1.0, None, ALU.max))
                        c.link(nc.vector.reciprocal(sg[:, :, 1:2], sg[:, :, 0:1]))
                        c.link(nc.vector.tensor_tensor(part[0][:, :, :], part[0][:, :, :], sg[:, :, 1:2].to_broadcast([P, NB, MSG]), ALU.mult))
                    dve.sem_inc(s["sum_ready"], 1)
                    for t in range(NB):
                        dve.wait_ge(s["out_ready"], g * NB + t + 1)
                        nc.vector.tensor_copy(o[:, t, :], OUT[t % 2][:, 0:M]).then_inc(s["out_copied"], 1)
                    dve.wait_ge(s["out_copied"], g * NB + NB)
                    x = T["x"][:, bass.ds(g * NB, NB), :]
                    if attr:
                        a = T["a"][:, bass.ds(g * NB, NB)].unsqueeze(2).to_broadcast([P, NB, M])
                        c.link(nc.vector.tensor_tensor(o[:, :, :], o[:, :, :], a, ALU.mult))
                    if gated:
                        sk = skip[:, bass.ds(g * NB, NB), :]
                        nc.vector.tensor_tensor(o[:, :, :], o[:, :, :], sk, ALU.add).then_inc(s["pre_ready"], 1)
                        dve.wait_ge(s["sig_ready"], g + 1)
                        c.link(nc.vector.tensor_tensor(o[:, :, 0:NS], o[:, :, 0:NS], sg[:, :, 0:NS], ALU.mult))
                        for t in range(NB):
                            nc.vector.tensor_tensor(o[:, t, 96:192].rearrange("p (c k) -> p c k", k=3), o[:, t, 96:192].rearrange("p (c k) -> p c k", k=3),
                                                    sg[:, t, NS:96].unsqueeze(2).to_broadcast([P, NV, 3]), ALU.mult)
                        c.link(nc.vector.tensor_tensor(x[:, :, 0:NS], x[:, :, 0:NS], o[:, :, 0:NS], ALU.add))
                        nc.vector.tensor_tensor(x[:, :, NS:FEAT], x[:, :, NS:FEAT], o[:, :, 96:192], ALU.add).then_inc(s["in_free"], 1)
                    else:
                        sk = skip[:, bass.ds(g * NB, NB), :]
                        c.link(nc.vector.tensor_copy(sg[:, :, 3:4], o[:, :, FEAT:FEAT + 1]))
                        c.link(nc.vector.tensor_tensor(o[:, :, 0:FEAT], o[:, :, 0:FEAT], sg[:, :, 3:4].to_broadcast([P, NB, FEAT]), ALU.mult))
                        c.link(nc.vector.tensor_tensor(o[:, :, 0:FEAT], o[:, :, 0:FEAT], sk[:, :, 0:FEAT], ALU.add))
                        c.link(nc.vector.tensor_tensor(x, x, o[:, :, 0:FEAT], ALU.add))
                        dve.sem_inc(s["in_free"], 1)
                    c.end()

            @block.scalar
            def _(act):
                with act.Fori(0, S.node_groups) as g:
                    for t in range(NB):
                        act.wait_ge(s["tr_ready"], g * NB + t + 1)
                        if t >= 2:
                            act.wait_ge(s["out_ready"], g * NB + t - 1)
                        else:
                            act.wait_ge(s["out_ready"], g * NB)
                        nc.scalar.activation(mT[t % 2][:, :, :], TR[t % 2][0:KC, :].rearrange("p (q n) -> p q n", n=P), ACT.Copy).then_inc(s["tr_copied"], 1)
                    if gated:
                        act.wait_ge(s["pre_ready"], g + 1)
                        nc.scalar.activation(sg[:, :, :], o[:, :, 0:96], ACT.Sigmoid).then_inc(s["sig_ready"], 1)

            @block.tensor
            def _(pe):
                pe.wait_ge(s["w_scaled"], 4)
                with pe.Fori(0, S.node_groups) as g:
                    pe.wait_ge(s["sum_ready"], g + 1)
                    for t in range(NB):
                        pe.wait_ge(s["tr_copied"], g * NB + max(t - 1, 0))
                        pe.wait_ge(s["out_copied"], g * NB + max(t - 1, 0))
                        tr, ot = TR[t % 2], OUT[t % 2]
                        for q in range(4):
                            ins = nc.tensor.transpose(tr[0:KC, q * P:(q + 1) * P], part[0][:, t, q * KC:(q + 1) * KC], T["ident"][:, :])
                        ins.then_inc(s["tr_ready"], 1)
                        pe.wait_ge(s["tr_copied"], g * NB + t + 1)
                        for q in range(4):
                            ins = nc.tensor.matmul(ot[:, 0:M], mT[t % 2][:, q, :], w[:, q, :], start=(q == 0), stop=(q == 3))
                        ins.then_inc(s["out_ready"], 1)


def inverse_root(nc, c, y, v, t):
    yi = y[:, :].bitcast(I32)
    c.link(nc.vector.tensor_scalar(yi, v[:, :].bitcast(I32), 1, None, ALU.logical_shift_right))
    c.link(nc.vector.tensor_scalar(yi, yi, -1.0, float(0x5F3759DF), ALU.mult, ALU.add))
    for _ in range(3):
        c.link(nc.vector.tensor_tensor(t[:, :], y[:, :], y[:, :], ALU.mult))
        c.link(nc.vector.scalar_tensor_tensor(t[:, :], t[:, :], -0.5, v[:, :], ALU.mult, ALU.mult))
        c.link(nc.vector.scalar_tensor_tensor(y[:, :], t[:, :], 1.5, y[:, :], ALU.add, ALU.mult))


R_ = 2 * NS + 3 * NV + NV + 3 * NV
WIDE = NS + 5 * NV
HEADS, HD = 8, 8
MSG2 = FEAT + HEADS
BIG = 1.6e38


def message_phase(nc, T, D, S, table_s, table_d, direction5, values, scores):
    H = 64
    names = ["w_loaded", "centred", "in_free0", "in_free1", "in_loaded0", "in_loaded1", "h_ready", "square_ready",
             "norm_ready", "tr_ready", "hid_done", "w_ready", "dve_step", "r_ready", "rt_ready", "rt_copied", "u_ready",
             "tanh_ready", "v_ready", "stored0", "stored1", "ones_ready"]
    with phase(nc, names) as s, ExitStack() as st:
        def sb(n, sh, dt=F32):
            return st.enter_context(nc.sbuf_tensor(f"msg_{n}", sh, dt))
        in_free = [s["in_free0"], s["in_free1"]]
        in_loaded = [s["in_loaded0"], s["in_loaded1"]]
        gathered, fetched = T["gathered"], T["gathered_count"]
        stored = [s["stored0"], s["stored1"]]
        w1, w2, w3 = sb("w1", [H + 1, H]), sb("w2", [H + 1, H]), sb("w3", [H + 1, 224])
        wm = sb("wm", [H + 1, 2])
        gb = sb("gb", [H, 4])
        wl = sb("wl", [P, 3, 256])
        ls = sb("ls", [P, 3])
        lb = sb("lb", [1, 256])
        dots = sb("dots", [P, H])
        at = [sb(f"at{b}", [H + 1, GE]) for b in range(2)]
        mi = [sb(f"mi{b}", [P, 2 * TG], I32) for b in range(2)]
        y5 = [sb(f"y5{b}", [P, TG, 5]) for b in range(2)]
        Gs = [sb(f"Gs{b}", [P, TG, WIDE]) for b in range(2)]
        Gd = [sb(f"Gd{b}", [P, TG, WIDE]) for b in range(2)]
        V = [sb(f"V{b}", [P, TG, FEAT]) for b in range(2)]
        xn = sb("xn", [P, TG, H])
        sq = sb("sq", [P, TG, H])
        rstd, rad, tmp = sb("rstd", [P, TG]), sb("rad", [P, TG]), sb("tmp", [P, TG])
        hT = [sb(f"hT{q}", [H + 1, GE]) for q in range(2)]
        dc = sb("dc", [P, TG, 4 * NV])
        t1, t2 = sb("t1", [P, TG, 3 * NV]), sb("t2", [P, TG, 3 * NV])
        R = [sb(f"R{q}", [P, R_]) for q in range(2)]
        RT = [sb(f"RT{q}", [P, 3 * P]) for q in range(2)]
        th = [sb(f"th{q}", [P, H]) for q in range(2)]
        sm = sb("sm", [P, H])
        HB, TB = T["bank"][0], T["bank"][1]
        WB = [T["bank"][2], T["bank"][3]]
        RB = [T["bank"][4], T["bank"][5]]
        UB = [T["bank"][6], T["bank"][7]]
        loads = 11
        per = 2 * (2 * 13 + 7 + 5 * TG)

        with nc.Block() as block:
            @block.sync
            def _(sp):
                for dst, src in ((w1, D["L2_rw1"]), (w2, D["L2_rw2"]), (w3, D["L2_rw3"]), (gb, D["L2_gb"]), (lb, D["L2_lin_b"]),
                                 (ls, D["L2_lin_scale"])):
                    sp.dma_start(dst[:, :], src).then_inc(s["w_loaded"], 16)
                for q in range(3):
                    k = min(P, R_ - q * P)
                    sp.dma_start(wl[0:k, q, :], D["L2_lin"][q * P:q * P + k, :]).then_inc(s["w_loaded"], 16)
                sp.dma_start(dots[:, :], D["L2_dots"].partition_broadcast(P)).then_inc(s["w_loaded"], 16)
                sp.dma_start(t1[:, 0, 0:1], D["node_vec1"][0:P, :]).then_inc(s["w_loaded"], 16)
                with sp.Fori(0, S.pairs) as i:
                    for b in range(2):
                        g = i * 2 + b
                        sp.wait_ge(in_free[b], i)
                        sp.sem_inc(T["past"], 1)
                        sp.dma_start(at[b][:, :], D["attr64"][:, bass.ds(g * GE, GE)]).then_inc(in_loaded[b], 16)
                        sp.dma_start(mi[b][:, :], D["by_dst"][bass.ds(g * P, P), :]).then_inc(in_loaded[b], 16)
                        sp.dma_start(y5[b][:, :, :], direction5[bass.ds(g * P, P), :].rearrange("p (t k) -> p t k", k=5)).then_inc(in_loaded[b], 16)

            @block.gpsimd
            def _(pool):
                with pool.Fori(0, S.pairs) as i:
                    for b in range(2):
                        pool.wait_ge(in_loaded[b], 48 * i + 48)
                        pool.wait_ge(in_free[b], i)
                        pool.sem_inc(T["past"], 1)
                        for t in range(TG):
                            pool.indirect_dma_start(Gs[b][:, t, :], None, table_s, bass.IndirectOffsetOnAxis(mi[b][:, t:t + 1], 0)).then_inc(gathered[b], 16)
                            pool.indirect_dma_start(Gd[b][:, t, :], None, table_d, bass.IndirectOffsetOnAxis(mi[b][:, TG + t:TG + t + 1], 0)).then_inc(gathered[b], 16)

            @block.vector
            def _(dve):
                dve.wait_ge(s["w_loaded"], 16 * loads)
                for n, w in enumerate((w1, w2)):
                    nc.vector.reduce_sum(wm[:, n:n + 1], w[:, :], AX.X).then_inc(s["centred"], 1)
                dve.wait_ge(s["centred"], 2)
                nc.vector.tensor_scalar(wm[:, :], wm[:, :], 1.0 / H, None, ALU.mult).then_inc(s["centred"], 1)
                dve.wait_ge(s["centred"], 3)
                for n, w in enumerate((w1, w2)):
                    nc.vector.tensor_scalar(w[:, :], w[:, :], wm[:, n:n + 1], None, ALU.subtract).then_inc(s["centred"], 1)
                for q in range(3):
                    k = min(P, R_ - q * P)
                    nc.vector.tensor_scalar(wl[0:k, q, :], wl[0:k, q, :], ls[0:k, q:q + 1], None, ALU.mult).then_inc(s["centred"], 1)
                nc.vector.memset(hT[0][H:H + 1, :], 1.0).then_inc(s["ones_ready"], 1)
                nc.vector.memset(hT[1][H:H + 1, :], 1.0).then_inc(s["ones_ready"], 1)
                with dve.Fori(0, S.pairs) as i:
                    c = Chain(dve, s["dve_step"], per, i)
                    for b in range(2):
                        g = i * 2 + b
                        for n in range(2):
                            dve.wait_ge(s["square_ready"], 2 * g + n + 1)
                            c.link(nc.vector.reduce_sum(rstd[:, :], sq[:, :, :], AX.X))
                            c.link(nc.vector.tensor_scalar(rad[:, :], rstd[:, :], 1.0 / H, EPS, ALU.mult, ALU.add))
                            inverse_root(nc, c, rstd, rad, tmp)
                            nc.vector.tensor_tensor(xn[:, :, :], HB[:, 0:TG * H].rearrange("p (t h) -> p t h", h=H),
                                                    rstd[:, :].unsqueeze(2).to_broadcast([P, TG, H]), ALU.mult).then_inc(s["norm_ready"], 1)
                            if n == 0:
                                dve.wait_ge(in_loaded[b], 48 * i + 48)
                                dve.wait_ge(gathered[b], fetched + 32 * TG * i + 32 * TG)
                                c.link(nc.vector.tensor_tensor(Gs[b][:, :, :], Gs[b][:, :, :], Gd[b][:, :, :], ALU.add))
                                v = Gs[b][:, :, NS:WIDE]

                                def yb(k):
                                    return y5[b][:, :, k:k + 3].unsqueeze(3).to_broadcast([P, TG, 3, NV])

                                def three(x):
                                    return x.rearrange("p t (k c) -> p t k c", c=NV)
                                c.link(nc.vector.tensor_tensor(three(t1[:, :, :]), three(v[:, :, 0:96]), yb(0), ALU.mult))
                                c.link(nc.vector.tensor_tensor(t1[:, :, 0:NV], t1[:, :, 0:NV], t1[:, :, NV:2 * NV], ALU.add))
                                c.link(nc.vector.tensor_tensor(dc[:, :, 0:NV], t1[:, :, 0:NV], t1[:, :, 2 * NV:3 * NV], ALU.add))
                                c.link(nc.vector.tensor_tensor(three(t1[:, :, :]), three(v[:, :, NV:4 * NV]), yb(2), ALU.mult))
                                c.link(nc.vector.tensor_tensor(three(t2[:, :, :]), three(v[:, :, 2 * NV:5 * NV]), yb(1), ALU.mult))
                                c.link(nc.vector.tensor_tensor(dc[:, :, NV:4 * NV], t1[:, :, :], t2[:, :, :], ALU.subtract))
                        for t in range(TG + 1):
                            if t < TG:
                                q = t % 2
                                dve.wait_ge(s["w_ready"], g * TG + t + 1)
                                dve.wait_ge(s["rt_ready"], g * TG + max(t - 1, 0))
                                w, m = WB[q], Gs[b]
                                nc.vector.tensor_tensor(R[q][:, 0:2 * NS].rearrange("p (m c) -> p m c", c=NS), w[:, 0:2 * NS].rearrange("p (m c) -> p m c", c=NS),
                                                        m[:, t, 0:NS].unsqueeze(1).to_broadcast([P, 2, NS]), ALU.mult)
                                nc.vector.tensor_tensor(R[q][:, 128:224].rearrange("p (k c) -> p k c", c=NV), w[:, 128:160].unsqueeze(1).to_broadcast([P, 3, NV]),
                                                        m[:, t, NS:FEAT].rearrange("p (k c) -> p k c", c=NV), ALU.mult)
                                nc.vector.tensor_tensor(R[q][:, 224:256], w[:, 160:192], dc[:, t, 0:NV], ALU.mult)
                                c.link(nc.vector.tensor_tensor(R[q][:, 256:352].rearrange("p (k c) -> p k c", c=NV), w[:, 192:224].unsqueeze(1).to_broadcast([P, 3, NV]),
                                                               dc[:, t, NV:4 * NV].rearrange("p (k c) -> p k c", c=NV), ALU.mult))
                                dve.sem_inc(s["r_ready"], 1)
                            if t > 0:
                                r = t - 1
                                q = r % 2
                                dve.wait_ge(s["tanh_ready"], g * TG + r + 1)
                                if r == 0:
                                    dve.wait_ge(stored[b], 16 * i)
                                u, vt = UB[q], V[b]
                                c.link(nc.vector.tensor_scalar(th[q][:, :], th[q][:, :], 0.4, 0.6, ALU.mult, ALU.add))
                                c.link(nc.vector.tensor_tensor(th[q][:, :], th[q][:, :], dots[:, :], ALU.mult))
                                c.link(nc.vector.tensor_tensor(sm[:, :], th[q][:, :], u[:, 0:H], ALU.mult))
                                nc.vector.reduce_sum(scores[:, :, bass.ds(g * TG + r, 1)].rearrange("p h o -> p (h o)"), sm[:, :].rearrange("p (h k) -> p h k", k=HD), AX.X)
                                nc.vector.tensor_copy(vt[:, r, 0:NS], u[:, H:2 * H])
                                c.link(nc.vector.tensor_tensor(t1[:, r, :].rearrange("p (k c) -> p k c", c=NV), u[:, 128:160].unsqueeze(1).to_broadcast([P, 3, NV]),
                                                               y5[b][:, r, 0:3].unsqueeze(2).to_broadcast([P, 3, NV]), ALU.mult))
                                nc.vector.tensor_tensor(vt[:, r, NS:FEAT], u[:, 160:256], t1[:, r, :], ALU.add).then_inc(s["v_ready"], 1)
                        dve.wait_ge(s["v_ready"], g * TG + TG)
                        dve.sem_inc(in_free[b], 1)
                    c.end()

            @block.scalar
            def _(act):
                act.wait_ge(s["w_loaded"], 16 * loads)
                act.wait_ge(s["ones_ready"], 2)
                with act.Fori(0, S.pairs) as i:
                    for b in range(2):
                        g = i * 2 + b
                        for n in range(2):
                            act.wait_ge(s["h_ready"], 2 * g + n + 1)
                            act.wait_ge(s["norm_ready"], 2 * g + n)
                            nc.scalar.activation(sq[:, :, :], HB[:, 0:TG * H].rearrange("p (t h) -> p t h", h=H), ACT.Square).then_inc(s["square_ready"], 1)
                            act.wait_ge(s["tr_ready"], 2 * g + n + 1)
                            nc.scalar.activation(hT[n][0:H, :], TB[0:H, :], ACT.Silu, scale=gb[:, 2 * n:2 * n + 1], bias=gb[:, 2 * n + 1:2 * n + 2]).then_inc(s["hid_done"], 1)
                        for t in range(TG):
                            q = t % 2
                            act.wait_ge(s["rt_ready"], g * TG + t + 1)
                            act.wait_ge(s["u_ready"], g * TG + max(t - 1, 0))
                            nc.scalar.activation(RT[q][:, 0:2 * P], RB[q][:, 0:2 * P], ACT.Copy)
                            nc.scalar.activation(RT[q][0:96, 2 * P:3 * P], RB[q][0:96, 2 * P:3 * P], ACT.Copy).then_inc(s["rt_copied"], 1)
                            act.wait_ge(s["u_ready"], g * TG + t + 1)
                            act.wait_ge(s["v_ready"], g * TG + max(t - 1, 0))
                            nc.scalar.activation(th[q][:, :], UB[q][:, 0:H], ACT.Tanh, scale=0.5).then_inc(s["tanh_ready"], 1)
                        act.wait_ge(s["v_ready"], g * TG + TG)
                        act.dma_start(values[bass.ds(g * P, P), :].rearrange("p (t f) -> p t f", f=FEAT), V[b][:, :, :]).then_inc(stored[b], 16)
                for b in range(2):
                    act.wait_ge(stored[b], 16 * S.pairs)

            @block.tensor
            def _(pe):
                pe.wait_ge(s["w_loaded"], 16 * loads)
                pe.wait_ge(s["centred"], 8)
                pe.wait_ge(s["ones_ready"], 2)
                with pe.Fori(0, S.pairs) as i:
                    for b in range(2):
                        g = i * 2 + b
                        pe.wait_ge(in_loaded[b], 48 * i + 48)
                        for n in range(2):
                            w = (w1, w2)[n]
                            pe.wait_ge(s["norm_ready"], 2 * g + n)
                            if n == 1:
                                pe.wait_ge(s["hid_done"], 2 * g + 1)
                            for t in range(TG):
                                x = at[b] if n == 0 else hT[0]
                                ins = nc.tensor.matmul(HB[:, t * H:(t + 1) * H], x[:, t * P:(t + 1) * P], w[:, :], start=(t == 0), stop=(t == TG - 1))
                            ins.then_inc(s["h_ready"], 1)
                            pe.wait_ge(s["norm_ready"], 2 * g + n + 1)
                            pe.wait_ge(s["hid_done"], 2 * g + n)
                            pe.sem_inc(T["past"], 1)
                            for t in range(TG):
                                ins = nc.tensor.transpose(TB[0:H, t * P:(t + 1) * P], xn[:, t, :], T["ident"][:, :])
                            ins.then_inc(s["tr_ready"], 1)
                        pe.wait_ge(s["hid_done"], 2 * g + 2)

                        def weights(t):
                            pe.wait_ge(s["r_ready"], g * TG + max(t - 1, 0))
                            nc.tensor.matmul(WB[t % 2][:, 0:224], hT[1][:, t * P:(t + 1) * P], w3[:, :], start=True, stop=True).then_inc(s["w_ready"], 1)
                        weights(0)
                        weights(1)
                        for t in range(TG):
                            q = t % 2
                            pe.wait_ge(s["r_ready"], g * TG + t + 1)
                            pe.wait_ge(s["rt_copied"], g * TG + max(t - 1, 0))
                            for k in range(3):
                                n = min(P, R_ - k * P)
                                ins = nc.tensor.transpose(RB[q][0:n, k * P:(k + 1) * P], R[q][:, k * P:k * P + n], T["ident"][:, :])
                            ins.then_inc(s["rt_ready"], 1)
                            if t + 2 < TG:
                                weights(t + 2)
                            pe.wait_ge(s["rt_copied"], g * TG + t + 1)
                            pe.wait_ge(s["v_ready"], g * TG + max(t - 1, 0))
                            for k in range(3):
                                n = min(P, R_ - k * P)
                                nc.tensor.matmul(UB[q][:, 0:256], RT[q][0:n, k * P:(k + 1) * P], wl[0:n, k, :], start=(k == 0), stop=False)
                            nc.tensor.matmul(UB[q][:, 0:256], T["ones"][0:1, :], lb[:, :], start=False, stop=True).then_inc(s["u_ready"], 1)
        T["gathered_count"] += 32 * TG * S.pairs


def softmax_phase(nc, T, D, S, scores, by_head, corner, carry_d):
    chunks = P // HEADS
    n = S.edge_rows // chunks
    blk = S.pairs
    assert blk <= P and blk * 8 == S.tiles and n * chunks == S.edge_rows
    names = ["tr_ready", "tr_copied", "out0", "out1", "loaded", "dve_step", "exp_ready", "stored", "in0", "in1", "back_ready", "back_copied"]
    with phase(nc, names) as s, ExitStack() as st:
        def sb(nm, sh, dt=F32):
            return st.enter_context(nc.sbuf_tensor(f"soft_{nm}", sh, dt))
        keys = sb("keys", [P, n + 2], I32)
        a, pen, f = sb("a", [P, n]), sb("pen", [P, n]), sb("f", [P, n])
        em = sb("em", [P, 4])
        eh = sb("eh", [HEADS, chunks, 2])
        ch = sb("ch", [HEADS, chunks + 2])
        ini = sb("ini", [P, 1])
        back = [sb(f"back{q}", [P, 8, P]) for q in range(2)]
        BK = T["bank"]
        with nc.Block() as block:
            @block.sync
            def _(sp):
                for h in range(HEADS):
                    src = bass.AP(D["dst_wide"].tensor, 0, [[n, chunks], [1, n + 2]])
                    sp.dma_start(keys[h * chunks:(h + 1) * chunks, :], src).then_inc(s["loaded"], 16)
                for h in range(HEADS):
                    sp.wait_ge(s["tr_copied"], 2 * h + 2)
                    dst = by_head[h:h + 1, :].rearrange("o (k r e) -> (o r) k e", r=blk, e=P)
                    sp.dma_start(dst, back[h % 2][0:blk, :, :]).then_inc(s[f"out{h % 2}"], 16)
                sp.wait_ge(s["out0"], 16 * 4)
                sp.wait_ge(s["out1"], 16 * 4)
                sp.dma_start(a[:, :], by_head.rearrange("h (c n) -> (h c) n", n=n)).then_inc(s["loaded"], 16)
                for d in range(2):
                    sp.wait_ge(s["dve_step"], 5 + 9 * d)
                    sp.dma_start(corner, em[:, 2 * d:2 * d + 2]).then_inc(s["stored"], 16)
                    sp.wait_ge(s["stored"], 16 + 32 * d)
                    sp.dma_start(eh[:, :, :], corner.rearrange("(h c) k -> h c k", h=HEADS)).then_inc(s["loaded"], 16)
                    sp.wait_ge(s["dve_step"], 7 + 9 * d)
                    o = 0 if d == 0 else 2
                    sp.dma_start(carry_d, ch[:, o:o + chunks]).then_inc(s["stored"], 16)
                    sp.wait_ge(s["stored"], 32 + 32 * d)
                    sp.dma_start(ini[:, :], carry_d.rearrange("h (c o) -> (h c) o", o=1)).then_inc(s["loaded"], 16)
                sp.wait_ge(s["exp_ready"], 1)
                sp.dma_start(by_head.rearrange("h (c n) -> (h c) n", n=n), a[:, :]).then_inc(s["stored"], 16)
                sp.wait_ge(s["stored"], 80)
                for h in range(HEADS):
                    if h >= 2:
                        sp.wait_ge(s["back_ready"], h - 1)
                    src = by_head[h:h + 1, :].rearrange("o (k r e) -> (o r) k e", r=blk, e=P)
                    sp.dma_start(back[h % 2][0:blk, :, :], src).then_inc(s[f"in{h % 2}"], 16)

            @block.tensor
            def _(pe):
                for h in range(HEADS):
                    for half in range(2):
                        m = 2 * h + half
                        if m >= 2:
                            pe.wait_ge(s["tr_copied"], m - 1)
                        for k in range(4):
                            kk = 4 * half + k
                            ins = nc.tensor.transpose(BK[m % 2][0:blk, k * P:(k + 1) * P], scores[:, h, kk * blk:(kk + 1) * blk], T["ident"][:, :])
                        ins.then_inc(s["tr_ready"], 1)
                for h in range(HEADS):
                    pe.wait_ge(s[f"in{h % 2}"], 16 * (h // 2 + 1))
                    for half in range(2):
                        m = 2 * h + half
                        if m >= 2:
                            pe.wait_ge(s["back_copied"], m - 1)
                        for k in range(4):
                            kk = 4 * half + k
                            ins = nc.tensor.transpose(BK[2 + m % 2][:, k * P:k * P + blk], back[h % 2][0:blk, kk, :], T["ident"][0:blk, 0:blk])
                        if half == 0:
                            ins.then_inc(s["tr_ready"], 1)
                        else:
                            ins.then_inc(s["back_ready"], 1)

            @block.vector
            def _(dve):
                c = Chain(dve, s["dve_step"])
                dve.wait_ge(s["loaded"], 16 * HEADS + 16)
                c.link(nc.vector.tensor_tensor(pen[:, :], keys[:, 1:n + 1], keys[:, 0:n], ALU.is_equal))
                c.link(nc.vector.tensor_scalar(pen[:, :], pen[:, :], 1.0, BIG, ALU.subtract, ALU.mult))
                c.link(nc.vector.tensor_reduce(em[:, 0:1], pen[:, :], AX.X, ALU.min))
                c.link(nc.vector.tensor_tensor_scan(f[:, :], pen[:, :], a[:, :], -BIG, ALU.add, ALU.max))
                c.link(nc.vector.tensor_copy(em[:, 1:2], f[:, n - 1:n]))
                dve.wait_ge(s["loaded"], 16 * HEADS + 32)
                c.link(nc.vector.memset(ch[:, :], -BIG))
                c.link(nc.vector.tensor_tensor_scan(ch[:, 1:chunks + 1], eh[:, :, 0], eh[:, :, 1], -BIG, ALU.add, ALU.max))
                dve.wait_ge(s["loaded"], 16 * HEADS + 48)
                c.link(nc.vector.tensor_tensor_scan(f[:, :], pen[:, :], a[:, :], ini[:, 0:1], ALU.add, ALU.max))
                c.link(nc.vector.tensor_tensor(pen[:, :], keys[:, 1:n + 1], keys[:, 2:n + 2], ALU.is_equal))
                c.link(nc.vector.tensor_scalar(pen[:, :], pen[:, :], 1.0, BIG, ALU.subtract, ALU.mult))
                c.link(nc.vector.tensor_reduce(em[:, 2:3], pen[:, :], AX.X, ALU.min))
                m = keys[:, 0:n].bitcast(F32)
                c.link(nc.vector.tensor_tensor_scan(m[:, ::-1], pen[:, ::-1], f[:, ::-1], -BIG, ALU.add, ALU.max))
                c.link(nc.vector.tensor_copy(em[:, 3:4], m[:, 0:1]))
                c.link(nc.vector.memset(ch[:, :], -BIG))
                dve.wait_ge(s["loaded"], 16 * HEADS + 64)
                c.link(nc.vector.tensor_tensor_scan(ch[:, chunks:0:-1], eh[:, ::-1, 0], eh[:, ::-1, 1], -BIG, ALU.add, ALU.max))
                c.link(nc.vector.tensor_copy(em[:, 0:1], em[:, 1:2]))
                dve.wait_ge(s["loaded"], 16 * HEADS + 80)
                c.link(nc.vector.tensor_tensor_scan(m[:, ::-1], pen[:, ::-1], f[:, ::-1], ini[:, 0:1], ALU.add, ALU.max))
                c.link(nc.vector.tensor_tensor(a[:, :], a[:, :], m[:, :], ALU.subtract))

            @block.scalar
            def _(act):
                for m in range(2 * HEADS):
                    h, half = m // 2, m % 2
                    act.wait_ge(s["tr_ready"], m + 1)
                    if half == 0 and h >= 2:
                        act.wait_ge(s[f"out{h % 2}"], 16 * (h // 2))
                    nc.scalar.activation(back[h % 2][0:blk, 4 * half:4 * half + 4, :], BK[m % 2][0:blk, :].rearrange("p (k e) -> p k e", e=P), ACT.Copy).then_inc(s["tr_copied"], 1)
                act.wait_ge(s["dve_step"], 18)
                nc.scalar.activation(a[:, :], a[:, :], ACT.Exp).then_inc(s["exp_ready"], 1)
                for m in range(2 * HEADS):
                    h, half = m // 2, m % 2
                    if half == 0:
                        act.wait_ge(s["tr_ready"], 2 * HEADS + h + 1)
                    else:
                        act.wait_ge(s["back_ready"], h + 1)
                    nc.scalar.activation(scores[:, h, 4 * half * blk:(4 * half + 4) * blk].rearrange("p (k r) -> p k r", r=blk),
                                         BK[2 + m % 2][:, :].rearrange("p (k e) -> p k e", e=P)[:, :, 0:blk], ACT.Copy).then_inc(s["back_copied"], 1)
                act.wait_ge(s["back_copied"], 2 * HEADS)


def attend_phase(nc, T, D, S, values, scores, agg):
    names = ["in_free0", "in_free1", "in_loaded0", "in_loaded1", "dve_step", "p_ready", "agg_ready", "msg_ready", "idx_ready"]
    with phase(nc, names) as s, ExitStack() as st:
        def sb(n, sh, dt=F32):
            return st.enter_context(nc.sbuf_tensor(f"att_{n}", sh, dt))
        in_free = [s["in_free0"], s["in_free1"]]
        in_loaded = [s["in_loaded0"], s["in_loaded1"]]
        added, summed = T["added"], T["added_count"]
        row = [sb(f"row{b}", [P, GE], I32) for b in range(2)]
        mi = [sb(f"mi{b}", [P, 2 * TG], I32) for b in range(2)]
        V = [sb(f"V{b}", [P, TG, FEAT]) for b in range(2)]
        keyf = [sb(f"keyf{b}", [P, TG]) for b in range(2)]
        cnt = [sb(f"cnt{b}", [P, 2, TG]) for b in range(2)]
        idx = [[sb(f"idx{b}{t}", [P, 1], I32) for t in range(TG)] for b in range(2)]
        Sk = [sb(f"S{b}", [P, TG, P]) for b in range(2)]
        junk = sb("junk", [P, P])
        prod = [sb(f"prod{b}", [P, TG, MSG2]) for b in range(2)]
        msg = [sb(f"msg{t}", [P, MSG2]) for t in range(TG)]
        AGG = [T["bank"][4], T["bank"][5]]
        steps = 2 + 2 * TG
        last = S.pairs - 1
        with nc.Block() as block:
            @block.sync
            def _(sp):
                with sp.Fori(0, S.pairs) as i:
                    for b in range(2):
                        g = i * 2 + b
                        sp.wait_ge(in_free[b], i)
                        sp.sem_inc(T["past"], 1)
                        sp.dma_start(V[b][:, :, :], values[bass.ds(g * P, P), :].rearrange("p (t f) -> p t f", f=FEAT)).then_inc(in_loaded[b], 16)
                        sp.dma_start(mi[b][:, :], D["by_dst"][bass.ds(g * P, P), :]).then_inc(in_loaded[b], 16)
                        sp.dma_start(row[b][:, :], D["dst_row"][:, bass.ds(g * GE, GE)].partition_broadcast(P)).then_inc(in_loaded[b], 16)

            @block.gpsimd
            def _(pool):
                with pool.Fori(0, S.pairs) as i:
                    for b in range(2):
                        g = i * 2 + b
                        pool.wait_ge(s["idx_ready"], g + 1)
                        for t in range(TG):
                            pool.wait_ge(s["msg_ready"], g * TG + t + 1)
                            pool.wait_ge(added[t], summed + 16 * g)
                            pool.sem_inc(T["past"], 1)
                            pool.indirect_dma_start(agg[t], bass.IndirectOffsetOnAxis(idx[b][t][:, 0:1], 0), msg[t][:, :], None,
                                                    compute_op=ALU.add).then_inc(added[t], 16)
                for t in range(TG):
                    pool.wait_ge(added[t], summed + 16 * S.groups)

            @block.vector
            def _(dve):
                with dve.Fori(0, S.pairs) as i:
                    c = Chain(dve, s["dve_step"], 2 * steps, i)
                    for b in range(2):
                        g = i * 2 + b
                        dve.wait_ge(in_loaded[b], 48 * i + 48)
                        dve.wait_ge(s["agg_ready"], 2 * TG * i)
                        c.link(nc.vector.tensor_copy(keyf[b][:, :], mi[b][:, TG:2 * TG]))
                        e = scores[:, :, bass.ds(g * TG, TG)]
                        nc.vector.tensor_copy(prod[b][:, :, FEAT:MSG2], e.rearrange("p h t -> p t h"))
                        nc.vector.tensor_tensor(prod[b][:, :, 0:NS].rearrange("p t (h k) -> p t h k", k=HD), V[b][:, :, 0:NS].rearrange("p t (h k) -> p t h k", k=HD),
                                                e.rearrange("p h t -> p t h").unsqueeze(3).to_broadcast([P, TG, HEADS, HD]), ALU.mult)
                        for t in range(TG):
                            r = row[b][:, t * P:(t + 1) * P]
                            et = scores[:, :, bass.ds(g * TG + t, 1)].rearrange("p h o -> p (h o)")
                            nc.vector.tensor_tensor(prod[b][:, t, NS:FEAT].rearrange("p (k h j) -> p k h j", k=3, j=NV // HEADS),
                                                    V[b][:, t, NS:FEAT].rearrange("p (k h j) -> p k h j", k=3, j=NV // HEADS),
                                                    et.unsqueeze(1).unsqueeze(3).to_broadcast([P, 3, HEADS, NV // HEADS]), ALU.mult)
                            nc.vector.tensor_scalar(Sk[b][:, t, :], r, keyf[b][:, t:t + 1], None, ALU.is_equal).then_inc(s["p_ready"], 1)
                            c.link(nc.vector.scalar_tensor_tensor(junk[:, :], r, keyf[b][:, t:t + 1], T["lower"][:, :], ALU.is_equal, ALU.mult,
                                                                  accum_out=cnt[b][:, 0, t:t + 1]))
                        c.link(nc.vector.tensor_tensor(cnt[b][:, 1, :], T["spare"][:, :], keyf[b][:, :], ALU.subtract))
                        dve.wait_ge(s["p_ready"], g * TG + TG)
                        nc.vector.tensor_scalar(cnt[b][:, 0, :], cnt[b][:, 0, :], 0.5, None, ALU.is_gt).then_inc(in_free[b], 1)
                        dve.wait_ge(in_free[b], i + 1)
                        for t in range(TG):
                            dve.wait_ge(added[t], summed + 32 * i)
                            c.link(nc.vector.scalar_tensor_tensor(idx[b][t][:, :], cnt[b][:, 0, t:t + 1], cnt[b][:, 1, t:t + 1], keyf[b][:, t:t + 1],
                                                                  ALU.mult, ALU.add))
                        dve.sem_inc(s["idx_ready"], 1)
                    c.end()

            @block.scalar
            def _(act):
                with act.Fori(0, S.groups) as g:
                    for t in range(TG):
                        act.wait_ge(s["agg_ready"], g * TG + t + 1)
                        act.wait_ge(added[t], summed + 16 * g)
                        nc.scalar.activation(msg[t][:, :], AGG[t % 2][:, 0:MSG2], ACT.Copy).then_inc(s["msg_ready"], 1)

            @block.tensor
            def _(pe):
                with pe.Fori(0, S.pairs) as i:
                    for b in range(2):
                        g = i * 2 + b
                        for t in range(TG):
                            pe.wait_ge(s["p_ready"], g * TG + t + 1)
                            pe.wait_ge(s["msg_ready"], g * TG + max(t - 1, 0))
                            nc.tensor.matmul(AGG[t % 2][:, 0:MSG2], Sk[b][:, t, :], prod[b][:, t, :], start=True, stop=True).then_inc(s["agg_ready"], 1)
        T["added_count"] += 16 * S.groups


def transformer_post(nc, T, D, S, agg, h_in):
    stages = [(FEAT, FEAT, "L2_proj"), (FEAT, 384, "L2_f1"), (320, FEAT, "L2_f2")]
    names = ["w_loaded", "in_loaded", "in_free", "dve_step", "in_ready", "tr_ready", "tr_copied", "out_ready", "out_copied",
             "var_ready", "root_ready", "pre_ready", "act_done"]
    with phase(nc, names) as s, ExitStack() as st:
        def sb(n, sh, dt=F32):
            return st.enter_context(nc.sbuf_tensor(f"tp_{n}", sh, dt))
        ws, bs = [], []
        for fi, fo, n in stages:
            ws.append([sb(f"w{n}{q}", [min(P, fi - q * P), fo]) for q in range(-(-fi // P))])
            bs.append(sb(f"b{n}", [P, fo]))
        nw = sum(len(w) for w in ws)
        pr = sb("pr", [P, 2 * FEAT])
        part = [sb(f"part{q}", [P, NB, MSG2]) for q in range(COPIES)]
        X = [sb("X0", [P, NB, FEAT]), sb("X1", [P, NB, FEAT]), sb("X2", [P, NB, 320])]
        O = [sb("O0", [P, NB, FEAT]), sb("O1", [P, NB, 384]), sb("O2", [P, NB, FEAT])]
        xm = sb("xm", [P, NB, FEAT])
        sq = sb("sq", [P, NB, FEAT])
        ev = sb("ev", [P, NB, 8])
        rd = sb("rd", [P, NB, HEADS])
        gate = sb("gate", [P, NB, 192])
        XT = [sb(f"XT{q}", [P, 3 * P]) for q in range(2)]
        TR = [T["bank"][6], T["bank"][7]]
        OUT = [T["bank"][4], T["bank"][5]]
        per = 22
        with nc.Block() as block:
            @block.sync
            def _(sp):
                for (fi, fo, n), w, b in zip(stages, ws, bs):
                    for q, part_w in enumerate(w):
                        k = part_w.shape[0]
                        sp.dma_start(part_w[:, :], D[n][q * P:q * P + k, :]).then_inc(s["w_loaded"], 16)
                    sp.dma_start(b[:, :], D[n + "_b"].partition_broadcast(P)).then_inc(s["w_loaded"], 16)
                sp.dma_start(pr[:, :], D["L2_ln2"].partition_broadcast(P)).then_inc(s["w_loaded"], 16)
                with sp.Fori(0, S.node_groups) as g:
                    sp.wait_ge(s["in_free"], g)
                    sp.sem_inc(T["past"], 1)
                    for q in range(COPIES):
                        rows = agg[q][0:S.node_rows, :].rearrange("(t p) f -> p t f", p=P)
                        sp.dma_start(part[q][:, :, :], rows[:, bass.ds(g * NB, NB), :]).then_inc(s["in_loaded"], 16)

            @block.vector
            def _(dve):
                dve.wait_ge(s["w_loaded"], 16 * (nw + 4))
                with dve.Fori(0, S.node_groups) as g:
                    c = Chain(dve, s["dve_step"], per, g)
                    a0 = T["a"][:, bass.ds(g * NB, NB)]

                    def product(stage):
                        dve.sem_inc(s["in_ready"], 1)
                        for t in range(NB):
                            m = 3 * NB * g + stage * NB + t
                            dve.wait_ge(s["out_ready"], m + 1)
                            fo = stages[stage][1]
                            nc.vector.tensor_tensor(O[stage][:, t, :], OUT[m_parity(stage, t)][:, 0:fo], bs[stage][:, :], ALU.add).then_inc(s["out_copied"], 1)
                        dve.wait_ge(s["out_copied"], 3 * NB * g + stage * NB + NB)

                    dve.wait_ge(s["in_loaded"], 64 * g + 64)
                    c.link(nc.vector.tensor_tensor(part[0][:, :, :], part[0][:, :, :], part[1][:, :, :], ALU.add))
                    c.link(nc.vector.tensor_tensor(part[2][:, :, :], part[2][:, :, :], part[3][:, :, :], ALU.add))
                    c.link(nc.vector.tensor_tensor(part[0][:, :, :], part[0][:, :, :], part[2][:, :, :], ALU.add))
                    c.link(nc.vector.tensor_scalar(rd[:, :, :], part[0][:, :, FEAT:MSG2], 1e-12, None, ALU.add))
                    c.link(nc.vector.reciprocal(rd[:, :, :], rd[:, :, :]))
                    nc.vector.tensor_tensor(X[0][:, :, 0:NS].rearrange("p t (h k) -> p t h k", k=HD), part[0][:, :, 0:NS].rearrange("p t (h k) -> p t h k", k=HD),
                                            rd[:, :, :].unsqueeze(3).to_broadcast([P, NB, HEADS, HD]), ALU.mult)
                    for t in range(NB):
                        ins = nc.vector.tensor_tensor(X[0][:, t, NS:FEAT].rearrange("p (k h j) -> p k h j", k=3, j=NV // HEADS),
                                                      part[0][:, t, NS:FEAT].rearrange("p (k h j) -> p k h j", k=3, j=NV // HEADS),
                                                      rd[:, t, :].unsqueeze(1).unsqueeze(3).to_broadcast([P, 3, HEADS, NV // HEADS]), ALU.mult)
                    c.link(ins)
                    dve.sem_inc(s["in_free"], 1)
                    product(0)
                    c.link(nc.vector.tensor_tensor(xm[:, :, :], O[0][:, :, :], h_in[:, bass.ds(g * NB, NB), 0:FEAT], ALU.add))
                    c.link(nc.vector.reduce_sum(ev[:, :, 0], xm[:, :, 0:NS], AX.X))
                    c.link(nc.vector.tensor_scalar(ev[:, :, 0], ev[:, :, 0], 1.0 / NS, None, ALU.mult))
                    nc.vector.tensor_copy(X[1][:, :, NS:FEAT], xm[:, :, NS:FEAT])
                    c.link(nc.vector.tensor_tensor(X[1][:, :, 0:NS], xm[:, :, 0:NS], ev[:, :, 0:1].to_broadcast([P, NB, NS]), ALU.subtract))
                    c.link(nc.vector.tensor_tensor(sq[:, :, :], X[1][:, :, :], X[1][:, :, :], ALU.mult))
                    c.link(nc.vector.reduce_sum(ev[:, :, 1], sq[:, :, 0:NS], AX.X))
                    c.link(nc.vector.reduce_sum(ev[:, :, 2], sq[:, :, NS:FEAT], AX.X))
                    c.link(nc.vector.tensor_scalar(ev[:, :, 1], ev[:, :, 1], 1.0 / NS, EPS, ALU.mult, ALU.add))
                    nc.vector.tensor_scalar(ev[:, :, 2], ev[:, :, 2], 1.0 / (3 * NV), EPS, ALU.mult, ALU.add).then_inc(s["var_ready"], 1)
                    dve.wait_ge(s["root_ready"], g + 1)
                    c.link(nc.vector.reciprocal(ev[:, :, 5:7], ev[:, :, 3:5]))
                    nc.vector.tensor_tensor(X[1][:, :, 0:NS], X[1][:, :, 0:NS], ev[:, :, 5:6].to_broadcast([P, NB, NS]), ALU.mult)
                    c.link(nc.vector.tensor_tensor(X[1][:, :, NS:FEAT], X[1][:, :, NS:FEAT], ev[:, :, 6:7].to_broadcast([P, NB, 96]), ALU.mult))
                    c.link(nc.vector.tensor_tensor(X[1][:, :, :], X[1][:, :, :], pr[:, 0:FEAT].unsqueeze(1).to_broadcast([P, NB, FEAT]), ALU.mult))
                    c.link(nc.vector.tensor_tensor(X[1][:, :, :], X[1][:, :, :], pr[:, FEAT:2 * FEAT].unsqueeze(1).to_broadcast([P, NB, FEAT]), ALU.add))
                    product(1)
                    nc.vector.tensor_tensor(O[1][:, :, :], O[1][:, :, :], a0.unsqueeze(2).to_broadcast([P, NB, 384]), ALU.mult).then_inc(s["pre_ready"], 1)
                    dve.wait_ge(s["act_done"], g + 1)
                    nc.vector.tensor_tensor(X[2][:, :, 0:P], O[1][:, :, 0:P], gate[:, :, 0:P], ALU.mult)
                    for t in range(NB):
                        ins = nc.vector.tensor_tensor(X[2][:, t, P:320].rearrange("p (k c) -> p k c", k=3), O[1][:, t, 192:384].rearrange("p (k c) -> p k c", k=3),
                                                      gate[:, t, P:192].unsqueeze(1).to_broadcast([P, 3, 64]), ALU.mult)
                    c.link(ins)
                    product(2)
                    c.link(nc.vector.tensor_tensor(O[2][:, :, :], O[2][:, :, :], a0.unsqueeze(2).to_broadcast([P, NB, FEAT]), ALU.mult))
                    c.link(nc.vector.tensor_tensor(O[2][:, :, :], O[2][:, :, :], xm[:, :, :], ALU.add))
                    x = T["x"][:, bass.ds(g * NB, NB), :]
                    c.link(nc.vector.tensor_tensor(x, x, O[2][:, :, :], ALU.add))
                    c.end()

            @block.scalar
            def _(act):
                with act.Fori(0, S.node_groups) as g:
                    for stage, (fi, fo, n) in enumerate(stages):
                        if stage == 1:
                            act.wait_ge(s["var_ready"], g + 1)
                            nc.scalar.activation(ev[:, :, 3:5], ev[:, :, 1:3], ACT.Sqrt).then_inc(s["root_ready"], 1)
                        if stage == 2:
                            act.wait_ge(s["pre_ready"], g + 1)
                            nc.scalar.activation(gate[:, :, :], O[1][:, :, 0:192], ACT.Sigmoid).then_inc(s["act_done"], 1)
                        for t in range(NB):
                            m = 3 * NB * g + stage * NB + t
                            q = m_parity(stage, t)
                            act.wait_ge(s["tr_ready"], m + 1)
                            if stage + t > 1 or t > 1:
                                act.wait_ge(s["out_ready"], m - 1)
                            else:
                                act.wait_ge(s["out_ready"], 3 * NB * g)
                            for k in range(len(ws[stage])):
                                r = ws[stage][k].shape[0]
                                ins = nc.scalar.activation(XT[q][0:r, k * P:(k + 1) * P], TR[q][0:r, k * P:(k + 1) * P], ACT.Copy)
                            ins.then_inc(s["tr_copied"], 1)

            @block.tensor
            def _(pe):
                pe.wait_ge(s["w_loaded"], 16 * (nw + 4))
                with pe.Fori(0, S.node_groups) as g:
                    for stage, (fi, fo, n) in enumerate(stages):
                        pe.wait_ge(s["in_ready"], 3 * g + stage + 1)
                        for t in range(NB):
                            m = 3 * NB * g + stage * NB + t
                            q = m_parity(stage, t)
                            if stage * NB + t > 1:
                                pe.wait_ge(s["out_copied"], m - 1)
                                pe.wait_ge(s["tr_copied"], m - 1)
                            else:
                                pe.wait_ge(s["out_copied"], 3 * NB * g)
                                pe.wait_ge(s["tr_copied"], 3 * NB * g)
                            for k, w in enumerate(ws[stage]):
                                r = w.shape[0]
                                ins = nc.tensor.transpose(TR[q][0:r, k * P:(k + 1) * P], X[stage][:, t, k * P:k * P + r], T["ident"][:, :])
                            ins.then_inc(s["tr_ready"], 1)
                            pe.wait_ge(s["tr_copied"], m + 1)
                            for k, w in enumerate(ws[stage]):
                                r = w.shape[0]
                                ins = nc.tensor.matmul(OUT[q][:, 0:fo], XT[q][0:r, k * P:(k + 1) * P], w[:, :], start=(k == 0), stop=(k == len(ws[stage]) - 1))
                            ins.then_inc(s["out_ready"], 1)


def m_parity(stage, t):
    return (stage * NB + t) % 2


def direction_phase(nc, D, S, direction4, direction5):
    n = S.groups * TG
    with phase(nc, ["loaded", "step", "radicand_ready", "root_ready", "stored"]) as s, ExitStack() as st:
        def sb(nm, sh, dt=F32):
            return st.enter_context(nc.sbuf_tensor(f"dir_{nm}", sh, dt))
        v, sq, r = sb("v", [P, n, 3]), sb("sq", [P, n, 3]), sb("r", [P, 2, n])
        y4, y5 = sb("y4", [P, n, 4]), sb("y5", [P, n, 5])
        with nc.Block() as block:
            @block.sync
            def _(sp):
                sp.dma_start(v[:, :, :].rearrange("p (g t) k -> p g (t k)", t=TG), D["attr3"].rearrange("(g p) c -> p g c", p=P)).then_inc(s["loaded"], 16)
                sp.wait_ge(s["step"], 9)
                sp.dma_start(direction4.rearrange("(g p) c -> p g c", p=P), y4[:, :, :].rearrange("p (g t) k -> p g (t k)", t=TG)).then_inc(s["stored"], 16)
                sp.dma_start(direction5.rearrange("(g p) c -> p g c", p=P), y5[:, :, :].rearrange("p (g t) k -> p g (t k)", t=TG)).then_inc(s["stored"], 16)
                sp.wait_ge(s["stored"], 32)

            @block.vector
            def _(dve):
                c = Chain(dve, s["step"])
                dve.wait_ge(s["loaded"], 16)
                c.link(nc.vector.tensor_tensor(sq[:, :, :], v[:, :, :], v[:, :, :], ALU.mult))
                c.link(nc.vector.reduce_sum(r[:, 0, :], sq[:, :, :], AX.X))
                c.link(nc.vector.tensor_scalar(r[:, 0, :], r[:, 0, :], 1.0 / 3.0, None, ALU.mult))
                nc.vector.tensor_scalar(r[:, 1, :], r[:, 0, :], 1e-12 / 3.0, None, ALU.add).then_inc(s["radicand_ready"], 1)
                dve.wait_ge(s["root_ready"], 1)
                c.link(nc.vector.reciprocal(sq[:, :, 0:2], sq[:, :, 0:2]))
                c.link(nc.vector.memset(y4[:, :, 0:1], 1.0))
                c.link(nc.vector.tensor_tensor(y4[:, :, 1:4], v[:, :, :], sq[:, :, 0:1].to_broadcast([P, n, 3]), ALU.mult))
                c.link(nc.vector.tensor_tensor(y5[:, :, 0:3], v[:, :, :], sq[:, :, 1:2].to_broadcast([P, n, 3]), ALU.mult))
                c.link(nc.vector.tensor_copy(y5[:, :, 3:5], y5[:, :, 0:2]))
                c.link(nc.vector.tensor_copy(r[:, 0, 0:1], r[:, 1, 0:1]))

            @block.scalar
            def _(act):
                act.wait_ge(s["radicand_ready"], 1)
                nc.scalar.activation(sq[:, :, 0:2].rearrange("p n k -> p k n"), r[:, :, :], ACT.Sqrt).then_inc(s["root_ready"], 1)


def store_phase(nc, T, S, out):
    full = S.nodes // P
    with phase(nc, ["stored"]) as s:
        with nc.Block() as block:
            @block.sync
            def _(sp):
                sp.dma_start(out[0:full * P, :].rearrange("(t p) f -> p t f", p=P), T["x"][:, 0:full, :]).then_inc(s["stored"], 16)
                rest = S.nodes - full * P
                if rest:
                    sp.dma_start(out[full * P:S.nodes, :], T["x"][0:rest, full, :]).then_inc(s["stored"], 16)
                sp.wait_ge(s["stored"], 32 if rest else 16)


def build(nc, D, out, S, layers):
    with ExitStack() as stack:
        def sb(n, sh, dt=F32):
            return stack.enter_context(nc.sbuf_tensor(n, sh, dt))
        T = {
            "x": sb("x_sb", [P, S.node_tiles, FEAT]),
            "a": sb("a_sb", [P, S.node_tiles]),
            "ident": sb("ident", [P, P]),
            "lower": sb("lower", [P, P]),
            "zero": sb("zero", [P, MSG]),
            "ones": sb("ones", [P, P]),
            "spare_i": sb("spare_i", [P, TG], I32),
            "spare": sb("spare", [P, TG]),
            "past": stack.enter_context(nc.semaphore("past")),
            "gathered_count": 0,
            "added_count": 0,
            "gathered": [stack.enter_context(nc.semaphore(f"gathered{b}")) for b in range(2)],
            "added": [stack.enter_context(nc.semaphore(f"added{t}")) for t in range(TG)],
            "bank": [stack.enter_context(nc.psum_tensor(f"bank{n}", [P, 512], F32)) for n in range(8)],
        }
        skip = sb("skip", [P, S.node_tiles, 192])

        def dram(n, sh, dt=F32):
            return nc.dram_tensor(n, sh, dt, kind="Internal").ap()
        agg = [dram(f"agg{q}", [S.agg_rows, MSG]) for q in range(COPIES)]
        table = dram("table", [S.node_rows, FEAT])
        load_constants(nc, T, D)
        if 0 in layers:
            zero_phase(nc, T, agg, MSG)
            node_pre(nc, T, D, S, "L0", D["L0_pre"], D["L0_pre_scale"], [table], FEAT, skip, True)
            edge_pass(nc, T, D, S, "L0", D["by_dst"], D["attr4"], D["dst_row"], D["attr64"][0:64, :], D["L0_fc1"], D["L0_fc2"],
                      table, agg, ACT.Silu, 1 / 8, True, False)
            node_post(nc, T, D, S, "L0", agg, D["L0_post"], D["L0_post_scale"], skip, True, True)
        if 1 in layers:
            zero_phase(nc, T, agg, MSG)
            node_pre(nc, T, D, S, "L1", D["L1_pre"], D["L1_pre_scale"], [table], FEAT, skip, True)
            edge_pass(nc, T, D, S, "L1", D["by_dst"], D["attr4"], D["dst_row"], D["attr16"], D["L1_fc1"], D["L1_fc2"],
                      table, agg, ACT.Silu, 1 / 4, False, True)
            node_post(nc, T, D, S, "L1", agg, D["L1_post"], D["L1_post_scale"], skip, False, True)
        direction4 = dram("direction4", [S.groups * P, 4 * TG])
        direction5 = dram("direction5", [S.groups * P, 5 * TG])
        if 2 in layers or 3 in layers:
            direction_phase(nc, D, S, direction4, direction5)
        if 2 in layers:
            agg2 = [dram(f"agg2{q}", [S.agg_rows, MSG2]) for q in range(COPIES)]
            table_s, table_d = dram("table_s", [S.node_rows, WIDE]), dram("table_d", [S.node_rows, WIDE])
            values = dram("values", [S.groups * P, TG * FEAT])
            by_head = dram("by_head", [HEADS, S.edge_rows])
            corner, carry = dram("corner", [P, 2]), dram("carry", [HEADS, P // HEADS])
            zero_phase(nc, T, agg2, MSG2)
            node_pre(nc, T, D, S, "L2", D["L2_pre"], D["L2_pre_scale"], [table_s, table_d], 2 * WIDE, skip, False, (D["L2_ln1"], D["L2_pre_b"]))
            with nc.sbuf_tensor("scores", [P, HEADS, S.tiles], F32) as scores:
                message_phase(nc, T, D, S, table_s, table_d, direction5, values, scores)
                softmax_phase(nc, T, D, S, scores, by_head, corner, carry)
                attend_phase(nc, T, D, S, values, scores, agg2)
            transformer_post(nc, T, D, S, agg2, skip)
        if 3 in layers:
            zero_phase(nc, T, agg, MSG)
            node_pre(nc, T, D, S, "L3", D["L3_pre"], D["L3_pre_scale"], [table], FEAT, skip, False)
            edge_pass(nc, T, D, S, "L3", D["by_src"], direction4, D["src_row"], D["attr64"][0:64, :], D["L3_fc1"], D["L3_fc2"],
                      table, agg, ACT.Relu, 1.0, True, False)
            node_post(nc, T, D, S, "L3", agg, D["L3_post"], D["L3_post_scale"], skip, True, False)
        store_phase(nc, T, S, out)


def kron3(w):
    out = np.zeros((w.shape[0], 3, w.shape[1], 3), np.float32)
    for k in range(3):
        out[:, k, :, k] = w
    return out.reshape(3 * w.shape[0], 3 * w.shape[1])


def kron3_major(w):
    out = np.zeros((w.shape[0], 3, 3, w.shape[1]), np.float32)
    for k in range(3):
        out[:, k, k, :] = w
    return out.reshape(3 * w.shape[0], 3 * w.shape[1])


def pre_weights(ws_table, wv_table, ws_skip=None, wv_skip=None):
    parts = [np.zeros((FEAT, NS), np.float32), np.zeros((FEAT, 3 * NV), np.float32)]
    parts[0][0:NS] = ws_table
    parts[1][NS:] = kron3_major(wv_table)
    if ws_skip is not None:
        a = np.zeros((FEAT, ws_skip.shape[1]), np.float32)
        a[0:NS] = ws_skip
        b = np.zeros((FEAT, 3 * NV), np.float32)
        b[NS:] = kron3(wv_skip)
        parts += [a, b]
    return np.concatenate(parts, 1)


def post_weights(ws, wv, cross, extra=None):
    cols = ws.shape[1]
    out = np.zeros((MSG, cols + 3 * NV + (1 if extra is not None else 0)), np.float32)
    out[A0:C0, 0:cols] = ws[0:NS]
    out[D0:X0, 0:cols] = ws[NS:]
    for k in range(3):
        out[B0 + NS * k:B0 + NS * (k + 1), cols + k:cols + 96:3] = wv[0:NS]
        out[C0 + NV * k:C0 + NV * (k + 1), cols + k:cols + 96:3] = wv[NS:NS + NV]
        if cross:
            out[X0 + NV * k:X0 + NV * (k + 1), cols + k:cols + 96:3] = wv[NS + NV:]
    if extra is not None:
        out[A0:C0, -1:] = extra[0:NS]
        out[D0:X0, -1:] = extra[NS:]
    return out


def mid_scales(s, v, dot, cross):
    out = np.full((MSG, 1), v, np.float32)
    out[A0:C0] = s
    out[D0:X0] = s * dot
    out[X0:B0] = v * cross
    return out


def half_scales(s, v):
    return np.concatenate([np.full((NS, 1), s, np.float32), np.full((3 * NV, 1), v, np.float32)])


def rows_of(a, count, fill):
    out = np.full((count,) + a.shape[1:], fill, a.dtype)
    out[0:len(a)] = a
    return out


def by_group(a, S):
    k = a.shape[1]
    return np.ascontiguousarray(a.reshape(S.groups, TG, P, k).transpose(0, 2, 1, 3).reshape(S.groups * P, TG * k))


def doubled(w, cross):
    return np.concatenate([w, w[:, -NV:]], 1) if cross else w


def layout(inputs, S):
    n = {k: np.asarray(v) for k, v in inputs.items()}
    a = {}
    a["x"] = rows_of(n["x"], S.node_rows, 0)
    a["node_vec1"] = rows_of(n["node_vec1"], S.node_rows, 0)
    last = S.node_rows - 1
    src, dst = (rows_of(n[k].reshape(-1, 1), S.edge_rows, last) for k in ("src", "dst"))
    gs, gd = by_group(src, S), by_group(dst, S)
    a["by_dst"] = np.concatenate([gs, gd], 1)
    a["by_src"] = np.concatenate([gd, gs], 1)
    a["dst_row"], a["src_row"] = dst.reshape(1, -1), src.reshape(1, -1)
    a["attr4"] = by_group(rows_of(n["edge_attr_4"], S.edge_rows, 0), S)
    a["attr3"] = by_group(rows_of(n["edge_attr_3"], S.edge_rows, 1), S)
    e64 = rows_of(n["edge_attr_64"], S.edge_rows, 0).T
    a["attr64"] = np.concatenate([e64, np.ones((1, S.edge_rows), np.float32)])
    a["attr16"] = np.ascontiguousarray(rows_of(n["edge_attr_16"], S.edge_rows, 0).T)
    q = {k[7:]: v for k, v in n.items() if k.startswith("L0_gnn_")}
    a["L0_pre"] = pre_weights(q["lin1_ws"], q["lin1_wv"], q["sc_ws"], q["sc_wv"])
    a["L0_pre_scale"] = half_scales(NS ** -0.5, NV ** -0.5)
    a["L0_fc1"], a["L0_fc2"] = q["fc_w1"], doubled(q["fc_w2"], True)
    a["L0_post"] = post_weights(q["lin2_ws"], q["lin2_wv"], True)
    a["L0_post_scale"] = mid_scales(96 ** -0.5 / 32, 128 ** -0.5 / 32, 3 ** -0.5, 2 ** -0.5)
    q = {k[7:]: v for k, v in n.items() if k.startswith("L1_gnn_")}
    a["L1_pre"] = pre_weights(q["Wl1_0"], q["Wl1_1"], q["Wsc0"], q["Wsc1"])
    a["L1_pre_scale"] = a["L0_pre_scale"]
    a["L1_fc1"], a["L1_fc2"] = q["Wfc1"], q["Wfc2"]
    a["L1_post"] = post_weights(q["Wl2_s"], q["Wl2_v"], False, q["Wa"])
    a["L1_post_scale"] = mid_scales(96 ** -0.5 / 8, 96 ** -0.5 / 8, 3 ** -0.5, 1.0)
    a["dst_wide"] = np.concatenate([np.full((1, 1), -1, np.int32), a["dst_row"], np.full((1, 1), -1, np.int32)], 1)
    q = {k[7:]: v for k, v in n.items() if k.startswith("L2_gnn_")}
    def wide(ws, wv):
        m = pre_weights(ws, wv)
        return np.concatenate([m, m[:, NS:NS + 2 * NV]], 1)
    a["L2_pre"] = np.concatenate([wide(q["msrc_ws"], q["msrc_wv"]), wide(q["mdst_ws"], q["mdst_wv"])], 1)
    a["L2_pre_scale"] = half_scales(1.0, 1.0)
    a["L2_pre_b"] = np.zeros((1, 2 * WIDE), np.float32)
    a["L2_pre_b"][0, WIDE:WIDE + NS] = q["mdst_bs"]

    def norm_rows(w0, b0, w1):
        return np.concatenate([w0, np.repeat(w1, 3), b0, np.zeros(3 * NV, np.float32)])[None]
    a["L2_ln1"] = norm_rows(q["ln1_w0"], q["ln1_b0"], q["ln1_w1"])
    a["L2_ln2"] = norm_rows(q["ln2_w0"], q["ln2_b0"], q["ln2_w1"])
    a["L2_rw1"] = np.concatenate([q["rw1"], q["rb1"][None]])
    a["L2_rw2"] = np.concatenate([q["rw2"], q["rb2"][None]])
    a["L2_rw3"] = np.concatenate([q["rw3"], q["roff"][None]])
    a["L2_gb"] = np.stack([q["rg1"], q["rbe1"], q["rg2"], q["rbe2"]], 1)
    lin, sc = np.zeros((R_, 256), np.float32), np.ones((3 * P, 1), np.float32)
    lin[0:NS, 0:128] = q["lin_ws"][0:NS]
    lin[NS:2 * NS, 128:160] = q["lin_wv"][0:NS]
    lin[224:256, 0:128] = q["lin_ws"][NS:]
    sc[224:256] = 3 ** -0.5
    for k in range(3):
        lin[128 + NV * k:160 + NV * k, 160 + NV * k:192 + NV * k] = q["lin_wv"][NS:NS + NV]
        lin[256 + NV * k:288 + NV * k, 160 + NV * k:192 + NV * k] = q["lin_wv"][NS + NV:]
    sc[256:352] = 2 ** -0.5
    a["L2_lin"], a["L2_lin_scale"] = lin, np.ascontiguousarray(sc.reshape(3, P).T)
    a["L2_lin_b"] = np.zeros((1, 256), np.float32)
    a["L2_lin_b"][0, 0:128] = q["lin_bs"]
    a["L2_dots"] = q["alpha_dot"].reshape(1, -1)
    def vec_rows(w):
        return kron3_major(w.T).T
    proj = np.zeros((FEAT, FEAT), np.float32)
    proj[0:NS, 0:NS] = q["proj_ws"]
    proj[NS:, NS:] = vec_rows(q["proj_wv"])
    a["L2_proj"] = proj
    a["L2_proj_b"] = np.zeros((1, FEAT), np.float32)
    a["L2_proj_b"][0, 0:NS] = q["proj_bs"]
    f1 = np.zeros((FEAT, 384), np.float32)
    f1[0:NS, 0:192] = q["f1_ws"]
    f1[NS:, 192:] = kron3_major(q["f1_wv"])
    a["L2_f1"] = f1
    a["L2_f1_b"] = np.zeros((1, 384), np.float32)
    a["L2_f1_b"][0, 0:192] = q["f1_bs"]
    f2 = np.zeros((320, FEAT), np.float32)
    f2[0:128, 0:NS] = q["f2_ws"]
    f2[128:, NS:] = vec_rows(q["f2_wv"])
    a["L2_f2"] = f2
    a["L2_f2_b"] = np.zeros((1, FEAT), np.float32)
    a["L2_f2_b"][0, 0:NS] = q["f2_bs"]
    q = {k[7:]: v for k, v in n.items() if k.startswith("L3_gnn_")}
    a["L3_pre"] = pre_weights(q["W_nl0"], q["W_nl1"], q["W_skip0"], q["W_skip1"])
    a["L3_pre_scale"] = half_scales(1.0, 1.0)
    a["L3_fc1"], a["L3_fc2"] = q["W_fc1"], doubled(q["W_fc2"], True)
    a["L3_post"] = post_weights(q["W_out_s"], q["W_out_v"], True)
    a["L3_post_scale"] = mid_scales(1 / 32, 1 / 32, 3 ** -0.5, 2 ** -0.5)
    return a


LAYERS = (0, 1, 2, 3)


def kernel(**inputs):
    from concourse import bacc
    from concourse.bass_utils import run_bass_kernel_spmd
    S = Shapes(inputs["x"].shape[0], inputs["src"].shape[0])
    arrays = {k: np.ascontiguousarray(v) for k, v in layout(inputs, S).items()}
    nc = bacc.Bacc("TRN2", target_bir_lowering=False, num_devices=1)
    D = {k: nc.dram_tensor(f"in_{k}", v.shape, mybir.dt.from_np(v.dtype), kind="ExternalInput").ap() for k, v in arrays.items()}
    D["shapes"] = S
    out = nc.dram_tensor("out_x", (S.nodes, FEAT), F32, kind="ExternalOutput").ap()
    build(nc, D, out, S, LAYERS)
    r = run_bass_kernel_spmd(nc, [{f"in_{k}": v for k, v in arrays.items()}], core_ids=[0])
    return r.results[0]["out_x"]
```

```python
import numpy as np
import concourse.bass as bass
from concourse import mybir
from contextlib import ExitStack, contextmanager

F32 = mybir.dt.float32
I32 = mybir.dt.int32
ALU = mybir.AluOpType
ACT = mybir.ActivationFunctionType
AX = mybir.AxisListType

P = 128
TG = 4
GE = TG * P
NB = 5
NS, NV = 64, 32
FEAT = NS + 3 * NV
COPIES = TG
MSG = 480
MSG_COUNT = 388
A0, D0, B0, C0, X0 = 0, 64, 96, 288, 384
EPS = 1e-5


class Shapes:

    def __init__(self, nodes, edges):
        self.nodes, self.edges = nodes, edges
        self.node_groups = -(-nodes // (NB * P))
        self.node_tiles = self.node_groups * NB
        self.node_rows = self.node_tiles * P
        assert nodes < self.node_rows, "the last row takes the padding edges"
        self.agg_rows = self.node_rows + P
        self.pairs = -(-edges // (2 * GE))
        self.groups = 2 * self.pairs
        self.tiles = self.groups * TG
        self.edge_rows = self.tiles * P


class Chain:

    def __init__(self, engine, sem, per_iteration=0, iteration=0):
        self.engine, self.sem, self.per, self.it, self.n = engine, sem, per_iteration, iteration, 0

    def link(self, instruction):
        self.n += 1
        instruction.then_inc(self.sem, 1)
        self.engine.wait_ge(self.sem, self.it * self.per + self.n)

    def end(self):
        assert self.n == self.per, f"links of an iteration: {self.n}"


@contextmanager
def phase(nc, names):
    with ExitStack() as stack:
        sems = {n: stack.enter_context(nc.semaphore(n)) for n in names}
        stack.enter_context(nc.allow_non_contiguous_dma(reason="small strided loads"))
        yield sems
        for s in sems.values():
            nc.gpsimd.sem_clear(s)
        nc.all_engine_barrier()


def load_constants(nc, T, D):
    with phase(nc, ["const_loaded", "mask_step"]) as s:
        with nc.Block() as block:
            @block.sync
            def _(sp):
                sp.dma_start(T["x"][:, :, :], D["x"].rearrange("(t p) f -> p t f", p=P)).then_inc(s["const_loaded"], 16)
                sp.dma_start(T["a"][:, :], D["node_vec1"].rearrange("(t p) o -> p (t o)", p=P)).then_inc(s["const_loaded"], 16)
                sp.wait_ge(s["const_loaded"], 32)

            @block.gpsimd
            def _(pool):
                pool.memset(T["ident"][:, :], 0.0).then_inc(s["mask_step"], 1)
                pool.memset(T["lower"][:, :], 1.0).then_inc(s["mask_step"], 1)
                pool.memset(T["zero"][:, :], 0.0).then_inc(s["mask_step"], 1)
                pool.memset(T["ones"][:, :], 1.0).then_inc(s["mask_step"], 1)
                pool.iota(T["spare_i"][:, :], pattern=[[0, TG]], base=D["shapes"].node_rows, channel_multiplier=1).then_inc(s["mask_step"], 1)
                pool.wait_ge(s["mask_step"], 5)
                pool.affine_select(out=T["ident"][:, :], in_=T["ident"][:, :], compare_op=ALU.not_equal, fill=1.0,
                                   base=0, pattern=[[-1, P]], channel_multiplier=1).then_inc(s["mask_step"], 1)
                pool.affine_select(out=T["lower"][:, :], in_=T["lower"][:, :], compare_op=ALU.is_gt, fill=0.0,
                                   base=0, pattern=[[-1, P]], channel_multiplier=1).then_inc(s["mask_step"], 1)
                pool.tensor_copy(T["spare"][:, :], T["spare_i"][:, :]).then_inc(s["mask_step"], 1)
                pool.wait_ge(s["mask_step"], 8)


def zero_phase(nc, T, tables, width):
    with phase(nc, ["zeroed"]) as s:
        with nc.Block() as block:
            @block.sync
            def _(sp):
                for table in tables:
                    rows = table.shape[0] // P
                    zeros = T["zero"][:, 0:width].unsqueeze(1).to_broadcast([P, rows, width])
                    sp.dma_start(table.rearrange("(t p) f -> p t f", p=P), zeros).then_inc(s["zeroed"], 16)
                sp.wait_ge(s["zeroed"], 16 * len(tables))


def norm_steps(nc, T, dve, c, s, src, h, stats, mv, g):
    for t in range(NB):
        ins = nc.vector.bn_stats(stats[:, t, :], src(t))
        ins.then_inc(s["dve_step"], 1)
    c.n += NB
    dve.wait_ge(s["dve_step"], c.it * c.per + c.n)
    dve.sem_inc(T["past"], 1)
    for t in range(NB):
        nc.vector.bn_aggr(mv[:, t, 0:2], stats[:, t, :]).then_inc(s["dve_step"], 1)
    c.n += NB
    dve.wait_ge(s["dve_step"], c.it * c.per + c.n)
    nc.vector.tensor_scalar(mv[:, :, 2], mv[:, :, 1], EPS, None, ALU.add).then_inc(s["var_ready"], 1)


NORM_LINKS = 2 * NB + 1 + NB + 1


def norm_finish(nc, dve, c, s, src, h, mv, roots):
    dve.wait_ge(s["root_ready"], roots)
    c.link(nc.vector.reciprocal(mv[:, :, 4], mv[:, :, 3]))
    for t in range(NB):
        nc.vector.tensor_scalar(h[:, t, :], src(t), mv[:, t, 0:1], mv[:, t, 4:5], ALU.subtract, ALU.mult).then_inc(s["dve_step"], 1)
    c.n += NB
    dve.wait_ge(s["dve_step"], c.it * c.per + c.n)
    c.link(nc.vector.tensor_scalar(h[:, :, :], h[:, :, :], 0.0, None, ALU.max))


def node_pre(nc, T, D, S, L, w_dram, scale_dram, tables, width, skip, attr, eq=None):
    M = w_dram.shape[1]
    skipw = M - width
    names = ["w_loaded", "w_scaled", "dve_step", "var_ready", "root_ready", "h_ready", "tr_ready", "tr_copied",
             "out_ready", "out_copied", "table_ready", "stored", "act_step"]
    with phase(nc, names) as s, ExitStack() as st:
        def sb(n, sh, dt=F32):
            return st.enter_context(nc.sbuf_tensor(f"{L}pre_{n}", sh, dt))
        w1, w2 = sb("w1", [P, M]), sb("w2", [NV, M])
        rs1, rs2 = sb("rs1", [P, 1]), sb("rs2", [NV, 1])
        stats, mv = sb("stats", [P, NB, 6]), sb("mv", [P, NB, 5])
        h = sb("h", [P, NB, FEAT])
        hT = sb("hT", [P, 2, 2 * P])
        tab = sb("tab", [P, NB, width])
        TR = [T["bank"][6], T["bank"][7]]
        OUT = [T["bank"][4], T["bank"][5]]
        loads = 4
        if eq:
            sq = sb("sq", [P, NB, FEAT])
            ev = sb("ev", [P, NB, 8])
            pr = sb("pr", [P, 2 * FEAT])
            bias = sb("bias", [P, width])
            loads = 6
        per = NORM_LINKS + (11 + 2 * NB if eq else 0)
        with nc.Block() as block:
            @block.sync
            def _(sp):
                sp.dma_start(w1[:, :], w_dram[0:P, :]).then_inc(s["w_loaded"], 16)
                sp.dma_start(w2[:, :], w_dram[P:FEAT, :]).then_inc(s["w_loaded"], 16)
                sp.dma_start(rs1[:, :], scale_dram[0:P, :]).then_inc(s["w_loaded"], 16)
                sp.dma_start(rs2[:, :], scale_dram[P:FEAT, :]).then_inc(s["w_loaded"], 16)
                if eq:
                    sp.dma_start(pr[:, :], eq[0].partition_broadcast(P)).then_inc(s["w_loaded"], 16)
                    sp.dma_start(bias[:, :], eq[1].partition_broadcast(P)).then_inc(s["w_loaded"], 16)
                with sp.Fori(0, S.node_groups) as g:
                    sp.wait_ge(s["table_ready"], g + 1)
                    sp.sem_inc(T["past"], 1)
                    for n, table in enumerate(tables):
                        rows = table.rearrange("(t p) f -> p t f", p=P)
                        part = width // len(tables)
                        sp.dma_start(rows[:, bass.ds(g * NB, NB), :], tab[:, :, n * part:(n + 1) * part]).then_inc(s["stored"], 16)
                    sp.wait_ge(s["stored"], 16 * len(tables) * (g + 1))
                    sp.sem_inc(T["past"], 1)

            @block.vector
            def _(dve):
                dve.wait_ge(s["w_loaded"], 16 * loads)
                nc.vector.tensor_scalar(w1[:, :], w1[:, :], rs1[:, 0:1], None, ALU.mult).then_inc(s["w_scaled"], 1)
                nc.vector.tensor_scalar(w2[:, :], w2[:, :], rs2[:, 0:1], None, ALU.mult).then_inc(s["w_scaled"], 1)
                with dve.Fori(0, S.node_groups) as g:
                    c = Chain(dve, s["dve_step"], per, g)
                    x = T["x"][:, bass.ds(g * NB, NB), :]
                    dve.wait_ge(s["tr_ready"], g * NB)
                    norm_steps(nc, T, dve, c, s, lambda t: x[:, t, :], h, stats, mv, g)
                    norm_finish(nc, dve, c, s, lambda t: x[:, t, :], h, mv, (2 if eq else 1) * g + 1)
                    if eq:
                        c.link(nc.vector.tensor_copy(skip[:, bass.ds(g * NB, NB), 0:FEAT], h[:, :, :]))
                        c.link(nc.vector.reduce_sum(ev[:, :, 0], h[:, :, 0:NS], AX.X))
                        c.link(nc.vector.tensor_scalar(ev[:, :, 0], ev[:, :, 0], 1.0 / NS, None, ALU.mult))
                        c.link(nc.vector.tensor_tensor(h[:, :, 0:NS], h[:, :, 0:NS],
                                                       ev[:, :, 0:1].to_broadcast([P, NB, NS]), ALU.subtract))
                        c.link(nc.vector.tensor_tensor(sq[:, :, :], h[:, :, :], h[:, :, :], ALU.mult))
                        c.link(nc.vector.reduce_sum(ev[:, :, 1], sq[:, :, 0:NS], AX.X))
                        c.link(nc.vector.reduce_sum(ev[:, :, 2], sq[:, :, NS:FEAT], AX.X))
                        c.link(nc.vector.tensor_scalar(ev[:, :, 1], ev[:, :, 1], 1.0 / NS, EPS, ALU.mult, ALU.add))
                        nc.vector.tensor_scalar(ev[:, :, 2], ev[:, :, 2], 1.0 / (3 * NV), EPS, ALU.mult, ALU.add).then_inc(s["var_ready"], 1)
                        dve.wait_ge(s["root_ready"], 2 * g + 2)
                        c.link(nc.vector.reciprocal(ev[:, :, 5:7], ev[:, :, 3:5]))
                        for t in range(NB):
                            c.link(nc.vector.tensor_scalar(h[:, t, 0:NS], h[:, t, 0:NS], ev[:, t, 5:6], None, ALU.mult))
                            c.link(nc.vector.tensor_scalar(h[:, t, NS:FEAT], h[:, t, NS:FEAT], ev[:, t, 6:7], None, ALU.mult))
                        c.link(nc.vector.tensor_tensor(h[:, :, :], h[:, :, :], pr[:, 0:FEAT].unsqueeze(1).to_broadcast([P, NB, FEAT]), ALU.mult))
                        c.link(nc.vector.tensor_tensor(h[:, :, :], h[:, :, :], pr[:, FEAT:2 * FEAT].unsqueeze(1).to_broadcast([P, NB, FEAT]), ALU.add))
                    c.end()
                    dve.sem_inc(s["h_ready"], 1)
                    dve.wait_ge(s["stored"], 16 * len(tables) * g)
                    for t in range(NB):
                        dve.wait_ge(s["out_ready"], g * NB + t + 1)
                        o = OUT[t % 2]
                        if eq:
                            nc.vector.tensor_tensor(tab[:, t, :], o[:, 0:width], bias[:, :], ALU.add).then_inc(s["out_copied"], 1)
                        else:
                            at = T["a"][:, bass.ds(g * NB + t, 1)] if attr else 1.0
                            nc.vector.tensor_scalar(tab[:, t, :], o[:, 0:width], at, None, ALU.mult).then_inc(s["act_step"], 1)
                        if skipw:
                            sk = skip[:, bass.ds(g * NB + t, 1), 0:skipw]
                            nc.vector.tensor_scalar(sk, o[:, width:M].unsqueeze(1), at, None, ALU.mult).then_inc(s["out_copied"], 1)
                    dve.wait_ge(s["out_copied"], g * NB + NB)
                    if not eq:
                        dve.wait_ge(s["act_step"], g * NB + NB)
                    dve.sem_inc(s["table_ready"], 1)

            @block.scalar
            def _(act):
                with act.Fori(0, S.node_groups) as g:
                    act.wait_ge(s["var_ready"], (2 if eq else 1) * g + 1)
                    nc.scalar.activation(mv[:, :, 3], mv[:, :, 2], ACT.Sqrt).then_inc(s["root_ready"], 1)
                    if eq:
                        act.wait_ge(s["var_ready"], 2 * g + 2)
                        nc.scalar.activation(ev[:, :, 3:5], ev[:, :, 1:3], ACT.Sqrt).then_inc(s["root_ready"], 1)
                    for t in range(NB):
                        act.wait_ge(s["tr_ready"], g * NB + t + 1)
                        if t >= 2:
                            act.wait_ge(s["out_ready"], g * NB + t - 1)
                        else:
                            act.wait_ge(s["out_ready"], g * NB)
                        nc.scalar.activation(hT[:, t % 2, 0:P], TR[t % 2][:, 0:P], ACT.Copy)
                        nc.scalar.activation(hT[0:NV, t % 2, P:2 * P], TR[t % 2][0:NV, P:2 * P], ACT.Copy).then_inc(s["tr_copied"], 1)

            @block.tensor
            def _(pe):
                pe.wait_ge(s["w_scaled"], 2)
                with pe.Fori(0, S.node_groups) as g:
                    pe.wait_ge(s["h_ready"], g + 1)
                    for t in range(NB):
                        if t >= 2:
                            pe.wait_ge(s["tr_copied"], g * NB + t - 1)
                            pe.wait_ge(s["out_copied"], g * NB + t - 1)
                        else:
                            pe.wait_ge(s["tr_copied"], g * NB)
                            pe.wait_ge(s["out_copied"], g * NB)
                        if not eq:
                            pe.wait_ge(s["act_step"], g * NB + max(t - 1, 0))
                        tr, o = TR[t % 2], OUT[t % 2]
                        nc.tensor.transpose(tr[:, 0:P], h[:, t, 0:P], T["ident"][:, :])
                        nc.tensor.transpose(tr[0:NV, P:2 * P], h[:, t, P:FEAT], T["ident"][:, :]).then_inc(s["tr_ready"], 1)
                        pe.wait_ge(s["tr_copied"], g * NB + t + 1)
                        nc.tensor.matmul(o[:, 0:M], hT[:, t % 2, 0:P], w1[:, :], start=True, stop=False)
                        nc.tensor.matmul(o[:, 0:M], hT[0:NV, t % 2, P:2 * P], w2[:, :], start=False, stop=True).then_inc(s["out_ready"], 1)


def edge_pass(nc, T, D, S, L, meta, sh_dram, keys, attrT, wA_dram, wB_dram, table, agg, hid_func, hid_scale,
              cross, in_order):
    K, H, W = attrT.shape[0], wA_dram.shape[1], wB_dram.shape[1]
    width, msg_w = table.shape[1], agg[0].shape[1]
    names = ["w_loaded", "ones_ready", "in_free0", "in_free1", "in_loaded0", "in_loaded1", "s_ready",
             "hid_ready", "hid_done", "w_ready", "dve_step", "q_ready", "p_ready", "agg_ready", "msg_ready", "idx_ready"]
    with phase(nc, names) as s, ExitStack() as st:
        def sb(n, sh, dt=F32):
            return st.enter_context(nc.sbuf_tensor(f"{L}e_{n}", sh, dt))
        in_free = [s["in_free0"], s["in_free1"]]
        in_loaded = [s["in_loaded0"], s["in_loaded1"]]
        gathered, fetched = T["gathered"], T["gathered_count"]
        added, summed = T["added"], T["added_count"]
        wA, wB = sb("wA", [K, H]), sb("wB", [H, W])
        at = [sb(f"at{b}", [K, GE]) for b in range(2)]
        row = [sb(f"row{b}", [P, GE], I32) for b in range(2)]
        mi = [sb(f"mi{b}", [P, 3 * TG], I32) for b in range(2)]
        sh = [sb(f"sh{b}", [P, TG, 6]) for b in range(2)]
        G = [sb(f"G{b}", [P, TG, width]) for b in range(2)]
        Q = [sb(f"Q{b}", [P, TG, MSG]) for b in range(2)]
        t1, t2 = sb("t1", [P, TG, 3 * NV]), sb("t2", [P, TG, 3 * NV])
        hidT = [sb(f"hidT{b}", [H, GE]) for b in range(2)]
        keyf = sb("keyf", [P, TG])
        rep = sb("rep", [P, TG])
        off = sb("off", [P, TG])
        junk = sb("junk", [P, P])
        idx = [sb(f"idx{b}", [P, TG], I32) for b in range(2)]
        Sk = [sb(f"S{b}", [P, TG, P]) for b in range(2)]
        prod = [sb(f"prod{t}", [P, msg_w]) for t in range(TG)]
        msg = [sb(f"msg{t}", [P, msg_w]) for t in range(TG)]
        HID = [T["bank"][0], T["bank"][1]]
        WPS = [T["bank"][n][:, 0:W] for n in (2, 3, 6, 7)]
        AGG = [T["bank"][4], T["bank"][5]]
        last = S.pairs - 1
        steps = (4 if in_order else 4 + TG) + (5 if cross else 3)

        def tile(g, t):
            return g * TG + t

        with nc.Block() as block:
            @block.sync
            def _(sp):
                def load(i, b):
                    g = i * 2 + b
                    sp.dma_start(at[b][:, :], attrT[:, bass.ds(g * GE, GE)]).then_inc(in_loaded[b], 16)
                    sp.dma_start(mi[b][:, :], meta[bass.ds(g * P, P), :]).then_inc(in_loaded[b], 16)
                    sp.dma_start(sh[b][:, :, :], sh_dram[bass.ds(g * P, P), :].rearrange("p (t k) -> p t k", k=6)).then_inc(in_loaded[b], 16)
                    sp.dma_start(row[b][:, :], keys[:, bass.ds(g * GE, GE)].partition_broadcast(P)).then_inc(in_loaded[b], 16)
                sp.dma_start(wA[:, :], wA_dram).then_inc(s["w_loaded"], 16)
                sp.dma_start(wB[:, :], wB_dram).then_inc(s["w_loaded"], 16)
                load(0, 0)
                load(0, 1)
                with sp.Fori(1, S.pairs) as i:
                    for b in range(2):
                        sp.wait_ge(in_free[b], i)
                        sp.sem_inc(T["past"], 1)
                        load(i, b)

            @block.gpsimd
            def _(pool):
                def gather(i, b):
                    pool.wait_ge(in_loaded[b], 64 * i + 64)
                    pool.sem_inc(T["past"], 1)
                    for t in range(TG):
                        pool.indirect_dma_start(G[b][:, t, :], None, table, bass.IndirectOffsetOnAxis(mi[b][:, t:t + 1], 0)).then_inc(gathered[b], 16)

                def scatter(i, b):
                    g = i * 2 + b
                    pool.wait_ge(s["idx_ready"], g + 1)
                    for t in range(TG):
                        pool.wait_ge(s["msg_ready"], tile(g, t) + 1)
                        pool.wait_ge(added[t], summed + 16 * g)
                        pool.sem_inc(T["past"], 1)
                        pool.indirect_dma_start(agg[t], bass.IndirectOffsetOnAxis(idx[b][:, t:t + 1], 0), msg[t][:, :],
                                                None, compute_op=ALU.add).then_inc(added[t], 16)
                gather(0, 0)
                gather(0, 1)
                with pool.Fori(0, last) as i:
                    for b in range(2):
                        gather(i + 1, b)
                        scatter(i, b)
                scatter(last, 0)
                scatter(last, 1)
                for t in range(TG):
                    pool.wait_ge(added[t], summed + 16 * S.groups)

            @block.vector
            def _(dve):
                if not cross:
                    for t in range(TG):
                        nc.vector.memset(prod[t][:, X0:msg_w], 1.0).then_inc(s["ones_ready"], 1)
                with dve.Fori(0, S.pairs) as i:
                    c = Chain(dve, s["dve_step"], 2 * steps, i)
                    for b in range(2):
                        g = i * 2 + b
                        key = mi[b][:, TG:2 * TG]
                        dve.wait_ge(in_loaded[b], 64 * i + 64)
                        nc.vector.tensor_copy(keyf[:, :], key)
                        if in_order:
                            c.link(nc.vector.tensor_tensor(rep[:, :], key, mi[b][:, 2 * TG:3 * TG], ALU.is_equal))
                        for t in range(TG):
                            r = row[b][:, t * P:(t + 1) * P]
                            if not in_order:
                                if t == 0:
                                    c.link(nc.vector.tensor_copy(off[:, :], T["spare"][:, :]))
                                c.link(nc.vector.scalar_tensor_tensor(junk[:, :], r, keyf[:, t:t + 1], T["lower"][:, :], ALU.is_equal, ALU.mult,
                                                                      accum_out=rep[:, t:t + 1]))
                            nc.vector.tensor_scalar(Sk[b][:, t, :], r, keyf[:, t:t + 1], None, ALU.is_equal).then_inc(s["s_ready"], 1)
                        c.link(nc.vector.tensor_tensor(off[:, :], T["spare"][:, :], keyf[:, :], ALU.subtract))
                        if in_order:
                            c.link(nc.vector.tensor_tensor(off[:, :], rep[:, :], off[:, :], ALU.mult))
                        else:
                            c.link(nc.vector.scalar_tensor_tensor(off[:, :], rep[:, :], 0.5, off[:, :], ALU.is_gt, ALU.mult))
                        for t in range(TG):
                            dve.wait_ge(added[t], summed + 32 * i)
                        c.link(nc.vector.tensor_tensor(idx[b][:, :], off[:, :], keyf[:, :], ALU.add))
                        dve.sem_inc(s["idx_ready"], 1)
                        dve.wait_ge(gathered[b], fetched + 16 * TG * i + 16 * TG)
                        v = G[b][:, :, NS:width]

                        def direction(k):
                            return sh[b][:, :, k:k + 3].unsqueeze(3).to_broadcast([P, TG, 3, NV])

                        def three(x):
                            return x.rearrange("p t (k c) -> p t k c", c=NV)
                        c.link(nc.vector.tensor_tensor(three(t1[:, :, :]), three(v[:, :, 0:96]), direction(1), ALU.mult))
                        if cross:
                            nc.vector.tensor_tensor(three(t2[:, :, :]), three(v[:, :, NV:4 * NV]), direction(3), ALU.mult)
                        c.link(nc.vector.tensor_tensor(t1[:, :, 0:NV], t1[:, :, 0:NV], t1[:, :, NV:2 * NV], ALU.add))
                        c.link(nc.vector.tensor_tensor(Q[b][:, :, D0:B0], t1[:, :, 0:NV], t1[:, :, 2 * NV:3 * NV], ALU.add))
                        if cross:
                            c.link(nc.vector.tensor_tensor(three(t1[:, :, :]), three(v[:, :, 2 * NV:5 * NV]), direction(2), ALU.mult))
                            c.link(nc.vector.tensor_tensor(Q[b][:, :, X0:MSG], t2[:, :, :], t1[:, :, :], ALU.subtract))
                        dve.wait_ge(s["q_ready"], tile(g, TG))
                        for t in range(TG):
                            dve.wait_ge(s["w_ready"], tile(g, t) + 1)
                            if t == 0:
                                dve.sem_inc(in_free[b], 1)
                            w, q, p = WPS[t], Q[b][:, t, :], prod[t]
                            nc.vector.tensor_tensor(p[:, 0:B0], w[:, 0:B0], q[:, 0:B0], ALU.mult)
                            nc.vector.tensor_tensor(p[:, B0:C0].rearrange("p (k c) -> p k c", c=NS), w[:, B0:B0 + NS].unsqueeze(1).to_broadcast([P, 3, NS]),
                                                    q[:, B0:C0].rearrange("p (k c) -> p k c", c=NS), ALU.mult)
                            m = 2 if cross else 1
                            nc.vector.tensor_tensor(p[:, C0:C0 + 96 * m].rearrange("p (m k c) -> p m k c", k=3, c=NV),
                                                    w[:, B0 + NS:W].rearrange("p (m c) -> p m c", c=NV).unsqueeze(2).to_broadcast([P, m, 3, NV]),
                                                    q[:, C0:C0 + 96 * m].rearrange("p (m k c) -> p m k c", k=3, c=NV), ALU.mult).then_inc(s["p_ready"], 1)
                    c.end()

            @block.scalar
            def _(act):
                def hidden(g, b):
                    act.wait_ge(s["hid_ready"], g + 1)
                    nc.scalar.activation(hidT[b][:, :], HID[b][0:H, :], hid_func, scale=hid_scale).then_inc(s["hid_done"], 1)

                def scaled(i, b, t):
                    g, q, e = G[b][:, t, :], Q[b][:, t, :], sh[b][:, t, :]
                    if t == 0:
                        act.wait_ge(gathered[b], fetched + 16 * TG * i + 16 * TG)
                        act.wait_ge(s["p_ready"], 2 * TG * i)
                    nc.scalar.activation(q[:, A0:D0], g[:, 0:NS], ACT.Copy, scale=e[:, 0:1])
                    for k in range(3):
                        nc.scalar.activation(q[:, B0 + NS * k:B0 + NS * (k + 1)], g[:, 0:NS], ACT.Copy, scale=e[:, k + 1:k + 2])
                    nc.scalar.activation(q[:, C0:X0], g[:, NS:FEAT], ACT.Copy, scale=e[:, 0:1]).then_inc(s["q_ready"], 1)

                def evacuate(g, t):
                    act.wait_ge(s["agg_ready"], tile(g, t) + 1)
                    act.wait_ge(added[t], summed + 16 * g)
                    nc.scalar.activation(msg[t][:, :], AGG[t % 2][:, 0:msg_w], ACT.Copy).then_inc(s["msg_ready"], 1)
                hidden(0, 0)
                for t in range(TG):
                    scaled(0, 0, t)
                with act.Fori(0, last) as i:
                    for b in range(2):
                        hidden(i * 2 + b + 1, 1 - b)
                        for t in range(TG):
                            evacuate(i * 2 + b, t)
                            scaled(i + b, 1 - b, t)
                hidden(2 * last + 1, 1)
                for t in range(TG):
                    evacuate(2 * last, t)
                    scaled(last, 1, t)
                for t in range(TG):
                    evacuate(2 * last + 1, t)

            @block.tensor
            def _(pe):
                def hidden(i, b):
                    pe.wait_ge(in_loaded[b], 64 * i + 64)
                    pe.sem_inc(T["past"], 1)
                    nc.tensor.matmul(HID[b][0:H, :], wA[:, :], at[b][:, :], start=True, stop=True).then_inc(s["hid_ready"], 1)

                def weights(g, b, t):
                    pe.wait_ge(s["hid_done"], g + 1)
                    nc.tensor.matmul(WPS[t], hidT[b][:, t * P:(t + 1) * P], wB[:, :], start=True, stop=True).then_inc(s["w_ready"], 1)

                def sums(g, b, t):
                    pe.wait_ge(s["s_ready"], tile(g, t) + 1)
                    pe.wait_ge(s["p_ready"], tile(g, t) + 1)
                    pe.wait_ge(s["msg_ready"], tile(g, max(t - 1, 0)))
                    nc.tensor.matmul(AGG[t % 2][:, 0:msg_w], Sk[b][:, t, :], prod[t][:, :], start=True, stop=True).then_inc(s["agg_ready"], 1)

                pe.wait_ge(s["w_loaded"], 32)
                if not cross:
                    pe.wait_ge(s["ones_ready"], TG)
                hidden(0, 0)
                for t in range(TG):
                    weights(0, 0, t)
                with pe.Fori(0, last) as i:
                    for b in range(2):
                        hidden(i + b, 1 - b)
                        for t in range(TG):
                            sums(i * 2 + b, b, t)
                            weights(i * 2 + b + 1, 1 - b, t)
                hidden(last, 1)
                for t in range(TG):
                    sums(2 * last, 0, t)
                    weights(2 * last + 1, 1, t)
                for t in range(TG):
                    sums(2 * last + 1, 1, t)
        T["gathered_count"] += 16 * TG * S.pairs
        T["added_count"] += 16 * S.groups


def node_post(nc, T, D, S, L, agg, w_dram, scale_dram, skip, gated, attr):
    M = w_dram.shape[1]
    msg_w = w_dram.shape[0]
    KC = msg_w // 4
    names = ["w_loaded", "w_scaled", "in_free", "in_loaded", "sum_ready", "dve_step", "tr_ready", "tr_copied", "out_ready",
             "out_copied", "pre_ready", "sig_ready"]
    with phase(nc, names) as s, ExitStack() as st:
        def sb(n, sh, dt=F32):
            return st.enter_context(nc.sbuf_tensor(f"{L}post_{n}", sh, dt))
        w = sb("w", [KC, 4, M])
        rs = sb("rs", [KC, 4])
        part = [sb(f"part{q}", [P, NB, msg_w]) for q in range(COPIES)]
        mT = [sb(f"mT{q}", [KC, 4, P]) for q in range(2)]
        o = sb("o", [P, NB, M])
        sg = sb("sg", [P, NB, 96])
        TR = [T["bank"][6], T["bank"][7]]
        OUT = [T["bank"][4], T["bank"][5]]
        per = (6 if attr else 5) if gated else 11
        with nc.Block() as block:
            @block.sync
            def _(sp):
                sp.dma_start(w[:, :, :], w_dram.rearrange("(q k) m -> k q m", k=KC)).then_inc(s["w_loaded"], 16)
                sp.dma_start(rs[:, :], scale_dram.rearrange("(q k) o -> k (q o)", k=KC)).then_inc(s["w_loaded"], 16)
                with sp.Fori(0, S.node_groups) as g:
                    sp.wait_ge(s["in_free"], g)
                    sp.sem_inc(T["past"], 1)
                    for q in range(COPIES):
                        rows = agg[q][0:S.node_rows, :].rearrange("(t p) f -> p t f", p=P)
                        sp.dma_start(part[q][:, :, :], rows[:, bass.ds(g * NB, NB), :]).then_inc(s["in_loaded"], 16)

            @block.vector
            def _(dve):
                dve.wait_ge(s["w_loaded"], 32)
                for q in range(4):
                    nc.vector.tensor_scalar(w[:, q, :], w[:, q, :], rs[:, q:q + 1], None, ALU.mult).then_inc(s["w_scaled"], 1)
                with dve.Fori(0, S.node_groups) as g:
                    c = Chain(dve, s["dve_step"], per, g)
                    dve.wait_ge(s["in_loaded"], 64 * g + 64)
                    c.link(nc.vector.tensor_tensor(part[0][:, :, :], part[0][:, :, :], part[1][:, :, :], ALU.add))
                    c.link(nc.vector.tensor_tensor(part[2][:, :, :], part[2][:, :, :], part[3][:, :, :], ALU.add))
                    c.link(nc.vector.tensor_tensor(part[0][:, :, :], part[0][:, :, :], part[2][:, :, :], ALU.add))
                    if not gated:
                        c.link(nc.vector.tensor_scalar(sg[:, :, 0:1], part[0][:, :, X0:X0 + 1], 1.0, None, ALU.max))
                        c.link(nc.vector.reciprocal(sg[:, :, 1:2], sg[:, :, 0:1]))
                        c.link(nc.vector.tensor_tensor(part[0][:, :, :], part[0][:, :, :], sg[:, :, 1:2].to_broadcast([P, NB, msg_w]), ALU.mult))
                    dve.sem_inc(s["sum_ready"], 1)
                    for t in range(NB):
                        dve.wait_ge(s["out_ready"], g * NB + t + 1)
                        nc.vector.tensor_copy(o[:, t, :], OUT[t % 2][:, 0:M]).then_inc(s["out_copied"], 1)
                    dve.wait_ge(s["out_copied"], g * NB + NB)
                    x = T["x"][:, bass.ds(g * NB, NB), :]
                    if attr:
                        a = T["a"][:, bass.ds(g * NB, NB)].unsqueeze(2).to_broadcast([P, NB, M])
                        c.link(nc.vector.tensor_tensor(o[:, :, :], o[:, :, :], a, ALU.mult))
                    if gated:
                        sk = skip[:, bass.ds(g * NB, NB), :]
                        nc.vector.tensor_tensor(o[:, :, :], o[:, :, :], sk, ALU.add).then_inc(s["pre_ready"], 1)
                        dve.wait_ge(s["sig_ready"], g + 1)
                        c.link(nc.vector.tensor_tensor(o[:, :, 0:NS], o[:, :, 0:NS], sg[:, :, 0:NS], ALU.mult))
                        for t in range(NB):
                            nc.vector.tensor_tensor(o[:, t, 96:192].rearrange("p (c k) -> p c k", k=3), o[:, t, 96:192].rearrange("p (c k) -> p c k", k=3),
                                                    sg[:, t, NS:96].unsqueeze(2).to_broadcast([P, NV, 3]), ALU.mult)
                        c.link(nc.vector.tensor_tensor(x[:, :, 0:NS], x[:, :, 0:NS], o[:, :, 0:NS], ALU.add))
                        nc.vector.tensor_tensor(x[:, :, NS:FEAT], x[:, :, NS:FEAT], o[:, :, 96:192], ALU.add).then_inc(s["in_free"], 1)
                    else:
                        sk = skip[:, bass.ds(g * NB, NB), :]
                        c.link(nc.vector.tensor_copy(sg[:, :, 3:4], o[:, :, FEAT:FEAT + 1]))
                        c.link(nc.vector.tensor_tensor(o[:, :, 0:FEAT], o[:, :, 0:FEAT], sg[:, :, 3:4].to_broadcast([P, NB, FEAT]), ALU.mult))
                        c.link(nc.vector.tensor_tensor(o[:, :, 0:FEAT], o[:, :, 0:FEAT], sk[:, :, 0:FEAT], ALU.add))
                        c.link(nc.vector.tensor_tensor(x, x, o[:, :, 0:FEAT], ALU.add))
                        dve.sem_inc(s["in_free"], 1)
                    c.end()

            @block.scalar
            def _(act):
                with act.Fori(0, S.node_groups) as g:
                    for t in range(NB):
                        act.wait_ge(s["tr_ready"], g * NB + t + 1)
                        if t >= 2:
                            act.wait_ge(s["out_ready"], g * NB + t - 1)
                        else:
                            act.wait_ge(s["out_ready"], g * NB)
                        nc.scalar.activation(mT[t % 2][:, :, :], TR[t % 2][0:KC, :].rearrange("p (q n) -> p q n", n=P), ACT.Copy).then_inc(s["tr_copied"], 1)
                    if gated:
                        act.wait_ge(s["pre_ready"], g + 1)
                        nc.scalar.activation(sg[:, :, :], o[:, :, 0:96], ACT.Sigmoid).then_inc(s["sig_ready"], 1)

            @block.tensor
            def _(pe):
                pe.wait_ge(s["w_scaled"], 4)
                with pe.Fori(0, S.node_groups) as g:
                    pe.wait_ge(s["sum_ready"], g + 1)
                    for t in range(NB):
                        pe.wait_ge(s["tr_copied"], g * NB + max(t - 1, 0))
                        pe.wait_ge(s["out_copied"], g * NB + max(t - 1, 0))
                        tr, ot = TR[t % 2], OUT[t % 2]
                        for q in range(4):
                            ins = nc.tensor.transpose(tr[0:KC, q * P:(q + 1) * P], part[0][:, t, q * KC:(q + 1) * KC], T["ident"][:, :])
                        ins.then_inc(s["tr_ready"], 1)
                        pe.wait_ge(s["tr_copied"], g * NB + t + 1)
                        for q in range(4):
                            ins = nc.tensor.matmul(ot[:, 0:M], mT[t % 2][:, q, :], w[:, q, :], start=(q == 0), stop=(q == 3))
                        ins.then_inc(s["out_ready"], 1)


def inverse_root(nc, c, y, v, t):
    yi = y[:, :].bitcast(I32)
    c.link(nc.vector.tensor_scalar(yi, v[:, :].bitcast(I32), 1, None, ALU.logical_shift_right))
    c.link(nc.vector.tensor_scalar(yi, yi, -1.0, float(0x5F3759DF), ALU.mult, ALU.add))
    for _ in range(3):
        c.link(nc.vector.tensor_tensor(t[:, :], y[:, :], y[:, :], ALU.mult))
        c.link(nc.vector.scalar_tensor_tensor(t[:, :], t[:, :], -0.5, v[:, :], ALU.mult, ALU.mult))
        c.link(nc.vector.scalar_tensor_tensor(y[:, :], t[:, :], 1.5, y[:, :], ALU.add, ALU.mult))


R_ = 2 * NS + NV + 3 * NV + 3 * NV
WIDE = NS + 5 * NV
HEADS, HD = 8, 8
MSG2 = FEAT + HEADS
BIG = 1.6e38


def message_phase(nc, T, D, S, table_s, table_d, direction5, values, scores):
    H = 64
    names = ["w_loaded", "centred", "in_free0", "in_free1", "in_loaded0", "in_loaded1", "h_ready", "square_ready",
             "norm_ready", "tr_ready", "hid_done", "w_ready", "dve_step", "r_ready", "rt_ready", "rt_copied", "u_ready",
             "u_copied", "v_ready", "stored0", "stored1", "ones_ready", "turned_loaded0", "turned_loaded1"]
    with phase(nc, names) as s, ExitStack() as st:
        def sb(n, sh, dt=F32):
            return st.enter_context(nc.sbuf_tensor(f"msg_{n}", sh, dt))
        in_free = [s["in_free0"], s["in_free1"]]
        in_loaded = [s["in_loaded0"], s["in_loaded1"]]
        turned_loaded = [s["turned_loaded0"], s["turned_loaded1"]]
        gathered, fetched = T["gathered"], T["gathered_count"]
        stored = [s["stored0"], s["stored1"]]
        w1, w2, w3 = sb("w1", [H + 1, H]), sb("w2", [H + 1, H]), sb("w3", [H + 1, 224])
        wm = sb("wm", [H + 1, 2])
        gb = sb("gb", [H, 4])
        wl = sb("wl", [P, 3, 256])
        ls = sb("ls", [P, 3])
        dots = sb("dots", [P, H])
        at = [sb(f"at{b}", [H + 1, GE]) for b in range(2)]
        mi = [sb(f"mi{b}", [P, 3 * TG], I32) for b in range(2)]
        y5 = [sb(f"y5{b}", [P, TG, 5]) for b in range(2)]
        turned = [sb(f"turned{b}", [P, TG, 5]) for b in range(2)]
        Gs = [sb(f"Gs{b}", [P, TG, WIDE]) for b in range(2)]
        Gd = [sb(f"Gd{b}", [P, TG, WIDE]) for b in range(2)]
        m = [sb(f"m{b}", [P, TG, WIDE]) for b in range(2)]
        dc = [sb(f"dc{b}", [P, TG, 4 * NV]) for b in range(2)]
        xn = sb("xn", [P, TG, H])
        sq = sb("sq", [P, TG, H])
        rstd, rad, tmp = sb("rstd", [P, TG]), sb("rad", [P, TG]), sb("tmp", [P, TG])
        hT = [sb(f"hT{q}", [H + 1, GE]) for q in range(2)]
        t1, t2, t3 = sb("t1", [P, TG, 3 * NV]), sb("t2", [P, TG, 3 * NV]), sb("t3", [P, TG, 3 * NV])
        R = [sb(f"R{q}", [P, R_]) for q in range(2)]
        RT = [sb(f"RT{q}", [P, 3 * P]) for q in range(2)]
        th = [sb(f"th{b}", [P, TG, H]) for b in range(2)]
        U = [sb(f"U{b}", [P, TG, 256]) for b in range(2)]
        sm = sb("sm", [P, TG, H])
        HB, TB = T["bank"][0], T["bank"][1]
        WB = [T["bank"][2], T["bank"][3]]
        RB = [T["bank"][4], T["bank"][5]]
        UB = [T["bank"][6], T["bank"][7]]
        loads = 10
        parts = [(P, 0, 256), (P, 32, 256), (R_ - 2 * P + 1, 32, 256)]
        first = 2 * 13 + 7
        per = 2 * (2 * 13 + 7 + TG + 5)
        last = S.pairs - 1

        def tile(i, b, t):
            return (i * 2 + b) * TG + t

        def periods(step, engine):
            step(0, 0, 0, 1, None)
            with engine.Fori(0, last) as k:
                step(k, 1, k + 1, 0, k)
                step(k + 1, 0, k + 1, 1, k)
            step(last, 1, None, None, last)

        with nc.Block() as block:
            @block.sync
            def _(sp):
                def load(i, b):
                    g = i * 2 + b
                    sp.dma_start(at[b][:, :], D["attr64"][:, bass.ds(g * GE, GE)]).then_inc(in_loaded[b], 16)
                    sp.dma_start(mi[b][:, :], D["by_dst"][bass.ds(g * P, P), :]).then_inc(in_loaded[b], 16)
                    sp.dma_start(y5[b][:, :, :], direction5[bass.ds(g * P, P), :].rearrange("p (t k) -> p t k", k=5)).then_inc(in_loaded[b], 16)
                for dst, src in ((w1, D["L2_rw1"]), (w2, D["L2_rw2"]), (w3, D["L2_rw3"]), (gb, D["L2_gb"]), (ls, D["L2_lin_scale"])):
                    sp.dma_start(dst[:, :], src).then_inc(s["w_loaded"], 16)
                for q in range(3):
                    k = parts[q][0]
                    sp.dma_start(wl[0:k, q, :], D["L2_lin"][q * P:q * P + k, :]).then_inc(s["w_loaded"], 16)
                sp.dma_start(dots[:, :], D["L2_dots"].partition_broadcast(P)).then_inc(s["w_loaded"], 16)
                sp.dma_start(t1[:, 0, 0:1], D["node_vec1"][0:P, :]).then_inc(s["w_loaded"], 16)
                load(0, 0)
                load(0, 1)
                with sp.Fori(1, S.pairs) as i:
                    for b in range(2):
                        sp.wait_ge(in_free[b], i)
                        sp.sem_inc(T["past"], 1)
                        load(i, b)

            @block.gpsimd
            def _(pool):
                with pool.Fori(0, S.pairs) as i:
                    for b in range(2):
                        pool.wait_ge(in_loaded[b], 48 * i + 48)
                        pool.sem_inc(T["past"], 1)
                        for t in range(TG):
                            pool.indirect_dma_start(Gs[b][:, t, :], None, table_s, bass.IndirectOffsetOnAxis(mi[b][:, t:t + 1], 0)).then_inc(gathered[b], 16)
                            pool.indirect_dma_start(Gd[b][:, t, :], None, table_d, bass.IndirectOffsetOnAxis(mi[b][:, TG + t:TG + t + 1], 0)).then_inc(gathered[b], 16)

            @block.vector
            def _(dve):
                dve.wait_ge(s["w_loaded"], 16 * loads)
                for n, w in enumerate((w1, w2)):
                    nc.vector.reduce_sum(wm[:, n:n + 1], w[:, :], AX.X).then_inc(s["centred"], 1)
                dve.wait_ge(s["centred"], 2)
                nc.vector.tensor_scalar(wm[:, :], wm[:, :], 1.0 / H, None, ALU.mult).then_inc(s["centred"], 1)
                dve.wait_ge(s["centred"], 3)
                for n, w in enumerate((w1, w2)):
                    nc.vector.tensor_scalar(w[:, :], w[:, :], wm[:, n:n + 1], None, ALU.subtract).then_inc(s["centred"], 1)
                for q in range(3):
                    k = parts[q][0]
                    nc.vector.tensor_scalar(wl[0:k, q, :], wl[0:k, q, :], ls[0:k, q:q + 1], None, ALU.mult).then_inc(s["centred"], 1)
                for q in range(2):
                    nc.vector.memset(hT[q][H:H + 1, :], 1.0).then_inc(s["ones_ready"], 1)
                    nc.vector.memset(RT[q][96:97, 2 * P:3 * P], 1.0).then_inc(s["ones_ready"], 1)

                def three(x):
                    return x.rearrange("p t (k c) -> p t k c", c=NV)

                def norm(c, i, b, n):
                    g = i * 2 + b
                    dve.wait_ge(s["square_ready"], 2 * g + n + 1)
                    c.link(nc.vector.reduce_sum(rstd[:, :], sq[:, :, :], AX.X))
                    c.link(nc.vector.tensor_scalar(rad[:, :], rstd[:, :], 1.0 / H, EPS, ALU.mult, ALU.add))
                    inverse_root(nc, c, rstd, rad, tmp)
                    nc.vector.tensor_tensor(xn[:, :, :], HB[:, 0:TG * H].rearrange("p (t h) -> p t h", h=H),
                                            rstd[:, :].unsqueeze(2).to_broadcast([P, TG, H]), ALU.mult).then_inc(s["norm_ready"], 1)

                def geometry(c, i, b):
                    def yb(k):
                        return y5[b][:, :, k:k + 3].unsqueeze(3).to_broadcast([P, TG, 3, NV])
                    dve.wait_ge(in_loaded[b], 48 * i + 48)
                    dve.wait_ge(gathered[b], fetched + 32 * TG * i + 32 * TG)
                    c.link(nc.vector.tensor_tensor(m[b][:, :, :], Gs[b][:, :, :], Gd[b][:, :, :], ALU.add))
                    v = m[b][:, :, NS:WIDE]
                    c.link(nc.vector.tensor_tensor(three(t1[:, :, :]), three(v[:, :, 0:96]), yb(0), ALU.mult))
                    c.link(nc.vector.tensor_tensor(t3[:, :, 0:NV], t1[:, :, 0:NV], t1[:, :, NV:2 * NV], ALU.add))
                    c.link(nc.vector.tensor_tensor(dc[b][:, :, 0:NV], t3[:, :, 0:NV], t1[:, :, 2 * NV:3 * NV], ALU.add))
                    c.link(nc.vector.tensor_tensor(three(t1[:, :, :]), three(v[:, :, NV:4 * NV]), yb(2), ALU.mult))
                    c.link(nc.vector.tensor_tensor(three(t2[:, :, :]), three(v[:, :, 2 * NV:5 * NV]), yb(1), ALU.mult))
                    c.link(nc.vector.tensor_tensor(dc[b][:, :, NV:4 * NV], t1[:, :, :], t2[:, :, :], ALU.subtract))
                    dve.sem_inc(in_free[b], 1)

                def product(c, i, b, t):
                    q = t % 2
                    dve.wait_ge(s["w_ready"], tile(i, b, t) + 1)
                    dve.wait_ge(s["rt_ready"], tile(i, b, max(t - 1, 0)))
                    w = WB[q]
                    nc.vector.tensor_tensor(R[q][:, 0:2 * NS].rearrange("p (m c) -> p m c", c=NS), w[:, 0:2 * NS].rearrange("p (m c) -> p m c", c=NS),
                                            m[b][:, t, 0:NS].unsqueeze(1).to_broadcast([P, 2, NS]), ALU.mult)
                    nc.vector.tensor_tensor(R[q][:, 128:160], w[:, 128:160], dc[b][:, t, 0:NV], ALU.mult)
                    nc.vector.tensor_tensor(R[q][:, 160:256].rearrange("p (k c) -> p k c", c=NV), w[:, 160:192].unsqueeze(1).to_broadcast([P, 3, NV]),
                                            dc[b][:, t, NV:4 * NV].rearrange("p (k c) -> p k c", c=NV), ALU.mult)
                    c.link(nc.vector.tensor_tensor(R[q][:, 256:352].rearrange("p (k c) -> p k c", c=NV), w[:, 192:224].unsqueeze(1).to_broadcast([P, 3, NV]),
                                                   m[b][:, t, NS:FEAT].rearrange("p (k c) -> p k c", c=NV), ALU.mult))
                    dve.sem_inc(s["r_ready"], 1)

                def finish(c, i, b):
                    dve.wait_ge(s["u_copied"], tile(i, b, TG))
                    dve.wait_ge(turned_loaded[b], 16 * i + 16)
                    c.link(nc.vector.tensor_scalar(th[b][:, :, :], th[b][:, :, :], 0.4, 0.6, ALU.mult, ALU.add))
                    c.link(nc.vector.tensor_tensor(th[b][:, :, :], th[b][:, :, :], dots[:, :].unsqueeze(1).to_broadcast([P, TG, H]), ALU.mult))
                    c.link(nc.vector.tensor_tensor(sm[:, :, :], th[b][:, :, :], U[b][:, :, 32:96], ALU.mult))
                    c.link(nc.vector.reduce_sum(scores[:, :, bass.ds((i * 2 + b) * TG, TG)].rearrange("p h t -> p t h"),
                                                sm[:, :, :].rearrange("p t (h k) -> p t h k", k=HD), AX.X))
                    c.link(nc.vector.tensor_tensor(three(t3[:, :, :]), U[b][:, :, 0:NV].unsqueeze(2).to_broadcast([P, TG, 3, NV]),
                                                   turned[b][:, :, 0:3].unsqueeze(3).to_broadcast([P, TG, 3, NV]), ALU.mult))
                    nc.vector.tensor_tensor(U[b][:, :, 160:256], U[b][:, :, 160:256], t3[:, :, :], ALU.add).then_inc(s["v_ready"], 1)

                def step(i, b, ni, nb, k):
                    c = chain[0]
                    product(c, i, b, 0)
                    if nb is not None:
                        norm(c, ni, nb, 0)
                    product(c, i, b, 1)
                    if nb is not None:
                        geometry(c, ni, nb)
                    product(c, i, b, 2)
                    if nb is not None:
                        norm(c, ni, nb, 1)
                    product(c, i, b, 3)
                    finish(c, i, b)
                head = Chain(dve, s["dve_step"])
                norm(head, 0, 0, 0)
                geometry(head, 0, 0)
                norm(head, 0, 0, 1)
                chain = [head]
                step(0, 0, 0, 1, None)
                start = head.n
                assert start == first + per // 2
                with dve.Fori(0, last) as k:
                    c = Chain(dve, s["dve_step"], per, k)
                    c.n = start
                    chain = [c]
                    step(k, 1, k + 1, 0, k)
                    step(k + 1, 0, k + 1, 1, k)
                    assert c.n == start + per
                c = Chain(dve, s["dve_step"], per, last)
                c.n = start
                chain = [c]
                step(last, 1, None, None, last)

            @block.scalar
            def _(act):
                def turn(i, b):
                    act.dma_start(turned[b][:, :, :], direction5[bass.ds((i * 2 + b) * P, P), :].rearrange("p (t k) -> p t k", k=5)).then_inc(turned_loaded[b], 16)

                def square(i, b, n):
                    g = i * 2 + b
                    act.wait_ge(s["h_ready"], 2 * g + n + 1)
                    if n:
                        act.wait_ge(s["norm_ready"], 2 * g + n)
                    nc.scalar.activation(sq[:, :, :], HB[:, 0:TG * H].rearrange("p (t h) -> p t h", h=H), ACT.Square).then_inc(s["square_ready"], 1)

                def hidden(i, b, n):
                    act.wait_ge(s["tr_ready"], 2 * (i * 2 + b) + n + 1)
                    nc.scalar.activation(hT[n][0:H, :], TB[0:H, :], ACT.Silu, scale=gb[:, 2 * n:2 * n + 1], bias=gb[:, 2 * n + 1:2 * n + 2]).then_inc(s["hid_done"], 1)

                def copies(i, b, t):
                    q = t % 2
                    act.wait_ge(s["rt_ready"], tile(i, b, t) + 1)
                    act.wait_ge(s["u_ready"], tile(i, b, max(t - 1, 0)))
                    nc.scalar.activation(RT[q][:, 0:2 * P], RB[q][:, 0:2 * P], ACT.Copy)
                    nc.scalar.activation(RT[q][0:96, 2 * P:3 * P], RB[q][0:96, 2 * P:3 * P], ACT.Copy).then_inc(s["rt_copied"], 1)
                    act.wait_ge(s["u_ready"], tile(i, b, t) + 1)
                    if t == 0:
                        act.wait_ge(stored[b], 16 * i)
                    nc.scalar.activation(th[b][:, t, :], UB[q][:, 32:96], ACT.Tanh, scale=0.5)
                    nc.scalar.activation(U[b][:, t, :], UB[q][:, 0:256], ACT.Copy).then_inc(s["u_copied"], 1)

                def store(i, b):
                    g = i * 2 + b
                    act.wait_ge(s["v_ready"], g + 1)
                    act.dma_start(values[bass.ds(g * P, P), :].rearrange("p (t f) -> p t f", f=FEAT), U[b][:, :, 96:256]).then_inc(stored[b], 16)

                def step(i, b, ni, nb, k):
                    if nb is not None:
                        square(ni, nb, 0)
                    copies(i, b, 0)
                    if nb is not None:
                        hidden(ni, nb, 0)
                    if k is not None:
                        pi, pb = (k, 0) if b else (k, 1)
                        store(pi, pb)
                        if nb is not None:
                            turn(ni, nb)
                    copies(i, b, 1)
                    if nb is not None:
                        square(ni, nb, 1)
                    copies(i, b, 2)
                    if nb is not None:
                        hidden(ni, nb, 1)
                    copies(i, b, 3)
                act.wait_ge(s["w_loaded"], 16 * loads)
                act.wait_ge(s["ones_ready"], 4)
                turn(0, 0)
                turn(0, 1)
                for n in range(2):
                    square(0, 0, n)
                    hidden(0, 0, n)
                periods(step, act)
                store(last, 1)
                for b in range(2):
                    act.wait_ge(stored[b], 16 * S.pairs)

            @block.tensor
            def _(pe):
                def layer(i, b, n):
                    g = i * 2 + b
                    w = (w1, w2)[n]
                    if n == 0:
                        pe.wait_ge(in_loaded[b], 48 * i + 48)
                    else:
                        pe.wait_ge(s["hid_done"], 2 * g + 1)
                    pe.wait_ge(s["norm_ready"], 2 * g + n)
                    for t in range(TG):
                        x = at[b] if n == 0 else hT[0]
                        ins = nc.tensor.matmul(HB[:, t * H:(t + 1) * H], x[:, t * P:(t + 1) * P], w[:, :], start=(t == 0), stop=(t == TG - 1))
                    ins.then_inc(s["h_ready"], 1)

                def turn(i, b, n):
                    g = i * 2 + b
                    pe.wait_ge(s["norm_ready"], 2 * g + n + 1)
                    pe.wait_ge(s["hid_done"], 2 * g + n)
                    pe.sem_inc(T["past"], 1)
                    for t in range(TG):
                        ins = nc.tensor.transpose(TB[0:H, t * P:(t + 1) * P], xn[:, t, :], T["ident"][:, :])
                    ins.then_inc(s["tr_ready"], 1)

                def weights(i, b, t):
                    if t == 0:
                        pe.wait_ge(s["hid_done"], 2 * (i * 2 + b) + 2)
                    pe.wait_ge(s["r_ready"], tile(i, b, max(t - 1, 0)))
                    nc.tensor.matmul(WB[t % 2][:, 0:224], hT[1][:, t * P:(t + 1) * P], w3[:, :], start=True, stop=True).then_inc(s["w_ready"], 1)

                def linear(i, b, t):
                    q = t % 2
                    pe.wait_ge(s["r_ready"], tile(i, b, t) + 1)
                    pe.wait_ge(s["rt_copied"], tile(i, b, max(t - 1, 0)))
                    for k in range(3):
                        n = min(P, R_ - k * P)
                        ins = nc.tensor.transpose(RB[q][0:n, k * P:(k + 1) * P], R[q][:, k * P:k * P + n], T["ident"][:, :])
                    ins.then_inc(s["rt_ready"], 1)
                    if t + 2 < TG:
                        weights(i, b, t + 2)
                    pe.wait_ge(s["rt_copied"], tile(i, b, t) + 1)
                    pe.wait_ge(s["u_copied"], tile(i, b, max(t - 1, 0)))
                    for k, (n, lo, hi) in enumerate(parts):
                        ins = nc.tensor.matmul(UB[q][:, lo:hi], RT[q][0:n, k * P:(k + 1) * P], wl[0:n, k, lo:hi], start=(k == 0), stop=(k == 2))
                    ins.then_inc(s["u_ready"], 1)

                def step(i, b, ni, nb, k):
                    weights(i, b, 0)
                    weights(i, b, 1)
                    if nb is not None:
                        layer(ni, nb, 0)
                    linear(i, b, 0)
                    if nb is not None:
                        turn(ni, nb, 0)
                    linear(i, b, 1)
                    if nb is not None:
                        layer(ni, nb, 1)
                    linear(i, b, 2)
                    if nb is not None:
                        turn(ni, nb, 1)
                    linear(i, b, 3)
                pe.wait_ge(s["w_loaded"], 16 * loads)
                pe.wait_ge(s["centred"], 8)
                pe.wait_ge(s["ones_ready"], 4)
                for n in range(2):
                    layer(0, 0, n)
                    turn(0, 0, n)
                periods(step, pe)
        T["gathered_count"] += 32 * TG * S.pairs


def softmax_phase(nc, T, D, S, scores, by_head, corner, carry_d):
    chunks = P // HEADS
    n = S.edge_rows // chunks
    blk = S.pairs
    assert blk <= P and blk * 8 == S.tiles and n * chunks == S.edge_rows
    names = ["tr_ready", "tr_copied", "out0", "out1", "loaded", "dve_step", "exp_ready", "stored", "in0", "in1", "back_ready", "back_copied"]
    with phase(nc, names) as s, ExitStack() as st:
        def sb(nm, sh, dt=F32):
            return st.enter_context(nc.sbuf_tensor(f"soft_{nm}", sh, dt))
        keys = sb("keys", [P, n + 2], I32)
        a, pen, f = sb("a", [P, n]), sb("pen", [P, n]), sb("f", [P, n])
        em = sb("em", [P, 4])
        eh = sb("eh", [HEADS, chunks, 2])
        ch = sb("ch", [HEADS, chunks + 2])
        ini = sb("ini", [P, 1])
        back = [sb(f"back{q}", [P, 8, P]) for q in range(2)]
        BK = T["bank"]
        with nc.Block() as block:
            @block.sync
            def _(sp):
                for h in range(HEADS):
                    src = bass.AP(D["dst_wide"].tensor, 0, [[n, chunks], [1, n + 2]])
                    sp.dma_start(keys[h * chunks:(h + 1) * chunks, :], src).then_inc(s["loaded"], 16)
                for h in range(HEADS):
                    sp.wait_ge(s["tr_copied"], 2 * h + 2)
                    dst = by_head[h:h + 1, :].rearrange("o (k r e) -> (o r) k e", r=blk, e=P)
                    sp.dma_start(dst, back[h % 2][0:blk, :, :]).then_inc(s[f"out{h % 2}"], 16)
                sp.wait_ge(s["out0"], 16 * 4)
                sp.wait_ge(s["out1"], 16 * 4)
                sp.dma_start(a[:, :], by_head.rearrange("h (c n) -> (h c) n", n=n)).then_inc(s["loaded"], 16)
                for d in range(2):
                    sp.wait_ge(s["dve_step"], 5 + 9 * d)
                    sp.dma_start(corner, em[:, 2 * d:2 * d + 2]).then_inc(s["stored"], 16)
                    sp.wait_ge(s["stored"], 16 + 32 * d)
                    sp.dma_start(eh[:, :, :], corner.rearrange("(h c) k -> h c k", h=HEADS)).then_inc(s["loaded"], 16)
                    sp.wait_ge(s["dve_step"], 7 + 9 * d)
                    o = 0 if d == 0 else 2
                    sp.dma_start(carry_d, ch[:, o:o + chunks]).then_inc(s["stored"], 16)
                    sp.wait_ge(s["stored"], 32 + 32 * d)
                    sp.dma_start(ini[:, :], carry_d.rearrange("h (c o) -> (h c) o", o=1)).then_inc(s["loaded"], 16)
                sp.wait_ge(s["exp_ready"], 1)
                sp.dma_start(by_head.rearrange("h (c n) -> (h c) n", n=n), a[:, :]).then_inc(s["stored"], 16)
                sp.wait_ge(s["stored"], 80)
                for h in range(HEADS):
                    if h >= 2:
                        sp.wait_ge(s["back_ready"], h - 1)
                    src = by_head[h:h + 1, :].rearrange("o (k r e) -> (o r) k e", r=blk, e=P)
                    sp.dma_start(back[h % 2][0:blk, :, :], src).then_inc(s[f"in{h % 2}"], 16)

            @block.tensor
            def _(pe):
                for h in range(HEADS):
                    for half in range(2):
                        m = 2 * h + half
                        if m >= 2:
                            pe.wait_ge(s["tr_copied"], m - 1)
                        for k in range(4):
                            kk = 4 * half + k
                            ins = nc.tensor.transpose(BK[m % 2][0:blk, k * P:(k + 1) * P], scores[:, h, kk * blk:(kk + 1) * blk], T["ident"][:, :])
                        ins.then_inc(s["tr_ready"], 1)
                for h in range(HEADS):
                    pe.wait_ge(s[f"in{h % 2}"], 16 * (h // 2 + 1))
                    for half in range(2):
                        m = 2 * h + half
                        if m >= 2:
                            pe.wait_ge(s["back_copied"], m - 1)
                        for k in range(4):
                            kk = 4 * half + k
                            ins = nc.tensor.transpose(BK[2 + m % 2][:, k * P:k * P + blk], back[h % 2][0:blk, kk, :], T["ident"][0:blk, 0:blk])
                        if half == 0:
                            ins.then_inc(s["tr_ready"], 1)
                        else:
                            ins.then_inc(s["back_ready"], 1)

            @block.vector
            def _(dve):
                c = Chain(dve, s["dve_step"])
                dve.wait_ge(s["loaded"], 16 * HEADS + 16)
                c.link(nc.vector.tensor_tensor(pen[:, :], keys[:, 1:n + 1], keys[:, 0:n], ALU.is_equal))
                c.link(nc.vector.tensor_scalar(pen[:, :], pen[:, :], 1.0, BIG, ALU.subtract, ALU.mult))
                c.link(nc.vector.tensor_reduce(em[:, 0:1], pen[:, :], AX.X, ALU.min))
                c.link(nc.vector.tensor_tensor_scan(f[:, :], pen[:, :], a[:, :], -BIG, ALU.add, ALU.max))
                c.link(nc.vector.tensor_copy(em[:, 1:2], f[:, n - 1:n]))
                dve.wait_ge(s["loaded"], 16 * HEADS + 32)
                c.link(nc.vector.memset(ch[:, :], -BIG))
                c.link(nc.vector.tensor_tensor_scan(ch[:, 1:chunks + 1], eh[:, :, 0], eh[:, :, 1], -BIG, ALU.add, ALU.max))
                dve.wait_ge(s["loaded"], 16 * HEADS + 48)
                c.link(nc.vector.tensor_tensor_scan(f[:, :], pen[:, :], a[:, :], ini[:, 0:1], ALU.add, ALU.max))
                c.link(nc.vector.tensor_tensor(pen[:, :], keys[:, 1:n + 1], keys[:, 2:n + 2], ALU.is_equal))
                c.link(nc.vector.tensor_scalar(pen[:, :], pen[:, :], 1.0, BIG, ALU.subtract, ALU.mult))
                c.link(nc.vector.tensor_reduce(em[:, 2:3], pen[:, :], AX.X, ALU.min))
                m = keys[:, 0:n].bitcast(F32)
                c.link(nc.vector.tensor_tensor_scan(m[:, ::-1], pen[:, ::-1], f[:, ::-1], -BIG, ALU.add, ALU.max))
                c.link(nc.vector.tensor_copy(em[:, 3:4], m[:, 0:1]))
                c.link(nc.vector.memset(ch[:, :], -BIG))
                dve.wait_ge(s["loaded"], 16 * HEADS + 64)
                c.link(nc.vector.tensor_tensor_scan(ch[:, chunks:0:-1], eh[:, ::-1, 0], eh[:, ::-1, 1], -BIG, ALU.add, ALU.max))
                c.link(nc.vector.tensor_copy(em[:, 0:1], em[:, 1:2]))
                dve.wait_ge(s["loaded"], 16 * HEADS + 80)
                c.link(nc.vector.tensor_tensor_scan(m[:, ::-1], pen[:, ::-1], f[:, ::-1], ini[:, 0:1], ALU.add, ALU.max))
                c.link(nc.vector.tensor_tensor(a[:, :], a[:, :], m[:, :], ALU.subtract))

            @block.scalar
            def _(act):
                for m in range(2 * HEADS):
                    h, half = m // 2, m % 2
                    act.wait_ge(s["tr_ready"], m + 1)
                    if half == 0 and h >= 2:
                        act.wait_ge(s[f"out{h % 2}"], 16 * (h // 2))
                    nc.scalar.activation(back[h % 2][0:blk, 4 * half:4 * half + 4, :], BK[m % 2][0:blk, :].rearrange("p (k e) -> p k e", e=P), ACT.Copy).then_inc(s["tr_copied"], 1)
                act.wait_ge(s["dve_step"], 18)
                nc.scalar.activation(a[:, :], a[:, :], ACT.Exp).then_inc(s["exp_ready"], 1)
                for m in range(2 * HEADS):
                    h, half = m // 2, m % 2
                    if half == 0:
                        act.wait_ge(s["tr_ready"], 2 * HEADS + h + 1)
                    else:
                        act.wait_ge(s["back_ready"], h + 1)
                    nc.scalar.activation(scores[:, h, 4 * half * blk:(4 * half + 4) * blk].rearrange("p (k r) -> p k r", r=blk),
                                         BK[2 + m % 2][:, :].rearrange("p (k e) -> p k e", e=P)[:, :, 0:blk], ACT.Copy).then_inc(s["back_copied"], 1)
                act.wait_ge(s["back_copied"], 2 * HEADS)


def attend_phase(nc, T, D, S, values, scores, agg):
    names = ["in_free0", "in_free1", "in_loaded0", "in_loaded1", "dve_step", "p_ready", "agg_ready", "msg_ready", "idx_ready"]
    with phase(nc, names) as s, ExitStack() as st:
        def sb(n, sh, dt=F32):
            return st.enter_context(nc.sbuf_tensor(f"att_{n}", sh, dt))
        in_free = [s["in_free0"], s["in_free1"]]
        in_loaded = [s["in_loaded0"], s["in_loaded1"]]
        added, summed = T["added"], T["added_count"]
        row = [sb(f"row{b}", [P, GE], I32) for b in range(2)]
        mi = [sb(f"mi{b}", [P, 3 * TG], I32) for b in range(2)]
        V = [sb(f"V{b}", [P, TG, FEAT]) for b in range(2)]
        keyf = [sb(f"keyf{b}", [P, TG]) for b in range(2)]
        cnt = [sb(f"cnt{b}", [P, 2, TG]) for b in range(2)]
        idx = [[sb(f"idx{b}{t}", [P, 1], I32) for t in range(TG)] for b in range(2)]
        Sk = [sb(f"S{b}", [P, TG, P]) for b in range(2)]
        junk = sb("junk", [P, P])
        prod = [sb(f"prod{b}", [P, TG, MSG2]) for b in range(2)]
        msg = [sb(f"msg{t}", [P, MSG2]) for t in range(TG)]
        AGG = [T["bank"][4], T["bank"][5]]
        steps = 2 + 2 * TG
        last = S.pairs - 1
        with nc.Block() as block:
            @block.sync
            def _(sp):
                with sp.Fori(0, S.pairs) as i:
                    for b in range(2):
                        g = i * 2 + b
                        sp.wait_ge(in_free[b], i)
                        sp.sem_inc(T["past"], 1)
                        sp.dma_start(V[b][:, :, :], values[bass.ds(g * P, P), :].rearrange("p (t f) -> p t f", f=FEAT)).then_inc(in_loaded[b], 16)
                        sp.dma_start(mi[b][:, :], D["by_dst"][bass.ds(g * P, P), :]).then_inc(in_loaded[b], 16)
                        sp.dma_start(row[b][:, :], D["dst_row"][:, bass.ds(g * GE, GE)].partition_broadcast(P)).then_inc(in_loaded[b], 16)

            @block.gpsimd
            def _(pool):
                with pool.Fori(0, S.pairs) as i:
                    for b in range(2):
                        g = i * 2 + b
                        pool.wait_ge(s["idx_ready"], g + 1)
                        for t in range(TG):
                            pool.wait_ge(s["msg_ready"], g * TG + t + 1)
                            pool.wait_ge(added[t], summed + 16 * g)
                            pool.sem_inc(T["past"], 1)
                            pool.indirect_dma_start(agg[t], bass.IndirectOffsetOnAxis(idx[b][t][:, 0:1], 0), msg[t][:, :], None,
                                                    compute_op=ALU.add).then_inc(added[t], 16)
                for t in range(TG):
                    pool.wait_ge(added[t], summed + 16 * S.groups)

            @block.vector
            def _(dve):
                with dve.Fori(0, S.pairs) as i:
                    c = Chain(dve, s["dve_step"], 2 * steps, i)
                    for b in range(2):
                        g = i * 2 + b
                        dve.wait_ge(in_loaded[b], 48 * i + 48)
                        dve.wait_ge(s["agg_ready"], 2 * TG * i)
                        c.link(nc.vector.tensor_copy(keyf[b][:, :], mi[b][:, TG:2 * TG]))
                        e = scores[:, :, bass.ds(g * TG, TG)]
                        nc.vector.tensor_copy(prod[b][:, :, FEAT:MSG2], e.rearrange("p h t -> p t h"))
                        nc.vector.tensor_tensor(prod[b][:, :, 0:NS].rearrange("p t (h k) -> p t h k", k=HD), V[b][:, :, 0:NS].rearrange("p t (h k) -> p t h k", k=HD),
                                                e.rearrange("p h t -> p t h").unsqueeze(3).to_broadcast([P, TG, HEADS, HD]), ALU.mult)
                        for t in range(TG):
                            r = row[b][:, t * P:(t + 1) * P]
                            et = scores[:, :, bass.ds(g * TG + t, 1)].rearrange("p h o -> p (h o)")
                            nc.vector.tensor_tensor(prod[b][:, t, NS:FEAT].rearrange("p (k h j) -> p k h j", k=3, j=NV // HEADS),
                                                    V[b][:, t, NS:FEAT].rearrange("p (k h j) -> p k h j", k=3, j=NV // HEADS),
                                                    et.unsqueeze(1).unsqueeze(3).to_broadcast([P, 3, HEADS, NV // HEADS]), ALU.mult)
                            nc.vector.tensor_scalar(Sk[b][:, t, :], r, keyf[b][:, t:t + 1], None, ALU.is_equal).then_inc(s["p_ready"], 1)
                            c.link(nc.vector.scalar_tensor_tensor(junk[:, :], r, keyf[b][:, t:t + 1], T["lower"][:, :], ALU.is_equal, ALU.mult,
                                                                  accum_out=cnt[b][:, 0, t:t + 1]))
                        c.link(nc.vector.tensor_tensor(cnt[b][:, 1, :], T["spare"][:, :], keyf[b][:, :], ALU.subtract))
                        dve.wait_ge(s["p_ready"], g * TG + TG)
                        nc.vector.tensor_scalar(cnt[b][:, 0, :], cnt[b][:, 0, :], 0.5, None, ALU.is_gt).then_inc(in_free[b], 1)
                        dve.wait_ge(in_free[b], i + 1)
                        for t in range(TG):
                            dve.wait_ge(added[t], summed + 32 * i)
                            c.link(nc.vector.scalar_tensor_tensor(idx[b][t][:, :], cnt[b][:, 0, t:t + 1], cnt[b][:, 1, t:t + 1], keyf[b][:, t:t + 1],
                                                                  ALU.mult, ALU.add))
                        dve.sem_inc(s["idx_ready"], 1)
                    c.end()

            @block.scalar
            def _(act):
                with act.Fori(0, S.groups) as g:
                    for t in range(TG):
                        act.wait_ge(s["agg_ready"], g * TG + t + 1)
                        act.wait_ge(added[t], summed + 16 * g)
                        nc.scalar.activation(msg[t][:, :], AGG[t % 2][:, 0:MSG2], ACT.Copy).then_inc(s["msg_ready"], 1)

            @block.tensor
            def _(pe):
                with pe.Fori(0, S.pairs) as i:
                    for b in range(2):
                        g = i * 2 + b
                        for t in range(TG):
                            pe.wait_ge(s["p_ready"], g * TG + t + 1)
                            pe.wait_ge(s["msg_ready"], g * TG + max(t - 1, 0))
                            nc.tensor.matmul(AGG[t % 2][:, 0:MSG2], Sk[b][:, t, :], prod[b][:, t, :], start=True, stop=True).then_inc(s["agg_ready"], 1)
        T["added_count"] += 16 * S.groups


def transformer_post(nc, T, D, S, agg, h_in):
    stages = [(FEAT, FEAT, "L2_proj"), (FEAT, 384, "L2_f1"), (320, FEAT, "L2_f2")]
    names = ["w_loaded", "in_loaded", "in_free", "dve_step", "in_ready", "tr_ready", "tr_copied", "out_ready", "out_copied",
             "var_ready", "root_ready", "pre_ready", "act_done"]
    with phase(nc, names) as s, ExitStack() as st:
        def sb(n, sh, dt=F32):
            return st.enter_context(nc.sbuf_tensor(f"tp_{n}", sh, dt))
        ws, bs = [], []
        for fi, fo, n in stages:
            ws.append([sb(f"w{n}{q}", [min(P, fi - q * P), fo]) for q in range(-(-fi // P))])
            bs.append(sb(f"b{n}", [P, fo]))
        nw = sum(len(w) for w in ws)
        pr = sb("pr", [P, 2 * FEAT])
        part = [sb(f"part{q}", [P, NB, MSG2]) for q in range(COPIES)]
        X = [sb("X0", [P, NB, FEAT]), sb("X1", [P, NB, FEAT]), sb("X2", [P, NB, 320])]
        O = [sb("O0", [P, NB, FEAT]), sb("O1", [P, NB, 384]), sb("O2", [P, NB, FEAT])]
        xm = sb("xm", [P, NB, FEAT])
        sq = sb("sq", [P, NB, FEAT])
        ev = sb("ev", [P, NB, 8])
        rd = sb("rd", [P, NB, HEADS])
        gate = sb("gate", [P, NB, 192])
        XT = [sb(f"XT{q}", [P, 3 * P]) for q in range(2)]
        TR = [T["bank"][6], T["bank"][7]]
        OUT = [T["bank"][4], T["bank"][5]]
        per = 22
        with nc.Block() as block:
            @block.sync
            def _(sp):
                for (fi, fo, n), w, b in zip(stages, ws, bs):
                    for q, part_w in enumerate(w):
                        k = part_w.shape[0]
                        sp.dma_start(part_w[:, :], D[n][q * P:q * P + k, :]).then_inc(s["w_loaded"], 16)
                    sp.dma_start(b[:, :], D[n + "_b"].partition_broadcast(P)).then_inc(s["w_loaded"], 16)
                sp.dma_start(pr[:, :], D["L2_ln2"].partition_broadcast(P)).then_inc(s["w_loaded"], 16)
                with sp.Fori(0, S.node_groups) as g:
                    sp.wait_ge(s["in_free"], g)
                    sp.sem_inc(T["past"], 1)
                    for q in range(COPIES):
                        rows = agg[q][0:S.node_rows, :].rearrange("(t p) f -> p t f", p=P)
                        sp.dma_start(part[q][:, :, :], rows[:, bass.ds(g * NB, NB), :]).then_inc(s["in_loaded"], 16)

            @block.vector
            def _(dve):
                dve.wait_ge(s["w_loaded"], 16 * (nw + 4))
                with dve.Fori(0, S.node_groups) as g:
                    c = Chain(dve, s["dve_step"], per, g)
                    a0 = T["a"][:, bass.ds(g * NB, NB)]

                    def product(stage):
                        dve.sem_inc(s["in_ready"], 1)
                        for t in range(NB):
                            m = 3 * NB * g + stage * NB + t
                            dve.wait_ge(s["out_ready"], m + 1)
                            fo = stages[stage][1]
                            nc.vector.tensor_tensor(O[stage][:, t, :], OUT[m_parity(stage, t)][:, 0:fo], bs[stage][:, :], ALU.add).then_inc(s["out_copied"], 1)
                        dve.wait_ge(s["out_copied"], 3 * NB * g + stage * NB + NB)

                    dve.wait_ge(s["in_loaded"], 64 * g + 64)
                    c.link(nc.vector.tensor_tensor(part[0][:, :, :], part[0][:, :, :], part[1][:, :, :], ALU.add))
                    c.link(nc.vector.tensor_tensor(part[2][:, :, :], part[2][:, :, :], part[3][:, :, :], ALU.add))
                    c.link(nc.vector.tensor_tensor(part[0][:, :, :], part[0][:, :, :], part[2][:, :, :], ALU.add))
                    c.link(nc.vector.tensor_scalar(rd[:, :, :], part[0][:, :, FEAT:MSG2], 1e-12, None, ALU.add))
                    c.link(nc.vector.reciprocal(rd[:, :, :], rd[:, :, :]))
                    nc.vector.tensor_tensor(X[0][:, :, 0:NS].rearrange("p t (h k) -> p t h k", k=HD), part[0][:, :, 0:NS].rearrange("p t (h k) -> p t h k", k=HD),
                                            rd[:, :, :].unsqueeze(3).to_broadcast([P, NB, HEADS, HD]), ALU.mult)
                    for t in range(NB):
                        ins = nc.vector.tensor_tensor(X[0][:, t, NS:FEAT].rearrange("p (k h j) -> p k h j", k=3, j=NV // HEADS),
                                                      part[0][:, t, NS:FEAT].rearrange("p (k h j) -> p k h j", k=3, j=NV // HEADS),
                                                      rd[:, t, :].unsqueeze(1).unsqueeze(3).to_broadcast([P, 3, HEADS, NV // HEADS]), ALU.mult)
                    c.link(ins)
                    dve.sem_inc(s["in_free"], 1)
                    product(0)
                    c.link(nc.vector.tensor_tensor(xm[:, :, :], O[0][:, :, :], h_in[:, bass.ds(g * NB, NB), 0:FEAT], ALU.add))
                    c.link(nc.vector.reduce_sum(ev[:, :, 0], xm[:, :, 0:NS], AX.X))
                    c.link(nc.vector.tensor_scalar(ev[:, :, 0], ev[:, :, 0], 1.0 / NS, None, ALU.mult))
                    nc.vector.tensor_copy(X[1][:, :, NS:FEAT], xm[:, :, NS:FEAT])
                    c.link(nc.vector.tensor_tensor(X[1][:, :, 0:NS], xm[:, :, 0:NS], ev[:, :, 0:1].to_broadcast([P, NB, NS]), ALU.subtract))
                    c.link(nc.vector.tensor_tensor(sq[:, :, :], X[1][:, :, :], X[1][:, :, :], ALU.mult))
                    c.link(nc.vector.reduce_sum(ev[:, :, 1], sq[:, :, 0:NS], AX.X))
                    c.link(nc.vector.reduce_sum(ev[:, :, 2], sq[:, :, NS:FEAT], AX.X))
                    c.link(nc.vector.tensor_scalar(ev[:, :, 1], ev[:, :, 1], 1.0 / NS, EPS, ALU.mult, ALU.add))
                    nc.vector.tensor_scalar(ev[:, :, 2], ev[:, :, 2], 1.0 / (3 * NV), EPS, ALU.mult, ALU.add).then_inc(s["var_ready"], 1)
                    dve.wait_ge(s["root_ready"], g + 1)
                    c.link(nc.vector.reciprocal(ev[:, :, 5:7], ev[:, :, 3:5]))
                    nc.vector.tensor_tensor(X[1][:, :, 0:NS], X[1][:, :, 0:NS], ev[:, :, 5:6].to_broadcast([P, NB, NS]), ALU.mult)
                    c.link(nc.vector.tensor_tensor(X[1][:, :, NS:FEAT], X[1][:, :, NS:FEAT], ev[:, :, 6:7].to_broadcast([P, NB, 96]), ALU.mult))
                    c.link(nc.vector.tensor_tensor(X[1][:, :, :], X[1][:, :, :], pr[:, 0:FEAT].unsqueeze(1).to_broadcast([P, NB, FEAT]), ALU.mult))
                    c.link(nc.vector.tensor_tensor(X[1][:, :, :], X[1][:, :, :], pr[:, FEAT:2 * FEAT].unsqueeze(1).to_broadcast([P, NB, FEAT]), ALU.add))
                    product(1)
                    nc.vector.tensor_tensor(O[1][:, :, :], O[1][:, :, :], a0.unsqueeze(2).to_broadcast([P, NB, 384]), ALU.mult).then_inc(s["pre_ready"], 1)
                    dve.wait_ge(s["act_done"], g + 1)
                    nc.vector.tensor_tensor(X[2][:, :, 0:P], O[1][:, :, 0:P], gate[:, :, 0:P], ALU.mult)
                    for t in range(NB):
                        ins = nc.vector.tensor_tensor(X[2][:, t, P:320].rearrange("p (k c) -> p k c", k=3), O[1][:, t, 192:384].rearrange("p (k c) -> p k c", k=3),
                                                      gate[:, t, P:192].unsqueeze(1).to_broadcast([P, 3, 64]), ALU.mult)
                    c.link(ins)
                    product(2)
                    c.link(nc.vector.tensor_tensor(O[2][:, :, :], O[2][:, :, :], a0.unsqueeze(2).to_broadcast([P, NB, FEAT]), ALU.mult))
                    c.link(nc.vector.tensor_tensor(O[2][:, :, :], O[2][:, :, :], xm[:, :, :], ALU.add))
                    x = T["x"][:, bass.ds(g * NB, NB), :]
                    c.link(nc.vector.tensor_tensor(x, x, O[2][:, :, :], ALU.add))
                    c.end()

            @block.scalar
            def _(act):
                with act.Fori(0, S.node_groups) as g:
                    for stage, (fi, fo, n) in enumerate(stages):
                        if stage == 1:
                            act.wait_ge(s["var_ready"], g + 1)
                            nc.scalar.activation(ev[:, :, 3:5], ev[:, :, 1:3], ACT.Sqrt).then_inc(s["root_ready"], 1)
                        if stage == 2:
                            act.wait_ge(s["pre_ready"], g + 1)
                            nc.scalar.activation(gate[:, :, :], O[1][:, :, 0:192], ACT.Sigmoid).then_inc(s["act_done"], 1)
                        for t in range(NB):
                            m = 3 * NB * g + stage * NB + t
                            q = m_parity(stage, t)
                            act.wait_ge(s["tr_ready"], m + 1)
                            if stage + t > 1 or t > 1:
                                act.wait_ge(s["out_ready"], m - 1)
                            else:
                                act.wait_ge(s["out_ready"], 3 * NB * g)
                            for k in range(len(ws[stage])):
                                r = ws[stage][k].shape[0]
                                ins = nc.scalar.activation(XT[q][0:r, k * P:(k + 1) * P], TR[q][0:r, k * P:(k + 1) * P], ACT.Copy)
                            ins.then_inc(s["tr_copied"], 1)

            @block.tensor
            def _(pe):
                pe.wait_ge(s["w_loaded"], 16 * (nw + 4))
                with pe.Fori(0, S.node_groups) as g:
                    for stage, (fi, fo, n) in enumerate(stages):
                        pe.wait_ge(s["in_ready"], 3 * g + stage + 1)
                        for t in range(NB):
                            m = 3 * NB * g + stage * NB + t
                            q = m_parity(stage, t)
                            if stage * NB + t > 1:
                                pe.wait_ge(s["out_copied"], m - 1)
                                pe.wait_ge(s["tr_copied"], m - 1)
                            else:
                                pe.wait_ge(s["out_copied"], 3 * NB * g)
                                pe.wait_ge(s["tr_copied"], 3 * NB * g)
                            for k, w in enumerate(ws[stage]):
                                r = w.shape[0]
                                ins = nc.tensor.transpose(TR[q][0:r, k * P:(k + 1) * P], X[stage][:, t, k * P:k * P + r], T["ident"][:, :])
                            ins.then_inc(s["tr_ready"], 1)
                            pe.wait_ge(s["tr_copied"], m + 1)
                            for k, w in enumerate(ws[stage]):
                                r = w.shape[0]
                                ins = nc.tensor.matmul(OUT[q][:, 0:fo], XT[q][0:r, k * P:(k + 1) * P], w[:, :], start=(k == 0), stop=(k == len(ws[stage]) - 1))
                            ins.then_inc(s["out_ready"], 1)


def m_parity(stage, t):
    return (stage * NB + t) % 2


def direction_phase(nc, D, S, direction6, direction5):
    n = S.groups * TG
    with phase(nc, ["loaded", "step", "radicand_ready", "root_ready", "stored"]) as s, ExitStack() as st:
        def sb(nm, sh, dt=F32):
            return st.enter_context(nc.sbuf_tensor(f"dir_{nm}", sh, dt))
        v, sq, r = sb("v", [P, n, 3]), sb("sq", [P, n, 3]), sb("r", [P, 2, n])
        y6, y5 = sb("y6", [P, n, 6]), sb("y5", [P, n, 5])
        with nc.Block() as block:
            @block.sync
            def _(sp):
                sp.dma_start(v[:, :, :].rearrange("p (g t) k -> p g (t k)", t=TG), D["attr3"].rearrange("(g p) c -> p g c", p=P)).then_inc(s["loaded"], 16)
                sp.wait_ge(s["step"], 9)
                sp.dma_start(direction6.rearrange("(g p) c -> p g c", p=P), y6[:, :, :].rearrange("p (g t) k -> p g (t k)", t=TG)).then_inc(s["stored"], 16)
                sp.dma_start(direction5.rearrange("(g p) c -> p g c", p=P), y5[:, :, :].rearrange("p (g t) k -> p g (t k)", t=TG)).then_inc(s["stored"], 16)
                sp.wait_ge(s["stored"], 32)

            @block.vector
            def _(dve):
                c = Chain(dve, s["step"])
                dve.wait_ge(s["loaded"], 16)
                c.link(nc.vector.tensor_tensor(sq[:, :, :], v[:, :, :], v[:, :, :], ALU.mult))
                c.link(nc.vector.reduce_sum(r[:, 0, :], sq[:, :, :], AX.X))
                c.link(nc.vector.tensor_scalar(r[:, 0, :], r[:, 0, :], 1.0 / 3.0, None, ALU.mult))
                nc.vector.tensor_scalar(r[:, 1, :], r[:, 0, :], 1e-12 / 3.0, None, ALU.add).then_inc(s["radicand_ready"], 1)
                dve.wait_ge(s["root_ready"], 1)
                c.link(nc.vector.reciprocal(sq[:, :, 0:2], sq[:, :, 0:2]))
                c.link(nc.vector.memset(y6[:, :, 0:1], 1.0))
                c.link(nc.vector.tensor_tensor(y6[:, :, 1:4], v[:, :, :], sq[:, :, 0:1].to_broadcast([P, n, 3]), ALU.mult))
                c.link(nc.vector.tensor_tensor(y5[:, :, 0:3], v[:, :, :], sq[:, :, 1:2].to_broadcast([P, n, 3]), ALU.mult))
                c.link(nc.vector.tensor_copy(y5[:, :, 3:5], y5[:, :, 0:2]))
                c.link(nc.vector.tensor_copy(y6[:, :, 4:6], y6[:, :, 1:3]))

            @block.scalar
            def _(act):
                act.wait_ge(s["radicand_ready"], 1)
                nc.scalar.activation(sq[:, :, 0:2].rearrange("p n k -> p k n"), r[:, :, :], ACT.Sqrt).then_inc(s["root_ready"], 1)


def store_phase(nc, T, S, out):
    full = S.nodes // P
    with phase(nc, ["stored"]) as s:
        with nc.Block() as block:
            @block.sync
            def _(sp):
                sp.dma_start(out[0:full * P, :].rearrange("(t p) f -> p t f", p=P), T["x"][:, 0:full, :]).then_inc(s["stored"], 16)
                rest = S.nodes - full * P
                if rest:
                    sp.dma_start(out[full * P:S.nodes, :], T["x"][0:rest, full, :]).then_inc(s["stored"], 16)
                sp.wait_ge(s["stored"], 32 if rest else 16)


def build(nc, D, out, S, layers):
    with ExitStack() as stack:
        def sb(n, sh, dt=F32):
            return stack.enter_context(nc.sbuf_tensor(n, sh, dt))
        T = {
            "x": sb("x_sb", [P, S.node_tiles, FEAT]),
            "a": sb("a_sb", [P, S.node_tiles]),
            "ident": sb("ident", [P, P]),
            "lower": sb("lower", [P, P]),
            "zero": sb("zero", [P, MSG]),
            "ones": sb("ones", [P, P]),
            "spare_i": sb("spare_i", [P, TG], I32),
            "spare": sb("spare", [P, TG]),
            "past": stack.enter_context(nc.semaphore("past")),
            "gathered_count": 0,
            "added_count": 0,
            "gathered": [stack.enter_context(nc.semaphore(f"gathered{b}")) for b in range(2)],
            "added": [stack.enter_context(nc.semaphore(f"added{t}")) for t in range(TG)],
            "bank": [stack.enter_context(nc.psum_tensor(f"bank{n}", [P, 512], F32)) for n in range(8)],
        }
        skip = sb("skip", [P, S.node_tiles, 192])

        def dram(n, sh, dt=F32):
            return nc.dram_tensor(n, sh, dt, kind="Internal").ap()
        agg = [dram(f"agg{q}", [S.agg_rows, MSG]) for q in range(COPIES)]
        agg_count = [dram(f"agg_count{q}", [S.agg_rows, MSG_COUNT]) for q in range(COPIES)]
        table, table_short = dram("table", [S.node_rows, WIDE]), dram("table_short", [S.node_rows, FEAT])
        load_constants(nc, T, D)
        if 0 in layers:
            zero_phase(nc, T, agg, MSG)
            node_pre(nc, T, D, S, "L0", D["L0_pre"], D["L0_pre_scale"], [table], WIDE, skip, True)
            edge_pass(nc, T, D, S, "L0", D["by_dst"], D["attr6"], D["dst_row"], D["attr64"][0:64, :], D["L0_fc1"], D["L0_fc2"],
                      table, agg, ACT.Silu, 1 / 8, True, True)
            node_post(nc, T, D, S, "L0", agg, D["L0_post"], D["L0_post_scale"], skip, True, True)
        if 1 in layers:
            zero_phase(nc, T, agg_count, MSG_COUNT)
            node_pre(nc, T, D, S, "L1", D["L1_pre"], D["L1_pre_scale"], [table_short], FEAT, skip, True)
            edge_pass(nc, T, D, S, "L1", D["by_dst"], D["attr6"], D["dst_row"], D["attr16"], D["L1_fc1"], D["L1_fc2"],
                      table_short, agg_count, ACT.Silu, 1 / 4, False, True)
            node_post(nc, T, D, S, "L1", agg_count, D["L1_post"], D["L1_post_scale"], skip, False, True)
        direction6 = dram("direction6", [S.groups * P, 6 * TG])
        direction5 = dram("direction5", [S.groups * P, 5 * TG])
        if 2 in layers or 3 in layers:
            direction_phase(nc, D, S, direction6, direction5)
        if 2 in layers:
            agg2 = [dram(f"agg2{q}", [S.agg_rows, MSG2]) for q in range(COPIES)]
            table_s, table_d = dram("table_s", [S.node_rows, WIDE]), dram("table_d", [S.node_rows, WIDE])
            values = dram("values", [S.groups * P, TG * FEAT])
            by_head = dram("by_head", [HEADS, S.edge_rows])
            corner, carry = dram("corner", [P, 2]), dram("carry", [HEADS, P // HEADS])
            zero_phase(nc, T, agg2, MSG2)
            node_pre(nc, T, D, S, "L2", D["L2_pre"], D["L2_pre_scale"], [table_s, table_d], 2 * WIDE, skip, False, (D["L2_ln1"], D["L2_pre_b"]))
            with nc.sbuf_tensor("scores", [P, HEADS, S.tiles], F32) as scores:
                message_phase(nc, T, D, S, table_s, table_d, direction5, values, scores)
                softmax_phase(nc, T, D, S, scores, by_head, corner, carry)
                attend_phase(nc, T, D, S, values, scores, agg2)
            transformer_post(nc, T, D, S, agg2, skip)
        if 3 in layers:
            zero_phase(nc, T, agg, MSG)
            node_pre(nc, T, D, S, "L3", D["L3_pre"], D["L3_pre_scale"], [table], WIDE, skip, False)
            edge_pass(nc, T, D, S, "L3", D["by_src"], direction6, D["src_row"], D["attr64"][0:64, :], D["L3_fc1"], D["L3_fc2"],
                      table, agg, ACT.Relu, 1.0, True, False)
            node_post(nc, T, D, S, "L3", agg, D["L3_post"], D["L3_post_scale"], skip, True, False)
        store_phase(nc, T, S, out)


def kron3(w):
    out = np.zeros((w.shape[0], 3, w.shape[1], 3), np.float32)
    for k in range(3):
        out[:, k, :, k] = w
    return out.reshape(3 * w.shape[0], 3 * w.shape[1])


def kron3_major(w):
    out = np.zeros((w.shape[0], 3, 3, w.shape[1]), np.float32)
    for k in range(3):
        out[:, k, k, :] = w
    return out.reshape(3 * w.shape[0], 3 * w.shape[1])


def pre_weights(ws_table, wv_table, ws_skip=None, wv_skip=None, wide=False):
    parts = [np.zeros((FEAT, NS), np.float32), np.zeros((FEAT, 3 * NV), np.float32)]
    parts[0][0:NS] = ws_table
    parts[1][NS:] = kron3_major(wv_table)
    if wide:
        parts.append(parts[1][:, 0:2 * NV])
    if ws_skip is not None:
        a = np.zeros((FEAT, ws_skip.shape[1]), np.float32)
        a[0:NS] = ws_skip
        b = np.zeros((FEAT, 3 * NV), np.float32)
        b[NS:] = kron3(wv_skip)
        parts += [a, b]
    return np.concatenate(parts, 1)


def post_weights(ws, wv, cross, extra=None):
    cols = ws.shape[1]
    out = np.zeros((MSG if cross else MSG_COUNT, cols + 3 * NV + (1 if extra is not None else 0)), np.float32)
    out[A0:D0, 0:cols] = ws[0:NS]
    out[D0:B0, 0:cols] = ws[NS:]
    for k in range(3):
        out[B0 + NS * k:B0 + NS * (k + 1), cols + k:cols + 96:3] = wv[0:NS]
        out[C0 + NV * k:C0 + NV * (k + 1), cols + k:cols + 96:3] = wv[NS:NS + NV]
        if cross:
            out[X0 + NV * k:X0 + NV * (k + 1), cols + k:cols + 96:3] = wv[NS + NV:]
    if extra is not None:
        out[A0:D0, -1:] = extra[0:NS]
        out[D0:B0, -1:] = extra[NS:]
    return out


def mid_scales(s, v, dot, cross, rows=MSG):
    out = np.full((rows, 1), v, np.float32)
    out[A0:D0] = s
    out[D0:B0] = s * dot
    out[X0:] = v * cross
    return out


def half_scales(s, v):
    return np.concatenate([np.full((NS, 1), s, np.float32), np.full((3 * NV, 1), v, np.float32)])


def rows_of(a, count, fill):
    out = np.full((count,) + a.shape[1:], fill, a.dtype)
    out[0:len(a)] = a
    return out


def by_group(a, S):
    k = a.shape[1]
    return np.ascontiguousarray(a.reshape(S.groups, TG, P, k).transpose(0, 2, 1, 3).reshape(S.groups * P, TG * k))


def weight_columns(w):
    return np.concatenate([w[:, 0:64], w[:, 160:192], w[:, 64:128], w[:, 128:160], w[:, 192:]], 1)


def layout(inputs, S):
    n = {k: np.asarray(v) for k, v in inputs.items()}
    a = {}
    a["x"] = rows_of(n["x"], S.node_rows, 0)
    a["node_vec1"] = rows_of(n["node_vec1"], S.node_rows, 0)
    last = S.node_rows - 1
    src, dst = (rows_of(n[k].reshape(-1, 1), S.edge_rows, last) for k in ("src", "dst"))
    gs, gd = by_group(src, S), by_group(dst, S)
    before = np.concatenate([np.full((S.tiles, 1), -1, np.int32), dst.reshape(S.tiles, P)[:, :-1]], 1)
    a["by_dst"] = np.concatenate([gs, gd, by_group(before.reshape(-1, 1), S)], 1)
    a["by_src"] = np.concatenate([gd, gs, gs], 1)
    a["dst_row"], a["src_row"] = dst.reshape(1, -1), src.reshape(1, -1)
    e4 = rows_of(n["edge_attr_4"], S.edge_rows, 0)
    a["attr6"] = by_group(np.concatenate([e4, e4[:, 1:3]], 1), S)
    a["attr3"] = by_group(rows_of(n["edge_attr_3"], S.edge_rows, 1), S)
    e64 = rows_of(n["edge_attr_64"], S.edge_rows, 0).T
    a["attr64"] = np.concatenate([e64, np.ones((1, S.edge_rows), np.float32)])
    a["attr16"] = np.ascontiguousarray(rows_of(n["edge_attr_16"], S.edge_rows, 0).T)
    q = {k[7:]: v for k, v in n.items() if k.startswith("L0_gnn_")}
    a["L0_pre"] = pre_weights(q["lin1_ws"], q["lin1_wv"], q["sc_ws"], q["sc_wv"], True)
    a["L0_pre_scale"] = half_scales(NS ** -0.5, NV ** -0.5)
    a["L0_fc1"], a["L0_fc2"] = q["fc_w1"], weight_columns(q["fc_w2"])
    a["L0_post"] = post_weights(q["lin2_ws"], q["lin2_wv"], True)
    a["L0_post_scale"] = mid_scales(96 ** -0.5 / 32, 128 ** -0.5 / 32, 3 ** -0.5, 2 ** -0.5)
    q = {k[7:]: v for k, v in n.items() if k.startswith("L1_gnn_")}
    a["L1_pre"] = pre_weights(q["Wl1_0"], q["Wl1_1"], q["Wsc0"], q["Wsc1"])
    a["L1_pre_scale"] = a["L0_pre_scale"]
    a["L1_fc1"], a["L1_fc2"] = q["Wfc1"], weight_columns(q["Wfc2"])
    a["L1_post"] = post_weights(q["Wl2_s"], q["Wl2_v"], False, q["Wa"])
    a["L1_post_scale"] = mid_scales(96 ** -0.5 / 8, 96 ** -0.5 / 8, 3 ** -0.5, 1.0, MSG_COUNT)
    a["dst_wide"] = np.concatenate([np.full((1, 1), -1, np.int32), a["dst_row"], np.full((1, 1), -1, np.int32)], 1)
    q = {k[7:]: v for k, v in n.items() if k.startswith("L2_gnn_")}
    def wide(ws, wv):
        m = pre_weights(ws, wv)
        return np.concatenate([m, m[:, NS:NS + 2 * NV]], 1)
    a["L2_pre"] = np.concatenate([wide(q["msrc_ws"], q["msrc_wv"]), wide(q["mdst_ws"], q["mdst_wv"])], 1)
    a["L2_pre_scale"] = half_scales(1.0, 1.0)
    a["L2_pre_b"] = np.zeros((1, 2 * WIDE), np.float32)
    a["L2_pre_b"][0, WIDE:WIDE + NS] = q["mdst_bs"]

    def norm_rows(w0, b0, w1):
        return np.concatenate([w0, np.repeat(w1, 3), b0, np.zeros(3 * NV, np.float32)])[None]
    a["L2_ln1"] = norm_rows(q["ln1_w0"], q["ln1_b0"], q["ln1_w1"])
    a["L2_ln2"] = norm_rows(q["ln2_w0"], q["ln2_b0"], q["ln2_w1"])
    a["L2_rw1"] = np.concatenate([q["rw1"], q["rb1"][None]])
    a["L2_rw2"] = np.concatenate([q["rw2"], q["rb2"][None]])
    r3 = np.concatenate([q["rw3"], q["roff"][None]])
    a["L2_rw3"] = np.concatenate([r3[:, 0:128], r3[:, 160:224], r3[:, 128:160]], 1)
    a["L2_gb"] = np.stack([q["rg1"], q["rbe1"], q["rg2"], q["rbe2"]], 1)
    lin, sc = np.zeros((R_ + 1, 256), np.float32), np.ones((3 * P, 1), np.float32)
    lin[0:NS, 32:160] = q["lin_ws"][0:NS]
    lin[NS:2 * NS, 0:32] = q["lin_wv"][0:NS]
    lin[128:160, 32:160] = q["lin_ws"][NS:]
    sc[128:160] = 3 ** -0.5
    sc[160:256] = 2 ** -0.5
    for k in range(3):
        lin[256 + NV * k:288 + NV * k, 160 + NV * k:192 + NV * k] = q["lin_wv"][NS:NS + NV]
        lin[160 + NV * k:192 + NV * k, 160 + NV * k:192 + NV * k] = q["lin_wv"][NS + NV:]
    lin[R_, 32:160] = q["lin_bs"]
    a["L2_lin"], a["L2_lin_scale"] = lin, np.ascontiguousarray(sc.reshape(3, P).T)
    a["L2_dots"] = q["alpha_dot"].reshape(1, -1)
    def vec_rows(w):
        return kron3_major(w.T).T
    proj = np.zeros((FEAT, FEAT), np.float32)
    proj[0:NS, 0:NS] = q["proj_ws"]
    proj[NS:, NS:] = vec_rows(q["proj_wv"])
    a["L2_proj"] = proj
    a["L2_proj_b"] = np.zeros((1, FEAT), np.float32)
    a["L2_proj_b"][0, 0:NS] = q["proj_bs"]
    f1 = np.zeros((FEAT, 384), np.float32)
    f1[0:NS, 0:192] = q["f1_ws"]
    f1[NS:, 192:] = kron3_major(q["f1_wv"])
    a["L2_f1"] = f1
    a["L2_f1_b"] = np.zeros((1, 384), np.float32)
    a["L2_f1_b"][0, 0:192] = q["f1_bs"]
    f2 = np.zeros((320, FEAT), np.float32)
    f2[0:128, 0:NS] = q["f2_ws"]
    f2[128:, NS:] = vec_rows(q["f2_wv"])
    a["L2_f2"] = f2
    a["L2_f2_b"] = np.zeros((1, FEAT), np.float32)
    a["L2_f2_b"][0, 0:NS] = q["f2_bs"]
    q = {k[7:]: v for k, v in n.items() if k.startswith("L3_gnn_")}
    a["L3_pre"] = pre_weights(q["W_nl0"], q["W_nl1"], q["W_skip0"], q["W_skip1"], True)
    a["L3_pre_scale"] = half_scales(1.0, 1.0)
    a["L3_fc1"], a["L3_fc2"] = q["W_fc1"], weight_columns(q["W_fc2"])
    a["L3_post"] = post_weights(q["W_out_s"], q["W_out_v"], True)
    a["L3_post_scale"] = mid_scales(1 / 32, 1 / 32, 3 ** -0.5, 2 ** -0.5)
    return a


LAYERS = (0, 1, 2, 3)


def kernel(**inputs):
    from concourse import bacc
    from concourse.bass_utils import run_bass_kernel_spmd
    S = Shapes(inputs["x"].shape[0], inputs["src"].shape[0])
    arrays = {k: np.ascontiguousarray(v) for k, v in layout(inputs, S).items()}
    nc = bacc.Bacc("TRN2", target_bir_lowering=False, num_devices=1)
    D = {k: nc.dram_tensor(f"in_{k}", v.shape, mybir.dt.from_np(v.dtype), kind="ExternalInput").ap() for k, v in arrays.items()}
    D["shapes"] = S
    out = nc.dram_tensor("out_x", (S.nodes, FEAT), F32, kind="ExternalOutput").ap()
    build(nc, D, out, S, LAYERS)
    r = run_bass_kernel_spmd(nc, [{f"in_{k}": v for k, v in arrays.items()}], core_ids=[0])
    return r.results[0]["out_x"]
```

```python
import numpy as np
import concourse.bass as bass
from concourse import mybir
from contextlib import ExitStack, contextmanager

F32 = mybir.dt.float32
I32 = mybir.dt.int32
ALU = mybir.AluOpType
ACT = mybir.ActivationFunctionType
AX = mybir.AxisListType

P = 128
TG = 4
GE = TG * P
NB = 5
NS, NV = 64, 32
FEAT = NS + 3 * NV
COPIES = TG
MSG = 480
MSG_COUNT = 388
A0, D0, B0, C0, X0 = 0, 64, 96, 288, 384
EPS = 1e-5


class Shapes:

    def __init__(self, nodes, edges):
        self.nodes, self.edges = nodes, edges
        self.node_groups = -(-nodes // (NB * P))
        self.node_tiles = self.node_groups * NB
        self.node_rows = self.node_tiles * P
        assert nodes < self.node_rows, "the last row takes the padding edges"
        self.agg_rows = self.node_rows + P
        self.pairs = -(-edges // (2 * GE))
        self.groups = 2 * self.pairs
        self.tiles = self.groups * TG
        self.edge_rows = self.tiles * P


class Chain:

    def __init__(self, engine, sem, per_iteration=0, iteration=0):
        self.engine, self.sem, self.per, self.it, self.n = engine, sem, per_iteration, iteration, 0

    def link(self, instruction):
        self.n += 1
        instruction.then_inc(self.sem, 1)
        self.engine.wait_ge(self.sem, self.it * self.per + self.n)

    def mark(self, instruction):
        self.n += 1
        instruction.then_inc(self.sem, 1)
        value = self.it * self.per + self.n
        return lambda: self.engine.wait_ge(self.sem, value)

    def end(self):
        assert self.n == self.per, f"links of an iteration: {self.n}"


@contextmanager
def phase(nc, names):
    with ExitStack() as stack:
        sems = {n: stack.enter_context(nc.semaphore(n)) for n in names}
        stack.enter_context(nc.allow_non_contiguous_dma(reason="small strided loads"))
        yield sems
        for s in sems.values():
            nc.gpsimd.sem_clear(s)
        nc.all_engine_barrier()


def load_constants(nc, T, D):
    with phase(nc, ["const_loaded", "mask_step"]) as s:
        with nc.Block() as block:
            @block.sync
            def _(sp):
                sp.dma_start(T["x"][:, :, :], D["x"].rearrange("(t p) f -> p t f", p=P)).then_inc(s["const_loaded"], 16)
                sp.dma_start(T["a"][:, :], D["node_vec1"].rearrange("(t p) o -> p (t o)", p=P)).then_inc(s["const_loaded"], 16)
                sp.wait_ge(s["const_loaded"], 32)

            @block.gpsimd
            def _(pool):
                pool.memset(T["ident"][:, :], 0.0).then_inc(s["mask_step"], 1)
                pool.memset(T["lower"][:, :], 1.0).then_inc(s["mask_step"], 1)
                pool.memset(T["zero"][:, :], 0.0).then_inc(s["mask_step"], 1)
                pool.iota(T["spare_i"][:, :], pattern=[[0, TG]], base=D["shapes"].node_rows, channel_multiplier=1).then_inc(s["mask_step"], 1)
                pool.wait_ge(s["mask_step"], 4)
                pool.affine_select(out=T["ident"][:, :], in_=T["ident"][:, :], compare_op=ALU.not_equal, fill=1.0,
                                   base=0, pattern=[[-1, P]], channel_multiplier=1).then_inc(s["mask_step"], 1)
                pool.affine_select(out=T["lower"][:, :], in_=T["lower"][:, :], compare_op=ALU.is_gt, fill=0.0,
                                   base=0, pattern=[[-1, P]], channel_multiplier=1).then_inc(s["mask_step"], 1)
                pool.tensor_copy(T["spare"][:, :], T["spare_i"][:, :]).then_inc(s["mask_step"], 1)
                pool.wait_ge(s["mask_step"], 7)


def norm_steps(nc, T, dve, c, s, src, h, stats, mv, g):
    for t in range(NB):
        ins = nc.vector.bn_stats(stats[:, t, :], src(t))
        ins.then_inc(s["dve_step"], 1)
    c.n += NB
    dve.wait_ge(s["dve_step"], c.it * c.per + c.n)
    dve.sem_inc(T["past"], 1)
    for t in range(NB):
        nc.vector.bn_aggr(mv[:, t, 0:2], stats[:, t, :]).then_inc(s["dve_step"], 1)
    c.n += NB
    dve.wait_ge(s["dve_step"], c.it * c.per + c.n)
    nc.vector.tensor_scalar(mv[:, :, 2], mv[:, :, 1], EPS, None, ALU.add).then_inc(s["var_ready"], 1)


NORM_LINKS = 2 * NB + 1 + NB + 1


def norm_finish(nc, dve, c, s, src, h, mv, roots):
    dve.wait_ge(s["root_ready"], roots)
    c.link(nc.vector.reciprocal(mv[:, :, 4], mv[:, :, 3]))
    for t in range(NB):
        nc.vector.tensor_scalar(h[:, t, :], src(t), mv[:, t, 0:1], mv[:, t, 4:5], ALU.subtract, ALU.mult).then_inc(s["dve_step"], 1)
    c.n += NB
    dve.wait_ge(s["dve_step"], c.it * c.per + c.n)
    c.link(nc.vector.tensor_scalar(h[:, :, :], h[:, :, :], 0.0, None, ALU.max))


def node_pre(nc, T, D, S, L, w_dram, scale_dram, tables, width, skip, attr, sums, eq=None):
    M = w_dram.shape[1]
    skipw = M - width
    names = ["w_loaded", "w_scaled", "dve_step", "var_ready", "root_ready", "h_ready", "tr_ready", "tr_copied",
             "out_ready", "out_copied", "table_ready", "stored", "act_step", "zeroed"]
    with phase(nc, names) as s, ExitStack() as st:
        def sb(n, sh, dt=F32):
            return st.enter_context(nc.sbuf_tensor(f"{L}pre_{n}", sh, dt))
        w1, w2 = sb("w1", [P, M]), sb("w2", [NV, M])
        rs1, rs2 = sb("rs1", [P, 1]), sb("rs2", [NV, 1])
        stats, mv = sb("stats", [P, NB, 6]), sb("mv", [P, NB, 5])
        h = sb("h", [P, NB, FEAT])
        hT = sb("hT", [P, 2, 2 * P])
        tab = sb("tab", [P, NB, width])
        TR = [T["bank"][6], T["bank"][7]]
        OUT = [T["bank"][4], T["bank"][5]]
        loads = 4
        if eq:
            sq = sb("sq", [P, NB, FEAT])
            ev = sb("ev", [P, NB, 8])
            pr = sb("pr", [P, 2 * FEAT])
            bias = sb("bias", [P, width])
            loads = 6
        per = NORM_LINKS + (11 + 2 * NB if eq else 0)
        with nc.Block() as block:
            @block.sync
            def _(sp):
                sp.dma_start(w1[:, :], w_dram[0:P, :]).then_inc(s["w_loaded"], 16)
                sp.dma_start(w2[:, :], w_dram[P:FEAT, :]).then_inc(s["w_loaded"], 16)
                sp.dma_start(rs1[:, :], scale_dram[0:P, :]).then_inc(s["w_loaded"], 16)
                sp.dma_start(rs2[:, :], scale_dram[P:FEAT, :]).then_inc(s["w_loaded"], 16)
                if eq:
                    sp.dma_start(pr[:, :], eq[0].partition_broadcast(P)).then_inc(s["w_loaded"], 16)
                    sp.dma_start(bias[:, :], eq[1].partition_broadcast(P)).then_inc(s["w_loaded"], 16)
                for table in sums:
                    rows, columns = table.shape[0] // P, table.shape[1]
                    zeros = T["zero"][:, 0:columns].unsqueeze(1).to_broadcast([P, rows, columns])
                    sp.dma_start(table.rearrange("(t p) f -> p t f", p=P), zeros).then_inc(s["zeroed"], 16)
                with sp.Fori(0, S.node_groups) as g:
                    sp.wait_ge(s["table_ready"], g + 1)
                    sp.sem_inc(T["past"], 1)
                    for n, table in enumerate(tables):
                        rows = table.rearrange("(t p) f -> p t f", p=P)
                        part = width // len(tables)
                        sp.dma_start(rows[:, bass.ds(g * NB, NB), :], tab[:, :, n * part:(n + 1) * part]).then_inc(s["stored"], 16)
                    sp.wait_ge(s["stored"], 16 * len(tables) * (g + 1))
                    sp.sem_inc(T["past"], 1)
                sp.wait_ge(s["zeroed"], 16 * len(sums))

            @block.vector
            def _(dve):
                dve.wait_ge(s["w_loaded"], 16 * loads)
                nc.vector.tensor_scalar(w1[:, :], w1[:, :], rs1[:, 0:1], None, ALU.mult).then_inc(s["w_scaled"], 1)
                nc.vector.tensor_scalar(w2[:, :], w2[:, :], rs2[:, 0:1], None, ALU.mult).then_inc(s["w_scaled"], 1)
                with dve.Fori(0, S.node_groups) as g:
                    c = Chain(dve, s["dve_step"], per, g)
                    x = T["x"][:, bass.ds(g * NB, NB), :]
                    dve.wait_ge(s["tr_ready"], g * NB)
                    norm_steps(nc, T, dve, c, s, lambda t: x[:, t, :], h, stats, mv, g)
                    norm_finish(nc, dve, c, s, lambda t: x[:, t, :], h, mv, (2 if eq else 1) * g + 1)
                    if eq:
                        c.link(nc.vector.tensor_copy(skip[:, bass.ds(g * NB, NB), 0:FEAT], h[:, :, :]))
                        c.link(nc.vector.reduce_sum(ev[:, :, 0], h[:, :, 0:NS], AX.X))
                        c.link(nc.vector.tensor_scalar(ev[:, :, 0], ev[:, :, 0], 1.0 / NS, None, ALU.mult))
                        c.link(nc.vector.tensor_tensor(h[:, :, 0:NS], h[:, :, 0:NS],
                                                       ev[:, :, 0:1].to_broadcast([P, NB, NS]), ALU.subtract))
                        c.link(nc.vector.tensor_tensor(sq[:, :, :], h[:, :, :], h[:, :, :], ALU.mult))
                        c.link(nc.vector.reduce_sum(ev[:, :, 1], sq[:, :, 0:NS], AX.X))
                        c.link(nc.vector.reduce_sum(ev[:, :, 2], sq[:, :, NS:FEAT], AX.X))
                        c.link(nc.vector.tensor_scalar(ev[:, :, 1], ev[:, :, 1], 1.0 / NS, EPS, ALU.mult, ALU.add))
                        nc.vector.tensor_scalar(ev[:, :, 2], ev[:, :, 2], 1.0 / (3 * NV), EPS, ALU.mult, ALU.add).then_inc(s["var_ready"], 1)
                        dve.wait_ge(s["root_ready"], 2 * g + 2)
                        c.link(nc.vector.reciprocal(ev[:, :, 5:7], ev[:, :, 3:5]))
                        for t in range(NB):
                            c.link(nc.vector.tensor_scalar(h[:, t, 0:NS], h[:, t, 0:NS], ev[:, t, 5:6], None, ALU.mult))
                            c.link(nc.vector.tensor_scalar(h[:, t, NS:FEAT], h[:, t, NS:FEAT], ev[:, t, 6:7], None, ALU.mult))
                        c.link(nc.vector.tensor_tensor(h[:, :, :], h[:, :, :], pr[:, 0:FEAT].unsqueeze(1).to_broadcast([P, NB, FEAT]), ALU.mult))
                        c.link(nc.vector.tensor_tensor(h[:, :, :], h[:, :, :], pr[:, FEAT:2 * FEAT].unsqueeze(1).to_broadcast([P, NB, FEAT]), ALU.add))
                    c.end()
                    dve.sem_inc(s["h_ready"], 1)
                    dve.wait_ge(s["stored"], 16 * len(tables) * g)
                    for t in range(NB):
                        dve.wait_ge(s["out_ready"], g * NB + t + 1)
                        o = OUT[t % 2]
                        if eq:
                            nc.vector.tensor_tensor(tab[:, t, :], o[:, 0:width], bias[:, :], ALU.add).then_inc(s["out_copied"], 1)
                        else:
                            at = T["a"][:, bass.ds(g * NB + t, 1)] if attr else 1.0
                            nc.vector.tensor_scalar(tab[:, t, :], o[:, 0:width], at, None, ALU.mult).then_inc(s["act_step"], 1)
                        if skipw:
                            sk = skip[:, bass.ds(g * NB + t, 1), 0:skipw]
                            nc.vector.tensor_scalar(sk, o[:, width:M].unsqueeze(1), at, None, ALU.mult).then_inc(s["out_copied"], 1)
                    dve.wait_ge(s["out_copied"], g * NB + NB)
                    if not eq:
                        dve.wait_ge(s["act_step"], g * NB + NB)
                    dve.sem_inc(s["table_ready"], 1)

            @block.scalar
            def _(act):
                with act.Fori(0, S.node_groups) as g:
                    act.wait_ge(s["var_ready"], (2 if eq else 1) * g + 1)
                    nc.scalar.activation(mv[:, :, 3], mv[:, :, 2], ACT.Sqrt).then_inc(s["root_ready"], 1)
                    if eq:
                        act.wait_ge(s["var_ready"], 2 * g + 2)
                        nc.scalar.activation(ev[:, :, 3:5], ev[:, :, 1:3], ACT.Sqrt).then_inc(s["root_ready"], 1)
                    for t in range(NB):
                        act.wait_ge(s["tr_ready"], g * NB + t + 1)
                        if t >= 2:
                            act.wait_ge(s["out_ready"], g * NB + t - 1)
                        else:
                            act.wait_ge(s["out_ready"], g * NB)
                        nc.scalar.activation(hT[:, t % 2, 0:P], TR[t % 2][:, 0:P], ACT.Copy)
                        nc.scalar.activation(hT[0:NV, t % 2, P:2 * P], TR[t % 2][0:NV, P:2 * P], ACT.Copy).then_inc(s["tr_copied"], 1)

            @block.tensor
            def _(pe):
                pe.wait_ge(s["w_scaled"], 2)

                def transpose(g, t):
                    pe.wait_ge(s["tr_copied"], g * NB + max(t - 1, 0))
                    tr = TR[t % 2]
                    nc.tensor.transpose(tr[:, 0:P], h[:, t, 0:P], T["ident"][:, :])
                    nc.tensor.transpose(tr[0:NV, P:2 * P], h[:, t, P:FEAT], T["ident"][:, :]).then_inc(s["tr_ready"], 1)
                with pe.Fori(0, S.node_groups) as g:
                    pe.wait_ge(s["h_ready"], g + 1)
                    transpose(g, 0)
                    for t in range(NB):
                        if t + 1 < NB:
                            transpose(g, t + 1)
                        pe.wait_ge(s["out_copied"], g * NB + max(t - 1, 0))
                        if not eq:
                            pe.wait_ge(s["act_step"], g * NB + max(t - 1, 0))
                        o = OUT[t % 2]
                        pe.wait_ge(s["tr_copied"], g * NB + t + 1)
                        nc.tensor.matmul(o[:, 0:M], hT[:, t % 2, 0:P], w1[:, :], start=True, stop=False)
                        nc.tensor.matmul(o[:, 0:M], hT[0:NV, t % 2, P:2 * P], w2[:, :], start=False, stop=True).then_inc(s["out_ready"], 1)


def edge_pass(nc, T, D, S, L, meta, sh_dram, keys, attrT, wA_dram, wB_dram, table, agg, hid_func, hid_scale,
              cross, in_order):
    K, H, W = attrT.shape[0], wA_dram.shape[1], wB_dram.shape[1]
    width, msg_w = table.shape[1], agg[0].shape[1]
    names = ["w_loaded", "all_loaded", "all_step", "ones_ready", "index_ready", "in_free0", "in_free1", "in_loaded0", "in_loaded1", "s_ready",
             "hid_ready", "hid_done", "w_ready", "dve_step", "q_ready", "p_ready", "agg_ready", "msg_ready", "idx_ready"]
    with phase(nc, names) as s, ExitStack() as st:
        def sb(n, sh, dt=F32):
            return st.enter_context(nc.sbuf_tensor(f"{L}e_{n}", sh, dt))
        in_free = [s["in_free0"], s["in_free1"]]
        in_loaded = [s["in_loaded0"], s["in_loaded1"]]
        gathered, fetched = T["gathered"], T["gathered_count"]
        added, summed = T["added"], T["added_count"]
        wA, wB = sb("wA", [K, H]), sb("wB", [H, W])
        at = [sb(f"at{b}", [K, GE]) for b in range(2)]
        row = [sb(f"row{b}", [P, GE], I32) for b in range(2)]
        every = [sb(n, [P, S.tiles + 2 * TG], I32) for n in ("rows", "keys", "before")]
        keyf, spare = sb("keyf", [P, S.tiles]), sb("spare", [P, S.tiles])
        mi = [sb(f"mi{b}", [P, TG], I32) for b in range(2)]
        sh = [sb(f"sh{b}", [P, TG, 6]) for b in range(2)]
        G = [sb(f"G{b}", [P, TG, width]) for b in range(2)]
        Q = [sb(f"Q{b}", [P, TG, MSG]) for b in range(2)]
        t1, t2 = sb("t1", [P, TG, 3 * NV]), sb("t2", [P, TG, 3 * NV])
        hidT = [sb(f"hidT{b}", [H, GE]) for b in range(2)]
        rep = sb("rep", [P, TG])
        off = sb("off", [P, TG])
        junk = sb("junk", [P, P])
        idx = [sb(f"idx{b}", [P, TG], I32) for b in range(2)]
        Sk = [sb(f"S{b}", [P, TG, P]) for b in range(2)]
        prod = [sb(f"prod{t}", [P, msg_w]) for t in range(TG)]
        msg = [sb(f"msg{t}", [P, msg_w]) for t in range(TG)]
        HID = [T["bank"][0], T["bank"][1]]
        WPS = [T["bank"][n][:, 0:W] for n in (2, 3, 6, 7)]
        AGG = [T["bank"][4], T["bank"][5]]
        last = S.pairs - 1
        steps = (1 if in_order else 2 + TG) + (5 if cross else 3)

        def tile(g, t):
            return g * TG + t

        with nc.Block() as block:
            @block.sync
            def _(sp):
                def load(i, b):
                    g = i * 2 + b
                    sp.dma_start(at[b][:, :], attrT[:, bass.ds(g * GE, GE)]).then_inc(in_loaded[b], 16)
                    sp.dma_start(sh[b][:, :, :], sh_dram[bass.ds(g * P, P), :].rearrange("p (t k) -> p t k", k=6)).then_inc(in_loaded[b], 16)
                    sp.dma_start(row[b][:, :], keys[:, bass.ds(g * GE, GE)].partition_broadcast(P)).then_inc(in_loaded[b], 16)
                sp.dma_start(wA[:, :], wA_dram).then_inc(s["w_loaded"], 16)
                sp.dma_start(wB[:, :], wB_dram).then_inc(s["w_loaded"], 16)
                for n, columns in enumerate(every):
                    sp.dma_start(columns[:, :], meta[n]).then_inc(s["all_loaded"], 16)
                load(0, 0)
                load(0, 1)
                with sp.Fori(1, S.pairs) as i:
                    for b in range(2):
                        sp.wait_ge(in_free[b], i)
                        sp.sem_inc(T["past"], 1)
                        load(i, b)

            @block.gpsimd
            def _(pool):
                def gather(i, b):
                    pool.wait_ge(s["index_ready"], i * 2 + b + 1)
                    pool.sem_inc(T["past"], 1)
                    for t in range(TG):
                        pool.indirect_dma_start(G[b][:, t, :], None, table, bass.IndirectOffsetOnAxis(mi[b][:, t:t + 1], 0)).then_inc(gathered[b], 16)

                def scatter(i, b):
                    g = i * 2 + b
                    pool.wait_ge(s["idx_ready"], g + 1)
                    for t in range(TG):
                        pool.wait_ge(s["msg_ready"], tile(g, t) + 1)
                        pool.wait_ge(added[t], summed + 16 * g)
                        pool.sem_inc(T["past"], 1)
                        pool.indirect_dma_start(agg[t], bass.IndirectOffsetOnAxis(idx[b][:, t:t + 1], 0), msg[t][:, :],
                                                None, compute_op=ALU.add).then_inc(added[t], 16)
                gather(0, 0)
                gather(0, 1)
                with pool.Fori(0, last) as i:
                    for b in range(2):
                        gather(i + 1, b)
                        scatter(i, b)
                scatter(last, 0)
                scatter(last, 1)
                for t in range(TG):
                    pool.wait_ge(added[t], summed + 16 * S.groups)

            @block.vector
            def _(dve):
                if not cross:
                    for t in range(TG):
                        nc.vector.memset(prod[t][:, X0:msg_w], 1.0).then_inc(s["ones_ready"], 1)
                c = Chain(dve, s["all_step"])
                dve.wait_ge(s["all_loaded"], 48)
                for b in range(2):
                    nc.vector.tensor_copy(mi[b][:, :], every[0][:, b * TG:(b + 1) * TG]).then_inc(s["index_ready"], 1)
                rows = S.tiles
                c.link(nc.vector.tensor_copy(keyf[:, :], every[1][:, 0:rows]))
                c.link(nc.vector.tensor_scalar(spare[:, :], keyf[:, :], -1.0, T["spare"][:, 0:1], ALU.mult, ALU.add))
                if in_order:
                    same = every[2].bitcast(F32)[:, 0:rows]
                    c.link(nc.vector.tensor_tensor(same, every[1][:, 0:rows], every[2][:, 0:rows], ALU.is_equal))
                    c.link(nc.vector.tensor_tensor(spare[:, :], spare[:, :], same, ALU.mult))
                    c.link(nc.vector.tensor_tensor(spare[:, :], spare[:, :], keyf[:, :], ALU.add))
                with dve.Fori(0, S.pairs) as i:
                    c = Chain(dve, s["dve_step"], 2 * steps, i)
                    for b in range(2):
                        g = i * 2 + b
                        key = keyf[:, bass.ds(g * TG, TG)]
                        dve.wait_ge(in_loaded[b], 48 * i + 48)
                        nc.vector.tensor_tensor(Sk[b][:, :, :], row[b][:, :].rearrange("p (t e) -> p t e", e=P),
                                                every[1][:, bass.ds(g * TG, TG)].unsqueeze(2).to_broadcast([P, TG, P]), ALU.is_equal).then_inc(s["s_ready"], 1)
                        if not in_order:
                            for t in range(TG):
                                c.link(nc.vector.scalar_tensor_tensor(junk[:, :], row[b][:, t * P:(t + 1) * P], keyf[:, bass.ds(g * TG + t, 1)], T["lower"][:, :],
                                                                      ALU.is_equal, ALU.mult, accum_out=rep[:, t:t + 1]))
                            c.link(nc.vector.scalar_tensor_tensor(off[:, :], rep[:, :], 0.5, spare[:, bass.ds(g * TG, TG)], ALU.is_gt, ALU.mult))
                        dve.wait_ge(gathered[b], fetched + 16 * TG * i + 16 * TG)
                        v = G[b][:, :, NS:width]

                        def direction(k):
                            return sh[b][:, :, k:k + 3].unsqueeze(3).to_broadcast([P, TG, 3, NV])

                        def three(x):
                            return x.rearrange("p t (k c) -> p t k c", c=NV)
                        c.link(nc.vector.tensor_tensor(three(t1[:, :, :]), three(v[:, :, 0:96]), direction(1), ALU.mult))
                        if cross:
                            nc.vector.tensor_tensor(three(t2[:, :, :]), three(v[:, :, NV:4 * NV]), direction(3), ALU.mult)
                        c.link(nc.vector.tensor_tensor(t1[:, :, 0:NV], t1[:, :, 0:NV], t1[:, :, NV:2 * NV], ALU.add))
                        c.link(nc.vector.tensor_tensor(Q[b][:, :, D0:B0], t1[:, :, 0:NV], t1[:, :, 2 * NV:3 * NV], ALU.add))
                        if cross:
                            c.link(nc.vector.tensor_tensor(three(t1[:, :, :]), three(v[:, :, 2 * NV:5 * NV]), direction(2), ALU.mult))
                            c.link(nc.vector.tensor_tensor(Q[b][:, :, X0:MSG], t2[:, :, :], t1[:, :, :], ALU.subtract))
                        for t in range(TG):
                            dve.wait_ge(s["w_ready"], tile(g, t) + 1)
                            dve.wait_ge(s["q_ready"], tile(g, t) + 1)
                            w, q, p = WPS[t], Q[b][:, t, :], prod[t]
                            nc.vector.tensor_tensor(p[:, 0:B0], w[:, 0:B0], q[:, 0:B0], ALU.mult)
                            nc.vector.tensor_tensor(p[:, B0:C0].rearrange("p (k c) -> p k c", c=NS), w[:, B0:B0 + NS].unsqueeze(1).to_broadcast([P, 3, NS]),
                                                    q[:, B0:C0].rearrange("p (k c) -> p k c", c=NS), ALU.mult)
                            m = 2 if cross else 1
                            nc.vector.tensor_tensor(p[:, C0:C0 + 96 * m].rearrange("p (m k c) -> p m k c", k=3, c=NV),
                                                    w[:, B0 + NS:W].rearrange("p (m c) -> p m c", c=NV).unsqueeze(2).to_broadcast([P, m, 3, NV]),
                                                    q[:, C0:C0 + 96 * m].rearrange("p (m k c) -> p m k c", k=3, c=NV), ALU.mult).then_inc(s["p_ready"], 1)
                            if t == 2:
                                dve.wait_ge(s["q_ready"], tile(g, TG))
                                nc.vector.tensor_copy(mi[b][:, :], every[0][:, bass.ds((g + 2) * TG, TG)]).then_inc(s["index_ready"], 1)
                                dve.sem_inc(in_free[b], 1)
                        dve.wait_ge(s["msg_ready"], tile(g, 0))
                        if in_order:
                            c.link(nc.vector.tensor_copy(idx[b][:, :], spare[:, bass.ds(g * TG, TG)]))
                        else:
                            c.link(nc.vector.tensor_tensor(idx[b][:, :], off[:, :], key, ALU.add))
                        dve.sem_inc(s["idx_ready"], 1)
                    c.end()

            @block.scalar
            def _(act):
                def hidden(g, b):
                    act.wait_ge(s["hid_ready"], g + 1)
                    nc.scalar.activation(hidT[b][:, :], HID[b][0:H, :], hid_func, scale=hid_scale).then_inc(s["hid_done"], 1)

                def scaled(i, b, t):
                    g, q, e = G[b][:, t, :], Q[b][:, t, :], sh[b][:, t, :]
                    if t == 0:
                        act.wait_ge(in_loaded[b], 48 * i + 48)
                        act.wait_ge(gathered[b], fetched + 16 * TG * i + 16 * TG)
                        act.wait_ge(s["p_ready"], 2 * TG * i)
                    nc.scalar.activation(q[:, A0:D0], g[:, 0:NS], ACT.Copy, scale=e[:, 0:1])
                    for k in range(3):
                        nc.scalar.activation(q[:, B0 + NS * k:B0 + NS * (k + 1)], g[:, 0:NS], ACT.Copy, scale=e[:, k + 1:k + 2])
                    nc.scalar.activation(q[:, C0:X0], g[:, NS:FEAT], ACT.Copy, scale=e[:, 0:1]).then_inc(s["q_ready"], 1)

                def evacuate(g, t):
                    act.wait_ge(s["agg_ready"], tile(g, t) + 1)
                    act.wait_ge(added[t], summed + 16 * g)
                    nc.scalar.activation(msg[t][:, :], AGG[t % 2][:, 0:msg_w], ACT.Copy).then_inc(s["msg_ready"], 1)

                def ahead_then_out(g, ni, nb):
                    for t in range(TG):
                        evacuate(g, t)
                        scaled(ni, nb, t)
                hidden(0, 0)
                for t in range(TG):
                    scaled(0, 0, t)
                with act.Fori(0, last) as i:
                    for b in range(2):
                        hidden(i * 2 + b + 1, 1 - b)
                        ahead_then_out(i * 2 + b, i + b, 1 - b)
                hidden(2 * last + 1, 1)
                ahead_then_out(2 * last, last, 1)
                for t in range(TG):
                    evacuate(2 * last + 1, t)

            @block.tensor
            def _(pe):
                def hidden(i, b):
                    pe.wait_ge(in_loaded[b], 48 * i + 48)
                    pe.sem_inc(T["past"], 1)
                    nc.tensor.matmul(HID[b][0:H, :], wA[:, :], at[b][:, :], start=True, stop=True).then_inc(s["hid_ready"], 1)

                def weights(g, b, t):
                    pe.wait_ge(s["hid_done"], g + 1)
                    nc.tensor.matmul(WPS[t], hidT[b][:, t * P:(t + 1) * P], wB[:, :], start=True, stop=True).then_inc(s["w_ready"], 1)

                def sums(g, b, t):
                    pe.wait_ge(s["s_ready"], g + 1)
                    pe.wait_ge(s["p_ready"], tile(g, t) + 1)
                    pe.wait_ge(s["msg_ready"], tile(g, max(t - 1, 0)))
                    nc.tensor.matmul(AGG[t % 2][:, 0:msg_w], Sk[b][:, t, :], prod[t][:, :], start=True, stop=True).then_inc(s["agg_ready"], 1)

                pe.wait_ge(s["w_loaded"], 32)
                if not cross:
                    pe.wait_ge(s["ones_ready"], TG)
                hidden(0, 0)
                for t in range(TG):
                    weights(0, 0, t)
                with pe.Fori(0, last) as i:
                    for b in range(2):
                        hidden(i + b, 1 - b)
                        for t in range(TG):
                            sums(i * 2 + b, b, t)
                            weights(i * 2 + b + 1, 1 - b, t)
                hidden(last, 1)
                for t in range(TG):
                    sums(2 * last, 0, t)
                    weights(2 * last + 1, 1, t)
                for t in range(TG):
                    sums(2 * last + 1, 1, t)
        T["gathered_count"] += 16 * TG * S.pairs
        T["added_count"] += 16 * S.groups


def node_post(nc, T, D, S, L, agg, w_dram, scale_dram, skip, gated, attr):
    M = w_dram.shape[1]
    msg_w = w_dram.shape[0]
    KC = msg_w // 4
    names = ["w_loaded", "w_scaled", "in_free", "in_loaded", "sum_ready", "dve_step", "tr_ready", "tr_copied", "out_ready",
             "out_copied", "pre_ready", "sig_ready"]
    with phase(nc, names) as s, ExitStack() as st:
        def sb(n, sh, dt=F32):
            return st.enter_context(nc.sbuf_tensor(f"{L}post_{n}", sh, dt))
        w = sb("w", [KC, 4, M])
        rs = sb("rs", [KC, 4])
        part = [sb(f"part{q}", [P, NB, msg_w]) for q in range(COPIES)]
        total = sb("total", [P, NB, msg_w])
        mT = [sb(f"mT{q}", [KC, 4, P]) for q in range(2)]
        o = sb("o", [P, NB, M])
        sg = sb("sg", [P, NB, 96])
        TR = [T["bank"][6], T["bank"][7]]
        OUT = [T["bank"][4], T["bank"][5]]
        per = (7 if attr else 6) if gated else 11
        with nc.Block() as block:
            @block.sync
            def _(sp):
                sp.dma_start(w[:, :, :], w_dram.rearrange("(q k) m -> k q m", k=KC)).then_inc(s["w_loaded"], 16)
                sp.dma_start(rs[:, :], scale_dram.rearrange("(q k) o -> k (q o)", k=KC)).then_inc(s["w_loaded"], 16)
                with sp.Fori(0, S.node_groups) as g:
                    sp.wait_ge(s["in_free"], g)
                    sp.sem_inc(T["past"], 1)
                    for q in range(COPIES):
                        rows = agg[q][0:S.node_rows, :].rearrange("(t p) f -> p t f", p=P)
                        sp.dma_start(part[q][:, :, :], rows[:, bass.ds(g * NB, NB), :]).then_inc(s["in_loaded"], 16)

            @block.vector
            def _(dve):
                dve.wait_ge(s["w_loaded"], 32)
                for q in range(4):
                    nc.vector.tensor_scalar(w[:, q, :], w[:, q, :], rs[:, q:q + 1], None, ALU.mult).then_inc(s["w_scaled"], 1)
                with dve.Fori(0, S.node_groups) as g:
                    c = Chain(dve, s["dve_step"], per, g)
                    dve.wait_ge(s["in_loaded"], 64 * g + 64)
                    c.link(nc.vector.tensor_tensor(part[0][:, :, :], part[0][:, :, :], part[1][:, :, :], ALU.add))
                    c.link(nc.vector.tensor_tensor(part[2][:, :, :], part[2][:, :, :], part[3][:, :, :], ALU.add))
                    c.link(nc.vector.tensor_tensor(total[:, :, :], part[0][:, :, :], part[2][:, :, :], ALU.add))
                    dve.sem_inc(s["in_free"], 1)
                    if not gated:
                        c.link(nc.vector.tensor_scalar(sg[:, :, 0:1], total[:, :, X0:X0 + 1], 1.0, None, ALU.max))
                        c.link(nc.vector.reciprocal(sg[:, :, 1:2], sg[:, :, 0:1]))
                        c.link(nc.vector.tensor_tensor(total[:, :, :], total[:, :, :], sg[:, :, 1:2].to_broadcast([P, NB, msg_w]), ALU.mult))
                    dve.sem_inc(s["sum_ready"], 1)
                    for t in range(NB):
                        dve.wait_ge(s["out_ready"], g * NB + t + 1)
                        nc.vector.tensor_copy(o[:, t, :], OUT[t % 2][:, 0:M]).then_inc(s["out_copied"], 1)
                    dve.wait_ge(s["out_copied"], g * NB + NB)
                    x = T["x"][:, bass.ds(g * NB, NB), :]
                    if attr:
                        a = T["a"][:, bass.ds(g * NB, NB)].unsqueeze(2).to_broadcast([P, NB, M])
                        c.link(nc.vector.tensor_tensor(o[:, :, :], o[:, :, :], a, ALU.mult))
                    if gated:
                        sk = skip[:, bass.ds(g * NB, NB), :]
                        nc.vector.tensor_tensor(o[:, :, :], o[:, :, :], sk, ALU.add).then_inc(s["pre_ready"], 1)
                        dve.wait_ge(s["sig_ready"], g + 1)
                        c.link(nc.vector.tensor_tensor(o[:, :, 0:NS], o[:, :, 0:NS], sg[:, :, 0:NS], ALU.mult))
                        for t in range(NB):
                            nc.vector.tensor_tensor(o[:, t, 96:192].rearrange("p (c k) -> p c k", k=3), o[:, t, 96:192].rearrange("p (c k) -> p c k", k=3),
                                                    sg[:, t, NS:96].unsqueeze(2).to_broadcast([P, NV, 3]), ALU.mult)
                        c.link(nc.vector.tensor_tensor(x[:, :, 0:NS], x[:, :, 0:NS], o[:, :, 0:NS], ALU.add))
                        c.link(nc.vector.tensor_tensor(x[:, :, NS:FEAT], x[:, :, NS:FEAT], o[:, :, 96:192], ALU.add))
                    else:
                        sk = skip[:, bass.ds(g * NB, NB), :]
                        c.link(nc.vector.tensor_copy(sg[:, :, 3:4], o[:, :, FEAT:FEAT + 1]))
                        c.link(nc.vector.tensor_tensor(o[:, :, 0:FEAT], o[:, :, 0:FEAT], sg[:, :, 3:4].to_broadcast([P, NB, FEAT]), ALU.mult))
                        c.link(nc.vector.tensor_tensor(o[:, :, 0:FEAT], o[:, :, 0:FEAT], sk[:, :, 0:FEAT], ALU.add))
                        c.link(nc.vector.tensor_tensor(x, x, o[:, :, 0:FEAT], ALU.add))
                    c.end()

            @block.scalar
            def _(act):
                with act.Fori(0, S.node_groups) as g:
                    for t in range(NB):
                        act.wait_ge(s["tr_ready"], g * NB + t + 1)
                        if t >= 2:
                            act.wait_ge(s["out_ready"], g * NB + t - 1)
                        else:
                            act.wait_ge(s["out_ready"], g * NB)
                        nc.scalar.activation(mT[t % 2][:, :, :], TR[t % 2][0:KC, :].rearrange("p (q n) -> p q n", n=P), ACT.Copy).then_inc(s["tr_copied"], 1)
                    if gated:
                        act.wait_ge(s["pre_ready"], g + 1)
                        nc.scalar.activation(sg[:, :, :], o[:, :, 0:96], ACT.Sigmoid).then_inc(s["sig_ready"], 1)

            @block.tensor
            def _(pe):
                pe.wait_ge(s["w_scaled"], 4)

                def transpose(g, t):
                    pe.wait_ge(s["tr_copied"], g * NB + max(t - 1, 0))
                    for q in range(4):
                        ins = nc.tensor.transpose(TR[t % 2][0:KC, q * P:(q + 1) * P], total[:, t, q * KC:(q + 1) * KC], T["ident"][:, :])
                    ins.then_inc(s["tr_ready"], 1)
                with pe.Fori(0, S.node_groups) as g:
                    pe.wait_ge(s["sum_ready"], g + 1)
                    transpose(g, 0)
                    for t in range(NB):
                        if t + 1 < NB:
                            transpose(g, t + 1)
                        pe.wait_ge(s["out_copied"], g * NB + max(t - 1, 0))
                        ot = OUT[t % 2]
                        pe.wait_ge(s["tr_copied"], g * NB + t + 1)
                        for q in range(4):
                            ins = nc.tensor.matmul(ot[:, 0:M], mT[t % 2][:, q, :], w[:, q, :], start=(q == 0), stop=(q == 3))
                        ins.then_inc(s["out_ready"], 1)


def inverse_root(nc, c, y, v, t, between=()):
    between = iter(between)

    def link(instruction):
        wait = c.mark(instruction)
        next(between, None)
        wait()
    yi = y[:, :].bitcast(I32)
    link(nc.vector.tensor_scalar(yi, v[:, :].bitcast(I32), 1, None, ALU.logical_shift_right))
    link(nc.vector.tensor_scalar(yi, yi, -1.0, float(0x5F3759DF), ALU.mult, ALU.add))
    for _ in range(3):
        link(nc.vector.tensor_tensor(t[:, :], y[:, :], y[:, :], ALU.mult))
        link(nc.vector.scalar_tensor_tensor(t[:, :], t[:, :], -0.5, v[:, :], ALU.mult, ALU.mult))
        link(nc.vector.scalar_tensor_tensor(y[:, :], t[:, :], 1.5, y[:, :], ALU.add, ALU.mult))


R_ = 2 * NS + NV + 3 * NV + 3 * NV
WIDE = NS + 5 * NV
HEADS, HD = 8, 8
MSG2 = FEAT + HEADS
BIG = 1.6e38


def message_phase(nc, T, D, S, table_s, table_d, direction5, values, scores):
    H = 64
    names = ["w_loaded", "centred", "in_free0", "in_free1", "in_loaded0", "in_loaded1", "at_loaded0", "at_loaded1", "h_ready", "square_ready",
             "norm_ready", "tr_ready", "hid_done", "w_ready", "dve_step", "r_ready", "rt_ready", "rt_copied", "u_ready",
             "u_copied", "v_ready", "stored0", "stored1", "ones_ready", "turned_loaded0", "turned_loaded1"]
    with phase(nc, names) as s, ExitStack() as st:
        def sb(n, sh, dt=F32):
            return st.enter_context(nc.sbuf_tensor(f"msg_{n}", sh, dt))
        in_free = [s["in_free0"], s["in_free1"]]
        in_loaded = [s["in_loaded0"], s["in_loaded1"]]
        at_loaded = [s["at_loaded0"], s["at_loaded1"]]
        turned_loaded = [s["turned_loaded0"], s["turned_loaded1"]]
        gathered, fetched = T["gathered"], T["gathered_count"]
        stored = [s["stored0"], s["stored1"]]
        w1, w2, w3 = sb("w1", [H + 1, H]), sb("w2", [H + 1, H]), sb("w3", [H + 1, 224])
        wm = sb("wm", [H + 1, 2])
        gb = sb("gb", [H, 4])
        wl = sb("wl", [P, 3, 256])
        ls = sb("ls", [P, 3])
        dots = sb("dots", [P, H])
        at = [sb(f"at{b}", [H + 1, GE]) for b in range(2)]
        mi = [sb(f"mi{b}", [P, 3 * TG], I32) for b in range(2)]
        y5 = [sb(f"y5{b}", [P, TG, 5]) for b in range(2)]
        turned = [sb(f"turned{b}", [P, TG, 5]) for b in range(2)]
        Gs = [sb(f"Gs{b}", [P, TG, WIDE]) for b in range(2)]
        Gd = [sb(f"Gd{b}", [P, TG, WIDE]) for b in range(2)]
        m = [sb(f"m{b}", [P, TG, WIDE]) for b in range(2)]
        dc = [sb(f"dc{b}", [P, TG, 4 * NV]) for b in range(2)]
        xn = sb("xn", [P, 2 * TG, H])
        sq = sb("sq", [P, 2 * TG, H])
        rstd, rad, tmp = sb("rstd", [P, 2 * TG]), sb("rad", [P, 2 * TG]), sb("tmp", [P, 2 * TG])
        hT = [sb(f"hT{q}", [H + 1, GE]) for q in range(3)]
        t1, t2, t3 = sb("t1", [P, TG, 3 * NV]), sb("t2", [P, TG, 3 * NV]), sb("t3", [P, TG, 3 * NV])
        R = [sb(f"R{q}", [P, R_]) for q in range(2)]
        RT = [sb(f"RT{q}", [P, 3 * P]) for q in range(2)]
        th = [sb(f"th{b}", [P, TG, H]) for b in range(2)]
        U = [sb(f"U{b}", [P, TG, 256]) for b in range(2)]
        sm = sb("sm", [P, TG, H])
        HB, TB = T["bank"][0], T["bank"][1]
        WB = [T["bank"][2], T["bank"][3]]
        RB = [T["bank"][4], T["bank"][5]]
        UB = [T["bank"][6], T["bank"][7]]
        loads = 9
        parts = [(P, 0, 256), (P, 32, 256), (R_ - 2 * P + 1, 32, 256)]
        per = 2 * (13 + 7 + 5)
        last = S.pairs - 1

        def halves(following, after):
            return (0 if following else TG), (2 * TG if after else TG)

        def tile(i, b, t):
            return (i * 2 + b) * TG + t

        def loop_body(step, k):
            step(k, 1, (k + 1, 0), (k + 1, 1), k)
            step(k + 1, 0, (k + 1, 1), (k + 2, 0), k)

        def after_loop(step):
            step(last - 1, 1, (last, 0), (last, 1), last - 1)
            step(last, 0, (last, 1), None, last - 1)
            step(last, 1, None, None, last)

        def periods(step, engine):
            step(0, 0, (0, 1), (1, 0), None)
            with engine.Fori(0, last - 1) as k:
                loop_body(step, k)
            after_loop(step)

        with nc.Block() as block:
            @block.sync
            def _(sp):
                def load(i, b):
                    g = i * 2 + b
                    sp.dma_start(mi[b][:, :], D["by_dst"][bass.ds(g * P, P), :]).then_inc(in_loaded[b], 16)
                    sp.dma_start(y5[b][:, :, :], direction5[bass.ds(g * P, P), :].rearrange("p (t k) -> p t k", k=5)).then_inc(in_loaded[b], 16)
                def load_scalars(i, b):
                    sp.dma_start(at[b][:, :], D["attr64"][:, bass.ds((i * 2 + b) * GE, GE)]).then_inc(at_loaded[b], 16)
                for dst, src in ((w1, D["L2_rw1"]), (w2, D["L2_rw2"]), (w3, D["L2_rw3"]), (gb, D["L2_gb"]), (ls, D["L2_lin_scale"])):
                    sp.dma_start(dst[:, :], src).then_inc(s["w_loaded"], 16)
                for q in range(3):
                    k = parts[q][0]
                    sp.dma_start(wl[0:k, q, :], D["L2_lin"][q * P:q * P + k, :]).then_inc(s["w_loaded"], 16)
                sp.dma_start(dots[:, :], D["L2_dots"].partition_broadcast(P)).then_inc(s["w_loaded"], 16)
                for b in range(2):
                    load_scalars(0, b)
                    load(0, b)
                with sp.Fori(1, S.pairs) as i:
                    for b in range(2):
                        sp.wait_ge(s["h_ready"], 2 * i + b - 1)
                        sp.sem_inc(T["past"], 1)
                        load_scalars(i, b)
                        sp.wait_ge(in_free[b], i)
                        sp.sem_inc(T["past"], 1)
                        load(i, b)

            @block.gpsimd
            def _(pool):
                with pool.Fori(0, S.pairs) as i:
                    for b in range(2):
                        pool.wait_ge(in_loaded[b], 32 * i + 32)
                        pool.sem_inc(T["past"], 1)
                        for t in range(TG):
                            pool.indirect_dma_start(Gs[b][:, t, :], None, table_s, bass.IndirectOffsetOnAxis(mi[b][:, t:t + 1], 0)).then_inc(gathered[b], 16)
                            pool.indirect_dma_start(Gd[b][:, t, :], None, table_d, bass.IndirectOffsetOnAxis(mi[b][:, TG + t:TG + t + 1], 0)).then_inc(gathered[b], 16)

            @block.vector
            def _(dve):
                dve.wait_ge(s["w_loaded"], 16 * loads)
                for n, w in enumerate((w1, w2)):
                    nc.vector.reduce_sum(wm[:, n:n + 1], w[:, :], AX.X).then_inc(s["centred"], 1)
                dve.wait_ge(s["centred"], 2)
                nc.vector.tensor_scalar(wm[:, :], wm[:, :], 1.0 / H, None, ALU.mult).then_inc(s["centred"], 1)
                dve.wait_ge(s["centred"], 3)
                for n, w in enumerate((w1, w2)):
                    nc.vector.tensor_scalar(w[:, :], w[:, :], wm[:, n:n + 1], None, ALU.subtract).then_inc(s["centred"], 1)
                for q in range(3):
                    k = parts[q][0]
                    nc.vector.tensor_scalar(wl[0:k, q, :], wl[0:k, q, :], ls[0:k, q:q + 1], None, ALU.mult).then_inc(s["centred"], 1)
                for q in range(3):
                    nc.vector.memset(hT[q][H:H + 1, :], 1.0).then_inc(s["ones_ready"], 1)
                for q in range(2):
                    nc.vector.memset(RT[q][96:97, 2 * P:3 * P], 1.0).then_inc(s["ones_ready"], 1)

                def three(x):
                    return x.rearrange("p t (k c) -> p t k c", c=NV)

                def norm(c, j, following, after, between=()):
                    lo, hi = halves(following, after)
                    dve.wait_ge(s["square_ready"], j + 1)
                    c.link(nc.vector.reduce_sum(rstd[:, lo:hi], sq[:, lo:hi, :], AX.X))
                    c.link(nc.vector.tensor_scalar(rad[:, lo:hi], rstd[:, lo:hi], 1.0 / H, EPS, ALU.mult, ALU.add))
                    inverse_root(nc, c, rstd[:, lo:hi], rad[:, lo:hi], tmp[:, lo:hi], between)
                    nc.vector.tensor_tensor(xn[:, lo:hi, :], HB[:, lo * H:hi * H].rearrange("p (t h) -> p t h", h=H),
                                            rstd[:, lo:hi].unsqueeze(2).to_broadcast([P, hi - lo, H]), ALU.mult).then_inc(s["norm_ready"], 1)

                def geometry(c, i, b, products=None):
                    def yb(k):
                        return y5[b][:, :, k:k + 3].unsqueeze(3).to_broadcast([P, TG, 3, NV])
                    dve.wait_ge(in_loaded[b], 32 * i + 32)
                    dve.wait_ge(gathered[b], fetched + 32 * TG * i + 32 * TG)
                    if products is not None:
                        dve.wait_ge(s["r_ready"], products)
                    done = c.mark(nc.vector.tensor_tensor(m[b][:, :, :], Gs[b][:, :, :], Gd[b][:, :, :], ALU.add))
                    v = m[b][:, :, NS:WIDE]
                    yield
                    done()
                    first = c.mark(nc.vector.tensor_tensor(three(t1[:, :, :]), three(v[:, :, 0:96]), yb(0), ALU.mult))
                    yield
                    turned_v = c.mark(nc.vector.tensor_tensor(three(t2[:, :, :]), three(v[:, :, 2 * NV:5 * NV]), yb(1), ALU.mult))
                    yield
                    first()
                    done = c.mark(nc.vector.tensor_tensor(t3[:, :, 0:NV], t1[:, :, 0:NV], t1[:, :, NV:2 * NV], ALU.add))
                    yield
                    done()
                    done = c.mark(nc.vector.tensor_tensor(dc[b][:, :, 0:NV], t3[:, :, 0:NV], t1[:, :, 2 * NV:3 * NV], ALU.add))
                    yield
                    done()
                    done = c.mark(nc.vector.tensor_tensor(three(t1[:, :, :]), three(v[:, :, NV:4 * NV]), yb(2), ALU.mult))
                    yield
                    turned_v()
                    done()
                    c.link(nc.vector.tensor_tensor(dc[b][:, :, NV:4 * NV], t1[:, :, :], t2[:, :, :], ALU.subtract))
                    dve.sem_inc(in_free[b], 1)

                def whole(steps):
                    for _ in steps:
                        pass

                def product(i, b, t):
                    q = t % 2
                    dve.wait_ge(s["w_ready"], tile(i, b, t) + 1)
                    dve.wait_ge(s["rt_ready"], tile(i, b, max(t - 1, 0)))
                    w = WB[q]
                    yield
                    nc.vector.tensor_tensor(R[q][:, 0:2 * NS].rearrange("p (m c) -> p m c", c=NS), w[:, 0:2 * NS].rearrange("p (m c) -> p m c", c=NS),
                                            m[b][:, t, 0:NS].unsqueeze(1).to_broadcast([P, 2, NS]), ALU.mult)
                    yield
                    nc.vector.tensor_tensor(R[q][:, 128:160], w[:, 128:160], dc[b][:, t, 0:NV], ALU.mult)
                    yield
                    nc.vector.tensor_tensor(R[q][:, 160:256].rearrange("p (k c) -> p k c", c=NV), w[:, 160:192].unsqueeze(1).to_broadcast([P, 3, NV]),
                                            dc[b][:, t, NV:4 * NV].rearrange("p (k c) -> p k c", c=NV), ALU.mult)
                    yield
                    nc.vector.tensor_tensor(R[q][:, 256:352].rearrange("p (k c) -> p k c", c=NV), w[:, 192:224].unsqueeze(1).to_broadcast([P, 3, NV]),
                                            m[b][:, t, NS:FEAT].rearrange("p (k c) -> p k c", c=NV), ALU.mult).then_inc(s["r_ready"], 1)

                def finish(c, i, b):
                    dve.wait_ge(s["u_copied"], tile(i, b, TG))
                    dve.wait_ge(turned_loaded[b], 16 * i + 16)
                    done = c.mark(nc.vector.tensor_scalar(th[b][:, :, :], th[b][:, :, :], 0.4, 0.6, ALU.mult, ALU.add))
                    yield
                    turned_u = c.mark(nc.vector.tensor_tensor(three(t3[:, :, :]), U[b][:, :, 0:NV].unsqueeze(2).to_broadcast([P, TG, 3, NV]),
                                                              turned[b][:, :, 0:3].unsqueeze(3).to_broadcast([P, TG, 3, NV]), ALU.mult))
                    yield
                    done()
                    done = c.mark(nc.vector.tensor_tensor(th[b][:, :, :], th[b][:, :, :], dots[:, :].unsqueeze(1).to_broadcast([P, TG, H]), ALU.mult))
                    yield
                    done()
                    done = c.mark(nc.vector.tensor_tensor(sm[:, :, :], th[b][:, :, :], U[b][:, :, 32:96], ALU.mult))
                    yield
                    done()
                    done = c.mark(nc.vector.reduce_sum(scores[:, :, bass.ds((i * 2 + b) * TG, TG)].rearrange("p h t -> p t h"),
                                                       sm[:, :, :].rearrange("p t (h k) -> p t h k", k=HD), AX.X))
                    yield
                    turned_u()
                    done()
                    nc.vector.tensor_tensor(U[b][:, :, 160:256], U[b][:, :, 160:256], t3[:, :, :], ALU.add).then_inc(s["v_ready"], 1)

                def step(i, b, following, after, k):
                    c = links[0]
                    whole(product(i, b, 0))
                    whole(product(i, b, 1))
                    between = product(i, b, 2)
                    if following:
                        norm(c, i * 2 + b + 2, following, after, between)
                    whole(between)
                    if k is not None:
                        whole(finish(c, *((k, 0) if b else (k, 1))))
                    whole(product(i, b, 3))
                    if following:
                        whole(geometry(c, *following, tile(i, b, 0)))
                head = Chain(dve, s["dve_step"])
                norm(head, 0, None, (0, 0))
                whole(geometry(head, 0, 0))
                norm(head, 1, (0, 0), (0, 1))
                links = [head]
                step(0, 0, (0, 1), (1, 0), None)
                start = head.n
                with dve.Fori(0, last - 1) as k:
                    c = Chain(dve, s["dve_step"], per, k)
                    c.n = start
                    links = [c]
                    loop_body(step, k)
                    assert c.n == start + per
                c = Chain(dve, s["dve_step"], per, last - 1)
                c.n = start
                links = [c]
                after_loop(step)
                whole(finish(c, last, 1))

            @block.scalar
            def _(act):
                def turn(i, b):
                    act.dma_start(turned[b][:, :, :], direction5[bass.ds((i * 2 + b) * P, P), :].rearrange("p (t k) -> p t k", k=5)).then_inc(turned_loaded[b], 16)

                def square(j, following, after):
                    lo, hi = halves(following, after)
                    act.wait_ge(s["h_ready"], j + 1)
                    nc.scalar.activation(sq[:, lo:hi, :], HB[:, lo * H:hi * H].rearrange("p (t h) -> p t h", h=H), ACT.Square).then_inc(s["square_ready"], 1)

                def hidden(i, b, n):
                    act.wait_ge(s["tr_ready"], 2 * (i * 2 + b) + n + 1)
                    nc.scalar.activation(hT[n + n * b][0:H, :], TB[0:H, :], ACT.Silu, scale=gb[:, 2 * n:2 * n + 1], bias=gb[:, 2 * n + 1:2 * n + 2]).then_inc(s["hid_done"], 1)

                def turned_out(i, b, t):
                    q = t % 2
                    act.wait_ge(s["rt_ready"], tile(i, b, t) + 1)
                    act.wait_ge(s["u_ready"], tile(i, b, max(t - 1, 0)))
                    nc.scalar.activation(RT[q][:, 0:2 * P], RB[q][:, 0:2 * P], ACT.Copy)
                    nc.scalar.activation(RT[q][0:96, 2 * P:3 * P], RB[q][0:96, 2 * P:3 * P], ACT.Copy).then_inc(s["rt_copied"], 1)

                def results(i, b, t):
                    q = t % 2
                    act.wait_ge(s["u_ready"], tile(i, b, t) + 1)
                    if t == 0:
                        act.wait_ge(stored[b], 16 * i)
                    nc.scalar.activation(th[b][:, t, :], UB[q][:, 32:96], ACT.Tanh, scale=0.5)
                    nc.scalar.activation(U[b][:, t, :], UB[q][:, 0:256], ACT.Copy).then_inc(s["u_copied"], 1)

                def store(i, b):
                    g = i * 2 + b
                    act.wait_ge(s["v_ready"], g + 1)
                    act.dma_start(values[bass.ds(g * P, P), :].rearrange("p (t f) -> p t f", f=FEAT), U[b][:, :, 96:256]).then_inc(stored[b], 16)

                def step(i, b, following, after, k):
                    if following:
                        square(i * 2 + b + 2, following, after)
                    turned_out(i, b, 0)
                    turned_out(i, b, 1)
                    results(i, b, 0)
                    if following:
                        hidden(*following, 1)
                    turned_out(i, b, 2)
                    results(i, b, 1)
                    if k is not None:
                        store(*((k, 0) if b else (k, 1)))
                        if following:
                            turn(*following)
                    if after:
                        hidden(*after, 0)
                    turned_out(i, b, 3)
                    results(i, b, 2)
                    results(i, b, 3)
                act.wait_ge(s["w_loaded"], 16 * loads)
                act.wait_ge(s["ones_ready"], 5)
                turn(0, 0)
                turn(0, 1)
                square(0, None, (0, 0))
                hidden(0, 0, 0)
                square(1, (0, 0), (0, 1))
                hidden(0, 0, 1)
                hidden(0, 1, 0)
                periods(step, act)
                store(last, 1)
                for b in range(2):
                    act.wait_ge(stored[b], 16 * S.pairs)

            @block.tensor
            def _(pe):
                def layer(j, following, after):
                    pe.wait_ge(s["norm_ready"], j)
                    lo, hi = halves(following, after)
                    if following:
                        pe.wait_ge(s["hid_done"], 2 * (j - 1) + 1)
                    if after:
                        pe.wait_ge(at_loaded[after[1]], 16 * after[0] + 16)
                    for t in range(lo, hi):
                        x, w = (hT[0], w2) if t < TG else (at[after[1]], w1)
                        ins = nc.tensor.matmul(HB[:, t * H:(t + 1) * H], x[:, t % TG * P:(t % TG + 1) * P], w[:, :], start=(t == lo), stop=(t == hi - 1))
                    ins.then_inc(s["h_ready"], 1)

                def turn(i, b, n):
                    g = i * 2 + b
                    pe.wait_ge(s["norm_ready"], g + n + 1)
                    pe.wait_ge(s["hid_done"], 2 * g + n)
                    pe.sem_inc(T["past"], 1)
                    for t in range(TG):
                        ins = nc.tensor.transpose(TB[0:H, t * P:(t + 1) * P], xn[:, (1 - n) * TG + t, :], T["ident"][:, :])
                    ins.then_inc(s["tr_ready"], 1)

                def weights(i, b, t):
                    if t == 0:
                        pe.wait_ge(s["hid_done"], 2 * (i * 2 + b) + 2)
                    nc.tensor.matmul(WB[t % 2][:, 0:224], hT[1 + b][:, t * P:(t + 1) * P], w3[:, :], start=True, stop=True).then_inc(s["w_ready"], 1)

                def transpose(i, b, t):
                    q = t % 2
                    pe.wait_ge(s["r_ready"], tile(i, b, t) + 1)
                    pe.wait_ge(s["rt_copied"], tile(i, b, max(t - 1, 0)))
                    for k in range(3):
                        n = min(P, R_ - k * P)
                        ins = nc.tensor.transpose(RB[q][0:n, k * P:(k + 1) * P], R[q][:, k * P:k * P + n], T["ident"][:, :])
                    ins.then_inc(s["rt_ready"], 1)
                    if t + 2 < TG:
                        weights(i, b, t + 2)

                def linear(i, b, t):
                    q = t % 2
                    pe.wait_ge(s["rt_copied"], tile(i, b, t) + 1)
                    pe.wait_ge(s["u_copied"], tile(i, b, max(t - 1, 0)))
                    for k, (n, lo, hi) in enumerate(parts):
                        ins = nc.tensor.matmul(UB[q][:, lo:hi], RT[q][0:n, k * P:(k + 1) * P], wl[0:n, k, lo:hi], start=(k == 0), stop=(k == 2))
                    ins.then_inc(s["u_ready"], 1)

                def step(i, b, following, after, k):
                    if following:
                        layer(i * 2 + b + 2, following, after)
                    transpose(i, b, 0)
                    transpose(i, b, 1)
                    linear(i, b, 0)
                    if following:
                        turn(*following, 1)
                    transpose(i, b, 2)
                    linear(i, b, 1)
                    if after:
                        turn(*after, 0)
                    transpose(i, b, 3)
                    linear(i, b, 2)
                    if following:
                        weights(*following, 0)
                        weights(*following, 1)
                    linear(i, b, 3)
                pe.wait_ge(s["w_loaded"], 16 * loads)
                pe.wait_ge(s["centred"], 8)
                pe.wait_ge(s["ones_ready"], 5)
                layer(0, None, (0, 0))
                turn(0, 0, 0)
                layer(1, (0, 0), (0, 1))
                turn(0, 0, 1)
                turn(0, 1, 0)
                for t in range(2):
                    weights(0, 0, t)
                periods(step, pe)
        T["gathered_count"] += 32 * TG * S.pairs


def softmax_phase(nc, T, D, S, scores, by_head, corner, carry_d):
    chunks = P // HEADS
    n = S.edge_rows // chunks
    blk = S.pairs
    assert blk <= P and blk * 8 == S.tiles and n * chunks == S.edge_rows
    names = ["tr_ready", "tr_copied", "out0", "out1", "loaded", "dve_step", "exp_ready", "stored", "in0", "in1", "back_ready", "back_copied"]
    with phase(nc, names) as s, ExitStack() as st:
        def sb(nm, sh, dt=F32):
            return st.enter_context(nc.sbuf_tensor(f"soft_{nm}", sh, dt))
        keys = sb("keys", [P, n + 2], I32)
        a, pen, f = sb("a", [P, n]), sb("pen", [P, n]), sb("f", [P, n])
        em = sb("em", [P, 4])
        eh = sb("eh", [HEADS, chunks, 2])
        ch = sb("ch", [HEADS, chunks + 2])
        ini = sb("ini", [P, 1])
        back = [sb(f"back{q}", [P, 8, P]) for q in range(2)]
        BK = T["bank"]
        with nc.Block() as block:
            @block.sync
            def _(sp):
                for h in range(HEADS):
                    src = bass.AP(D["dst_wide"].tensor, 0, [[n, chunks], [1, n + 2]])
                    sp.dma_start(keys[h * chunks:(h + 1) * chunks, :], src).then_inc(s["loaded"], 16)
                for h in range(HEADS):
                    sp.wait_ge(s["tr_copied"], 2 * h + 2)
                    dst = by_head[h:h + 1, :].rearrange("o (k r e) -> (o r) k e", r=blk, e=P)
                    sp.dma_start(dst, back[h % 2][0:blk, :, :]).then_inc(s[f"out{h % 2}"], 16)
                sp.wait_ge(s["out0"], 16 * 4)
                sp.wait_ge(s["out1"], 16 * 4)
                sp.dma_start(a[:, :], by_head.rearrange("h (c n) -> (h c) n", n=n)).then_inc(s["loaded"], 16)
                for d in range(2):
                    sp.wait_ge(s["dve_step"], 5 + 9 * d)
                    sp.dma_start(corner, em[:, 2 * d:2 * d + 2]).then_inc(s["stored"], 16)
                    sp.wait_ge(s["stored"], 16 + 32 * d)
                    sp.dma_start(eh[:, :, :], corner.rearrange("(h c) k -> h c k", h=HEADS)).then_inc(s["loaded"], 16)
                    sp.wait_ge(s["dve_step"], 7 + 9 * d)
                    o = 0 if d == 0 else 2
                    sp.dma_start(carry_d, ch[:, o:o + chunks]).then_inc(s["stored"], 16)
                    sp.wait_ge(s["stored"], 32 + 32 * d)
                    sp.dma_start(ini[:, :], carry_d.rearrange("h (c o) -> (h c) o", o=1)).then_inc(s["loaded"], 16)
                sp.wait_ge(s["exp_ready"], 1)
                sp.dma_start(by_head.rearrange("h (c n) -> (h c) n", n=n), a[:, :]).then_inc(s["stored"], 16)
                sp.wait_ge(s["stored"], 80)
                for h in range(HEADS):
                    if h >= 2:
                        sp.wait_ge(s["back_ready"], h - 1)
                    src = by_head[h:h + 1, :].rearrange("o (k r e) -> (o r) k e", r=blk, e=P)
                    sp.dma_start(back[h % 2][0:blk, :, :], src).then_inc(s[f"in{h % 2}"], 16)

            @block.tensor
            def _(pe):
                for h in range(HEADS):
                    for half in range(2):
                        m = 2 * h + half
                        if m >= 2:
                            pe.wait_ge(s["tr_copied"], m - 1)
                        for k in range(4):
                            kk = 4 * half + k
                            ins = nc.tensor.transpose(BK[m % 2][0:blk, k * P:(k + 1) * P], scores[:, h, kk * blk:(kk + 1) * blk], T["ident"][:, :])
                        ins.then_inc(s["tr_ready"], 1)
                for h in range(HEADS):
                    pe.wait_ge(s[f"in{h % 2}"], 16 * (h // 2 + 1))
                    for half in range(2):
                        m = 2 * h + half
                        if m >= 2:
                            pe.wait_ge(s["back_copied"], m - 1)
                        for k in range(4):
                            kk = 4 * half + k
                            ins = nc.tensor.transpose(BK[2 + m % 2][:, k * P:k * P + blk], back[h % 2][0:blk, kk, :], T["ident"][0:blk, 0:blk])
                        if half == 0:
                            ins.then_inc(s["tr_ready"], 1)
                        else:
                            ins.then_inc(s["back_ready"], 1)

            @block.vector
            def _(dve):
                c = Chain(dve, s["dve_step"])
                dve.wait_ge(s["loaded"], 16 * HEADS + 16)
                c.link(nc.vector.tensor_tensor(pen[:, :], keys[:, 1:n + 1], keys[:, 0:n], ALU.is_equal))
                c.link(nc.vector.tensor_scalar(pen[:, :], pen[:, :], 1.0, BIG, ALU.subtract, ALU.mult))
                c.link(nc.vector.tensor_reduce(em[:, 0:1], pen[:, :], AX.X, ALU.min))
                c.link(nc.vector.tensor_tensor_scan(f[:, :], pen[:, :], a[:, :], -BIG, ALU.add, ALU.max))
                c.link(nc.vector.tensor_copy(em[:, 1:2], f[:, n - 1:n]))
                dve.wait_ge(s["loaded"], 16 * HEADS + 32)
                c.link(nc.vector.memset(ch[:, :], -BIG))
                c.link(nc.vector.tensor_tensor_scan(ch[:, 1:chunks + 1], eh[:, :, 0], eh[:, :, 1], -BIG, ALU.add, ALU.max))
                dve.wait_ge(s["loaded"], 16 * HEADS + 48)
                c.link(nc.vector.tensor_tensor_scan(f[:, :], pen[:, :], a[:, :], ini[:, 0:1], ALU.add, ALU.max))
                c.link(nc.vector.tensor_tensor(pen[:, :], keys[:, 1:n + 1], keys[:, 2:n + 2], ALU.is_equal))
                c.link(nc.vector.tensor_scalar(pen[:, :], pen[:, :], 1.0, BIG, ALU.subtract, ALU.mult))
                c.link(nc.vector.tensor_reduce(em[:, 2:3], pen[:, :], AX.X, ALU.min))
                m = keys[:, 0:n].bitcast(F32)
                c.link(nc.vector.tensor_tensor_scan(m[:, ::-1], pen[:, ::-1], f[:, ::-1], -BIG, ALU.add, ALU.max))
                c.link(nc.vector.tensor_copy(em[:, 3:4], m[:, 0:1]))
                c.link(nc.vector.memset(ch[:, :], -BIG))
                dve.wait_ge(s["loaded"], 16 * HEADS + 64)
                c.link(nc.vector.tensor_tensor_scan(ch[:, chunks:0:-1], eh[:, ::-1, 0], eh[:, ::-1, 1], -BIG, ALU.add, ALU.max))
                c.link(nc.vector.tensor_copy(em[:, 0:1], em[:, 1:2]))
                dve.wait_ge(s["loaded"], 16 * HEADS + 80)
                c.link(nc.vector.tensor_tensor_scan(m[:, ::-1], pen[:, ::-1], f[:, ::-1], ini[:, 0:1], ALU.add, ALU.max))
                c.link(nc.vector.tensor_tensor(a[:, :], a[:, :], m[:, :], ALU.subtract))

            @block.scalar
            def _(act):
                for m in range(2 * HEADS):
                    h, half = m // 2, m % 2
                    act.wait_ge(s["tr_ready"], m + 1)
                    if half == 0 and h >= 2:
                        act.wait_ge(s[f"out{h % 2}"], 16 * (h // 2))
                    nc.scalar.activation(back[h % 2][0:blk, 4 * half:4 * half + 4, :], BK[m % 2][0:blk, :].rearrange("p (k e) -> p k e", e=P), ACT.Copy).then_inc(s["tr_copied"], 1)
                act.wait_ge(s["dve_step"], 18)
                nc.scalar.activation(a[:, :], a[:, :], ACT.Exp).then_inc(s["exp_ready"], 1)
                for m in range(2 * HEADS):
                    h, half = m // 2, m % 2
                    if half == 0:
                        act.wait_ge(s["tr_ready"], 2 * HEADS + h + 1)
                    else:
                        act.wait_ge(s["back_ready"], h + 1)
                    nc.scalar.activation(scores[:, h, 4 * half * blk:(4 * half + 4) * blk].rearrange("p (k r) -> p k r", r=blk),
                                         BK[2 + m % 2][:, :].rearrange("p (k e) -> p k e", e=P)[:, :, 0:blk], ACT.Copy).then_inc(s["back_copied"], 1)
                act.wait_ge(s["back_copied"], 2 * HEADS)


def attend_phase(nc, T, D, S, values, scores, agg):
    names = ["in_free0", "in_free1", "in_loaded0", "in_loaded1", "all_loaded", "all_step", "dve_step", "s_ready", "p_ready", "agg_ready", "msg_ready", "idx_ready"]
    with phase(nc, names) as s, ExitStack() as st:
        def sb(n, sh, dt=F32):
            return st.enter_context(nc.sbuf_tensor(f"att_{n}", sh, dt))
        in_free = [s["in_free0"], s["in_free1"]]
        in_loaded = [s["in_loaded0"], s["in_loaded1"]]
        added, summed = T["added"], T["added_count"]
        row = [sb(f"row{b}", [P, GE], I32) for b in range(2)]
        every = [sb(n, [P, S.tiles + 2 * TG], I32) for n in ("keys", "before")]
        keyf, spare = sb("keyf", [P, S.tiles]), sb("spare", [P, S.tiles])
        V = [sb(f"V{b}", [P, TG, FEAT]) for b in range(2)]
        idx = [sb(f"idx{b}", [P, TG], I32) for b in range(2)]
        Sk = [sb(f"S{b}", [P, TG, P]) for b in range(2)]
        prod = [sb(f"prod{b}", [P, TG, MSG2]) for b in range(2)]
        msg = [sb(f"msg{t}", [P, MSG2]) for t in range(TG)]
        AGG = [T["bank"][4], T["bank"][5]]
        steps = 1
        last = S.pairs - 1
        with nc.Block() as block:
            @block.sync
            def _(sp):
                for n, columns in enumerate(every):
                    sp.dma_start(columns[:, :], (D["dst_all"], D["dst_before"])[n]).then_inc(s["all_loaded"], 16)
                with sp.Fori(0, S.pairs) as i:
                    for b in range(2):
                        g = i * 2 + b
                        sp.wait_ge(in_free[b], i)
                        sp.sem_inc(T["past"], 1)
                        sp.dma_start(V[b][:, :, :], values[bass.ds(g * P, P), :].rearrange("p (t f) -> p t f", f=FEAT)).then_inc(in_loaded[b], 16)
                        sp.dma_start(row[b][:, :], D["dst_row"][:, bass.ds(g * GE, GE)].partition_broadcast(P)).then_inc(in_loaded[b], 16)

            @block.gpsimd
            def _(pool):
                with pool.Fori(0, S.pairs) as i:
                    for b in range(2):
                        g = i * 2 + b
                        pool.wait_ge(s["idx_ready"], g + 1)
                        for t in range(TG):
                            pool.wait_ge(s["msg_ready"], g * TG + t + 1)
                            pool.wait_ge(added[t], summed + 16 * g)
                            pool.sem_inc(T["past"], 1)
                            pool.indirect_dma_start(agg[t], bass.IndirectOffsetOnAxis(idx[b][:, t:t + 1], 0), msg[t][:, :], None,
                                                    compute_op=ALU.add).then_inc(added[t], 16)
                for t in range(TG):
                    pool.wait_ge(added[t], summed + 16 * S.groups)

            @block.vector
            def _(dve):
                c = Chain(dve, s["all_step"])
                dve.wait_ge(s["all_loaded"], 32)
                rows = S.tiles
                c.link(nc.vector.tensor_copy(keyf[:, :], every[0][:, 0:rows]))
                c.link(nc.vector.tensor_scalar(spare[:, :], keyf[:, :], -1.0, T["spare"][:, 0:1], ALU.mult, ALU.add))
                same = every[1].bitcast(F32)[:, 0:rows]
                c.link(nc.vector.tensor_tensor(same, every[0][:, 0:rows], every[1][:, 0:rows], ALU.is_equal))
                c.link(nc.vector.tensor_tensor(spare[:, :], spare[:, :], same, ALU.mult))
                c.link(nc.vector.tensor_tensor(spare[:, :], spare[:, :], keyf[:, :], ALU.add))
                with dve.Fori(0, S.pairs) as i:
                    c = Chain(dve, s["dve_step"], 2 * steps, i)
                    for b in range(2):
                        g = i * 2 + b
                        dve.wait_ge(in_loaded[b], 32 * i + 32)
                        dve.wait_ge(s["agg_ready"], 2 * TG * i)
                        nc.vector.tensor_tensor(Sk[b][:, :, :], row[b][:, :].rearrange("p (t e) -> p t e", e=P),
                                                every[0][:, bass.ds(g * TG, TG)].unsqueeze(2).to_broadcast([P, TG, P]), ALU.is_equal).then_inc(s["s_ready"], 1)
                        e = scores[:, :, bass.ds(g * TG, TG)]
                        nc.vector.tensor_copy(prod[b][:, :, FEAT:MSG2], e.rearrange("p h t -> p t h"))
                        nc.vector.tensor_tensor(prod[b][:, :, 0:NS].rearrange("p t (h k) -> p t h k", k=HD), V[b][:, :, 0:NS].rearrange("p t (h k) -> p t h k", k=HD),
                                                e.rearrange("p h t -> p t h").unsqueeze(3).to_broadcast([P, TG, HEADS, HD]), ALU.mult)
                        for t in range(TG):
                            et = scores[:, :, bass.ds(g * TG + t, 1)].rearrange("p h o -> p (h o)")
                            nc.vector.tensor_tensor(prod[b][:, t, NS:FEAT].rearrange("p (k h j) -> p k h j", k=3, j=NV // HEADS),
                                                    V[b][:, t, NS:FEAT].rearrange("p (k h j) -> p k h j", k=3, j=NV // HEADS),
                                                    et.unsqueeze(1).unsqueeze(3).to_broadcast([P, 3, HEADS, NV // HEADS]), ALU.mult).then_inc(s["p_ready"], 1)
                        dve.wait_ge(s["msg_ready"], g * TG)
                        c.link(nc.vector.tensor_copy(idx[b][:, :], spare[:, bass.ds(g * TG, TG)]))
                        dve.sem_inc(s["idx_ready"], 1)
                        dve.wait_ge(s["p_ready"], g * TG + TG)
                        dve.sem_inc(in_free[b], 1)
                    c.end()

            @block.scalar
            def _(act):
                with act.Fori(0, S.groups) as g:
                    for t in range(TG):
                        act.wait_ge(s["agg_ready"], g * TG + t + 1)
                        act.wait_ge(added[t], summed + 16 * g)
                        nc.scalar.activation(msg[t][:, :], AGG[t % 2][:, 0:MSG2], ACT.Copy).then_inc(s["msg_ready"], 1)

            @block.tensor
            def _(pe):
                with pe.Fori(0, S.pairs) as i:
                    for b in range(2):
                        g = i * 2 + b
                        for t in range(TG):
                            pe.wait_ge(s["s_ready"], g + 1)
                            pe.wait_ge(s["p_ready"], g * TG + t + 1)
                            pe.wait_ge(s["msg_ready"], g * TG + max(t - 1, 0))
                            nc.tensor.matmul(AGG[t % 2][:, 0:MSG2], Sk[b][:, t, :], prod[b][:, t, :], start=True, stop=True).then_inc(s["agg_ready"], 1)
        T["added_count"] += 16 * S.groups


def transformer_post(nc, T, D, S, agg, h_in):
    stages = [(FEAT, FEAT, "L2_proj"), (FEAT, 384, "L2_f1"), (320, FEAT, "L2_f2")]
    names = ["w_loaded", "in_loaded", "in_free", "dve_step", "in_ready", "tr_ready", "tr_copied", "out_ready", "out_copied",
             "var_ready", "root_ready", "pre_ready", "act_done"]
    with phase(nc, names) as s, ExitStack() as st:
        def sb(n, sh, dt=F32):
            return st.enter_context(nc.sbuf_tensor(f"tp_{n}", sh, dt))
        ws, bs = [], []
        for fi, fo, n in stages:
            ws.append([sb(f"w{n}{q}", [min(P, fi - q * P), fo]) for q in range(-(-fi // P))])
            bs.append(sb(f"b{n}", [P, fo]))
        nw = sum(len(w) for w in ws)
        pr = sb("pr", [P, 2 * FEAT])
        part = [sb(f"part{q}", [P, NB, MSG2]) for q in range(COPIES)]
        X = [sb("X0", [P, NB, FEAT]), sb("X1", [P, NB, FEAT]), sb("X2", [P, NB, 320])]
        O = [sb("O0", [P, NB, FEAT]), sb("O1", [P, NB, 384]), sb("O2", [P, NB, FEAT])]
        xm = sb("xm", [P, NB, FEAT])
        sq = sb("sq", [P, NB, FEAT])
        ev = sb("ev", [P, NB, 8])
        rd = sb("rd", [P, NB, HEADS])
        gate = sb("gate", [P, NB, 192])
        XT = [sb(f"XT{q}", [P, 3 * P]) for q in range(2)]
        TR = [T["bank"][6], T["bank"][7]]
        OUT = [T["bank"][4], T["bank"][5]]
        per = 22
        with nc.Block() as block:
            @block.sync
            def _(sp):
                for (fi, fo, n), w, b in zip(stages, ws, bs):
                    for q, part_w in enumerate(w):
                        k = part_w.shape[0]
                        sp.dma_start(part_w[:, :], D[n][q * P:q * P + k, :]).then_inc(s["w_loaded"], 16)
                    sp.dma_start(b[:, :], D[n + "_b"].partition_broadcast(P)).then_inc(s["w_loaded"], 16)
                sp.dma_start(pr[:, :], D["L2_ln2"].partition_broadcast(P)).then_inc(s["w_loaded"], 16)
                with sp.Fori(0, S.node_groups) as g:
                    sp.wait_ge(s["in_free"], g)
                    sp.sem_inc(T["past"], 1)
                    for q in range(COPIES):
                        rows = agg[q][0:S.node_rows, :].rearrange("(t p) f -> p t f", p=P)
                        sp.dma_start(part[q][:, :, :], rows[:, bass.ds(g * NB, NB), :]).then_inc(s["in_loaded"], 16)

            @block.vector
            def _(dve):
                dve.wait_ge(s["w_loaded"], 16 * (nw + 4))
                with dve.Fori(0, S.node_groups) as g:
                    c = Chain(dve, s["dve_step"], per, g)
                    a0 = T["a"][:, bass.ds(g * NB, NB)]

                    def product(stage):
                        dve.sem_inc(s["in_ready"], 1)
                        for t in range(NB):
                            m = 3 * NB * g + stage * NB + t
                            dve.wait_ge(s["out_ready"], m + 1)
                            fo = stages[stage][1]
                            nc.vector.tensor_tensor(O[stage][:, t, :], OUT[m_parity(stage, t)][:, 0:fo], bs[stage][:, :], ALU.add).then_inc(s["out_copied"], 1)
                        dve.wait_ge(s["out_copied"], 3 * NB * g + stage * NB + NB)

                    dve.wait_ge(s["in_loaded"], 64 * g + 64)
                    c.link(nc.vector.tensor_tensor(part[0][:, :, :], part[0][:, :, :], part[1][:, :, :], ALU.add))
                    c.link(nc.vector.tensor_tensor(part[2][:, :, :], part[2][:, :, :], part[3][:, :, :], ALU.add))
                    c.link(nc.vector.tensor_tensor(part[0][:, :, :], part[0][:, :, :], part[2][:, :, :], ALU.add))
                    c.link(nc.vector.tensor_scalar(rd[:, :, :], part[0][:, :, FEAT:MSG2], 1e-12, None, ALU.add))
                    c.link(nc.vector.reciprocal(rd[:, :, :], rd[:, :, :]))
                    nc.vector.tensor_tensor(X[0][:, :, 0:NS].rearrange("p t (h k) -> p t h k", k=HD), part[0][:, :, 0:NS].rearrange("p t (h k) -> p t h k", k=HD),
                                            rd[:, :, :].unsqueeze(3).to_broadcast([P, NB, HEADS, HD]), ALU.mult)
                    for t in range(NB):
                        ins = nc.vector.tensor_tensor(X[0][:, t, NS:FEAT].rearrange("p (k h j) -> p k h j", k=3, j=NV // HEADS),
                                                      part[0][:, t, NS:FEAT].rearrange("p (k h j) -> p k h j", k=3, j=NV // HEADS),
                                                      rd[:, t, :].unsqueeze(1).unsqueeze(3).to_broadcast([P, 3, HEADS, NV // HEADS]), ALU.mult)
                    c.link(ins)
                    dve.sem_inc(s["in_free"], 1)
                    product(0)
                    c.link(nc.vector.tensor_tensor(xm[:, :, :], O[0][:, :, :], h_in[:, bass.ds(g * NB, NB), 0:FEAT], ALU.add))
                    c.link(nc.vector.reduce_sum(ev[:, :, 0], xm[:, :, 0:NS], AX.X))
                    c.link(nc.vector.tensor_scalar(ev[:, :, 0], ev[:, :, 0], 1.0 / NS, None, ALU.mult))
                    nc.vector.tensor_copy(X[1][:, :, NS:FEAT], xm[:, :, NS:FEAT])
                    c.link(nc.vector.tensor_tensor(X[1][:, :, 0:NS], xm[:, :, 0:NS], ev[:, :, 0:1].to_broadcast([P, NB, NS]), ALU.subtract))
                    c.link(nc.vector.tensor_tensor(sq[:, :, :], X[1][:, :, :], X[1][:, :, :], ALU.mult))
                    c.link(nc.vector.reduce_sum(ev[:, :, 1], sq[:, :, 0:NS], AX.X))
                    c.link(nc.vector.reduce_sum(ev[:, :, 2], sq[:, :, NS:FEAT], AX.X))
                    c.link(nc.vector.tensor_scalar(ev[:, :, 1], ev[:, :, 1], 1.0 / NS, EPS, ALU.mult, ALU.add))
                    nc.vector.tensor_scalar(ev[:, :, 2], ev[:, :, 2], 1.0 / (3 * NV), EPS, ALU.mult, ALU.add).then_inc(s["var_ready"], 1)
                    dve.wait_ge(s["root_ready"], g + 1)
                    c.link(nc.vector.reciprocal(ev[:, :, 5:7], ev[:, :, 3:5]))
                    nc.vector.tensor_tensor(X[1][:, :, 0:NS], X[1][:, :, 0:NS], ev[:, :, 5:6].to_broadcast([P, NB, NS]), ALU.mult)
                    c.link(nc.vector.tensor_tensor(X[1][:, :, NS:FEAT], X[1][:, :, NS:FEAT], ev[:, :, 6:7].to_broadcast([P, NB, 96]), ALU.mult))
                    c.link(nc.vector.tensor_tensor(X[1][:, :, :], X[1][:, :, :], pr[:, 0:FEAT].unsqueeze(1).to_broadcast([P, NB, FEAT]), ALU.mult))
                    c.link(nc.vector.tensor_tensor(X[1][:, :, :], X[1][:, :, :], pr[:, FEAT:2 * FEAT].unsqueeze(1).to_broadcast([P, NB, FEAT]), ALU.add))
                    product(1)
                    nc.vector.tensor_tensor(O[1][:, :, :], O[1][:, :, :], a0.unsqueeze(2).to_broadcast([P, NB, 384]), ALU.mult).then_inc(s["pre_ready"], 1)
                    dve.wait_ge(s["act_done"], g + 1)
                    nc.vector.tensor_tensor(X[2][:, :, 0:P], O[1][:, :, 0:P], gate[:, :, 0:P], ALU.mult)
                    for t in range(NB):
                        ins = nc.vector.tensor_tensor(X[2][:, t, P:320].rearrange("p (k c) -> p k c", k=3), O[1][:, t, 192:384].rearrange("p (k c) -> p k c", k=3),
                                                      gate[:, t, P:192].unsqueeze(1).to_broadcast([P, 3, 64]), ALU.mult)
                    c.link(ins)
                    product(2)
                    c.link(nc.vector.tensor_tensor(O[2][:, :, :], O[2][:, :, :], a0.unsqueeze(2).to_broadcast([P, NB, FEAT]), ALU.mult))
                    c.link(nc.vector.tensor_tensor(O[2][:, :, :], O[2][:, :, :], xm[:, :, :], ALU.add))
                    x = T["x"][:, bass.ds(g * NB, NB), :]
                    c.link(nc.vector.tensor_tensor(x, x, O[2][:, :, :], ALU.add))
                    c.end()

            @block.scalar
            def _(act):
                with act.Fori(0, S.node_groups) as g:
                    for stage, (fi, fo, n) in enumerate(stages):
                        if stage == 1:
                            act.wait_ge(s["var_ready"], g + 1)
                            nc.scalar.activation(ev[:, :, 3:5], ev[:, :, 1:3], ACT.Sqrt).then_inc(s["root_ready"], 1)
                        if stage == 2:
                            act.wait_ge(s["pre_ready"], g + 1)
                            nc.scalar.activation(gate[:, :, :], O[1][:, :, 0:192], ACT.Sigmoid).then_inc(s["act_done"], 1)
                        for t in range(NB):
                            m = 3 * NB * g + stage * NB + t
                            q = m_parity(stage, t)
                            act.wait_ge(s["tr_ready"], m + 1)
                            if stage + t > 1 or t > 1:
                                act.wait_ge(s["out_ready"], m - 1)
                            else:
                                act.wait_ge(s["out_ready"], 3 * NB * g)
                            for k in range(len(ws[stage])):
                                r = ws[stage][k].shape[0]
                                ins = nc.scalar.activation(XT[q][0:r, k * P:(k + 1) * P], TR[q][0:r, k * P:(k + 1) * P], ACT.Copy)
                            ins.then_inc(s["tr_copied"], 1)

            @block.tensor
            def _(pe):
                pe.wait_ge(s["w_loaded"], 16 * (nw + 4))

                def transpose(g, stage, t):
                    q = m_parity(stage, t)
                    pe.wait_ge(s["tr_copied"], 3 * NB * g + max(stage * NB + t - 1, 0))
                    for k, w in enumerate(ws[stage]):
                        r = w.shape[0]
                        ins = nc.tensor.transpose(TR[q][0:r, k * P:(k + 1) * P], X[stage][:, t, k * P:k * P + r], T["ident"][:, :])
                    ins.then_inc(s["tr_ready"], 1)
                with pe.Fori(0, S.node_groups) as g:
                    for stage, (fi, fo, n) in enumerate(stages):
                        pe.wait_ge(s["in_ready"], 3 * g + stage + 1)
                        transpose(g, stage, 0)
                        for t in range(NB):
                            m = 3 * NB * g + stage * NB + t
                            q = m_parity(stage, t)
                            if t + 1 < NB:
                                transpose(g, stage, t + 1)
                            pe.wait_ge(s["out_copied"], 3 * NB * g + max(stage * NB + t - 1, 0))
                            pe.wait_ge(s["tr_copied"], m + 1)
                            for k, w in enumerate(ws[stage]):
                                r = w.shape[0]
                                ins = nc.tensor.matmul(OUT[q][:, 0:fo], XT[q][0:r, k * P:(k + 1) * P], w[:, :], start=(k == 0), stop=(k == len(ws[stage]) - 1))
                            ins.then_inc(s["out_ready"], 1)


def m_parity(stage, t):
    return (stage * NB + t) % 2


def direction_phase(nc, D, S, direction6, direction5):
    n = S.groups * TG
    with phase(nc, ["loaded", "step", "radicand_ready", "root_ready", "stored"]) as s, ExitStack() as st:
        def sb(nm, sh, dt=F32):
            return st.enter_context(nc.sbuf_tensor(f"dir_{nm}", sh, dt))
        v, sq, r = sb("v", [P, n, 3]), sb("sq", [P, n, 3]), sb("r", [P, 2, n])
        y6, y5 = sb("y6", [P, n, 6]), sb("y5", [P, n, 5])
        with nc.Block() as block:
            @block.sync
            def _(sp):
                sp.dma_start(v[:, :, :].rearrange("p (g t) k -> p g (t k)", t=TG), D["attr3"].rearrange("(g p) c -> p g c", p=P)).then_inc(s["loaded"], 16)
                sp.wait_ge(s["step"], 9)
                sp.dma_start(direction6.rearrange("(g p) c -> p g c", p=P), y6[:, :, :].rearrange("p (g t) k -> p g (t k)", t=TG)).then_inc(s["stored"], 16)
                sp.dma_start(direction5.rearrange("(g p) c -> p g c", p=P), y5[:, :, :].rearrange("p (g t) k -> p g (t k)", t=TG)).then_inc(s["stored"], 16)
                sp.wait_ge(s["stored"], 32)

            @block.vector
            def _(dve):
                c = Chain(dve, s["step"])
                dve.wait_ge(s["loaded"], 16)
                c.link(nc.vector.tensor_tensor(sq[:, :, :], v[:, :, :], v[:, :, :], ALU.mult))
                c.link(nc.vector.reduce_sum(r[:, 0, :], sq[:, :, :], AX.X))
                c.link(nc.vector.tensor_scalar(r[:, 0, :], r[:, 0, :], 1.0 / 3.0, None, ALU.mult))
                nc.vector.tensor_scalar(r[:, 1, :], r[:, 0, :], 1e-12 / 3.0, None, ALU.add).then_inc(s["radicand_ready"], 1)
                dve.wait_ge(s["root_ready"], 1)
                c.link(nc.vector.reciprocal(sq[:, :, 0:2], sq[:, :, 0:2]))
                c.link(nc.vector.memset(y6[:, :, 0:1], 1.0))
                c.link(nc.vector.tensor_tensor(y6[:, :, 1:4], v[:, :, :], sq[:, :, 0:1].to_broadcast([P, n, 3]), ALU.mult))
                c.link(nc.vector.tensor_tensor(y5[:, :, 0:3], v[:, :, :], sq[:, :, 1:2].to_broadcast([P, n, 3]), ALU.mult))
                c.link(nc.vector.tensor_copy(y5[:, :, 3:5], y5[:, :, 0:2]))
                c.link(nc.vector.tensor_copy(y6[:, :, 4:6], y6[:, :, 1:3]))

            @block.scalar
            def _(act):
                act.wait_ge(s["radicand_ready"], 1)
                nc.scalar.activation(sq[:, :, 0:2].rearrange("p n k -> p k n"), r[:, :, :], ACT.Sqrt).then_inc(s["root_ready"], 1)


def store_phase(nc, T, S, out):
    full = S.nodes // P
    with phase(nc, ["stored"]) as s:
        with nc.Block() as block:
            @block.sync
            def _(sp):
                sp.dma_start(out[0:full * P, :].rearrange("(t p) f -> p t f", p=P), T["x"][:, 0:full, :]).then_inc(s["stored"], 16)
                rest = S.nodes - full * P
                if rest:
                    sp.dma_start(out[full * P:S.nodes, :], T["x"][0:rest, full, :]).then_inc(s["stored"], 16)
                sp.wait_ge(s["stored"], 32 if rest else 16)


def build(nc, D, out, S, layers):
    with ExitStack() as stack:
        def sb(n, sh, dt=F32):
            return stack.enter_context(nc.sbuf_tensor(n, sh, dt))
        T = {
            "x": sb("x_sb", [P, S.node_tiles, FEAT]),
            "a": sb("a_sb", [P, S.node_tiles]),
            "ident": sb("ident", [P, P]),
            "lower": sb("lower", [P, P]),
            "zero": sb("zero", [P, MSG]),
            "spare_i": sb("spare_i", [P, TG], I32),
            "spare": sb("spare", [P, TG]),
            "past": stack.enter_context(nc.semaphore("past")),
            "gathered_count": 0,
            "added_count": 0,
            "gathered": [stack.enter_context(nc.semaphore(f"gathered{b}")) for b in range(2)],
            "added": [stack.enter_context(nc.semaphore(f"added{t}")) for t in range(TG)],
            "bank": [stack.enter_context(nc.psum_tensor(f"bank{n}", [P, 512], F32)) for n in range(8)],
        }
        skip = sb("skip", [P, S.node_tiles, 192])

        def dram(n, sh, dt=F32):
            return nc.dram_tensor(n, sh, dt, kind="Internal").ap()
        agg = [dram(f"agg{q}", [S.agg_rows, MSG]) for q in range(COPIES)]
        agg_count = [dram(f"agg_count{q}", [S.agg_rows, MSG_COUNT]) for q in range(COPIES)]
        table, table_short = dram("table", [S.node_rows, WIDE]), dram("table_short", [S.node_rows, FEAT])
        load_constants(nc, T, D)
        if 0 in layers:
            node_pre(nc, T, D, S, "L0", D["L0_pre"], D["L0_pre_scale"], [table], WIDE, skip, True, agg)
            edge_pass(nc, T, D, S, "L0", [D["src_all"], D["dst_all"], D["dst_before"]], D["attr6"], D["dst_row"], D["attr64"][0:64, :], D["L0_fc1"], D["L0_fc2"],
                      table, agg, ACT.Silu, 1 / 8, True, True)
            node_post(nc, T, D, S, "L0", agg, D["L0_post"], D["L0_post_scale"], skip, True, True)
        if 1 in layers:
            node_pre(nc, T, D, S, "L1", D["L1_pre"], D["L1_pre_scale"], [table_short], FEAT, skip, True, agg_count)
            edge_pass(nc, T, D, S, "L1", [D["src_all"], D["dst_all"], D["dst_before"]], D["attr6"], D["dst_row"], D["attr16"], D["L1_fc1"], D["L1_fc2"],
                      table_short, agg_count, ACT.Silu, 1 / 4, False, True)
            node_post(nc, T, D, S, "L1", agg_count, D["L1_post"], D["L1_post_scale"], skip, False, True)
        direction6 = dram("direction6", [S.groups * P, 6 * TG])
        direction5 = dram("direction5", [S.groups * P, 5 * TG])
        if 2 in layers or 3 in layers:
            direction_phase(nc, D, S, direction6, direction5)
        if 2 in layers:
            agg2 = [dram(f"agg2{q}", [S.agg_rows, MSG2]) for q in range(COPIES)]
            table_s, table_d = dram("table_s", [S.node_rows, WIDE]), dram("table_d", [S.node_rows, WIDE])
            values = dram("values", [S.groups * P, TG * FEAT])
            by_head = dram("by_head", [HEADS, S.edge_rows])
            corner, carry = dram("corner", [P, 2]), dram("carry", [HEADS, P // HEADS])
            node_pre(nc, T, D, S, "L2", D["L2_pre"], D["L2_pre_scale"], [table_s, table_d], 2 * WIDE, skip, False, agg2, (D["L2_ln1"], D["L2_pre_b"]))
            with nc.sbuf_tensor("scores", [P, HEADS, S.tiles], F32) as scores:
                message_phase(nc, T, D, S, table_s, table_d, direction5, values, scores)
                softmax_phase(nc, T, D, S, scores, by_head, corner, carry)
                attend_phase(nc, T, D, S, values, scores, agg2)
            transformer_post(nc, T, D, S, agg2, skip)
        if 3 in layers:
            node_pre(nc, T, D, S, "L3", D["L3_pre"], D["L3_pre_scale"], [table], WIDE, skip, False, agg)
            edge_pass(nc, T, D, S, "L3", [D["dst_all"], D["src_all"], D["dst_before"]], direction6, D["src_row"], D["attr64"][0:64, :], D["L3_fc1"], D["L3_fc2"],
                      table, agg, ACT.Relu, 1.0, True, False)
            node_post(nc, T, D, S, "L3", agg, D["L3_post"], D["L3_post_scale"], skip, True, False)
        store_phase(nc, T, S, out)


def kron3(w):
    out = np.zeros((w.shape[0], 3, w.shape[1], 3), np.float32)
    for k in range(3):
        out[:, k, :, k] = w
    return out.reshape(3 * w.shape[0], 3 * w.shape[1])


def kron3_major(w):
    out = np.zeros((w.shape[0], 3, 3, w.shape[1]), np.float32)
    for k in range(3):
        out[:, k, k, :] = w
    return out.reshape(3 * w.shape[0], 3 * w.shape[1])


def pre_weights(ws_table, wv_table, ws_skip=None, wv_skip=None, wide=False):
    parts = [np.zeros((FEAT, NS), np.float32), np.zeros((FEAT, 3 * NV), np.float32)]
    parts[0][0:NS] = ws_table
    parts[1][NS:] = kron3_major(wv_table)
    if wide:
        parts.append(parts[1][:, 0:2 * NV])
    if ws_skip is not None:
        a = np.zeros((FEAT, ws_skip.shape[1]), np.float32)
        a[0:NS] = ws_skip
        b = np.zeros((FEAT, 3 * NV), np.float32)
        b[NS:] = kron3(wv_skip)
        parts += [a, b]
    return np.concatenate(parts, 1)


def post_weights(ws, wv, cross, extra=None):
    cols = ws.shape[1]
    out = np.zeros((MSG if cross else MSG_COUNT, cols + 3 * NV + (1 if extra is not None else 0)), np.float32)
    out[A0:D0, 0:cols] = ws[0:NS]
    out[D0:B0, 0:cols] = ws[NS:]
    for k in range(3):
        out[B0 + NS * k:B0 + NS * (k + 1), cols + k:cols + 96:3] = wv[0:NS]
        out[C0 + NV * k:C0 + NV * (k + 1), cols + k:cols + 96:3] = wv[NS:NS + NV]
        if cross:
            out[X0 + NV * k:X0 + NV * (k + 1), cols + k:cols + 96:3] = wv[NS + NV:]
    if extra is not None:
        out[A0:D0, -1:] = extra[0:NS]
        out[D0:B0, -1:] = extra[NS:]
    return out


def mid_scales(s, v, dot, cross, rows=MSG):
    out = np.full((rows, 1), v, np.float32)
    out[A0:D0] = s
    out[D0:B0] = s * dot
    out[X0:] = v * cross
    return out


def half_scales(s, v):
    return np.concatenate([np.full((NS, 1), s, np.float32), np.full((3 * NV, 1), v, np.float32)])


def rows_of(a, count, fill):
    out = np.full((count,) + a.shape[1:], fill, a.dtype)
    out[0:len(a)] = a
    return out


def by_group(a, S):
    k = a.shape[1]
    return np.ascontiguousarray(a.reshape(S.groups, TG, P, k).transpose(0, 2, 1, 3).reshape(S.groups * P, TG * k))


def weight_columns(w):
    return np.concatenate([w[:, 0:64], w[:, 160:192], w[:, 64:128], w[:, 128:160], w[:, 192:]], 1)


def layout(inputs, S):
    n = {k: np.asarray(v) for k, v in inputs.items()}
    a = {}
    a["x"] = rows_of(n["x"], S.node_rows, 0)
    a["node_vec1"] = rows_of(n["node_vec1"], S.node_rows, 0)
    last = S.node_rows - 1
    src, dst = (rows_of(n[k].reshape(-1, 1), S.edge_rows, last) for k in ("src", "dst"))
    gs, gd = by_group(src, S), by_group(dst, S)
    before = np.concatenate([np.full((S.tiles, 1), -1, np.int32), dst.reshape(S.tiles, P)[:, :-1]], 1)
    a["by_dst"] = np.concatenate([gs, gd, by_group(before.reshape(-1, 1), S)], 1)

    def by_tile(v):
        return np.concatenate([v.reshape(S.tiles, P).T, np.zeros((P, 2 * TG), np.int32)], 1)
    a["src_all"], a["dst_all"], a["dst_before"] = by_tile(src), by_tile(dst), by_tile(before)
    a["dst_row"], a["src_row"] = dst.reshape(1, -1), src.reshape(1, -1)
    e4 = rows_of(n["edge_attr_4"], S.edge_rows, 0)
    a["attr6"] = by_group(np.concatenate([e4, e4[:, 1:3]], 1), S)
    a["attr3"] = by_group(rows_of(n["edge_attr_3"], S.edge_rows, 1), S)
    e64 = rows_of(n["edge_attr_64"], S.edge_rows, 0).T
    a["attr64"] = np.concatenate([e64, np.ones((1, S.edge_rows), np.float32)])
    a["attr16"] = np.ascontiguousarray(rows_of(n["edge_attr_16"], S.edge_rows, 0).T)
    q = {k[7:]: v for k, v in n.items() if k.startswith("L0_gnn_")}
    a["L0_pre"] = pre_weights(q["lin1_ws"], q["lin1_wv"], q["sc_ws"], q["sc_wv"], True)
    a["L0_pre_scale"] = half_scales(NS ** -0.5, NV ** -0.5)
    a["L0_fc1"], a["L0_fc2"] = q["fc_w1"], weight_columns(q["fc_w2"])
    a["L0_post"] = post_weights(q["lin2_ws"], q["lin2_wv"], True)
    a["L0_post_scale"] = mid_scales(96 ** -0.5 / 32, 128 ** -0.5 / 32, 3 ** -0.5, 2 ** -0.5)
    q = {k[7:]: v for k, v in n.items() if k.startswith("L1_gnn_")}
    a["L1_pre"] = pre_weights(q["Wl1_0"], q["Wl1_1"], q["Wsc0"], q["Wsc1"])
    a["L1_pre_scale"] = a["L0_pre_scale"]
    a["L1_fc1"], a["L1_fc2"] = q["Wfc1"], weight_columns(q["Wfc2"])
    a["L1_post"] = post_weights(q["Wl2_s"], q["Wl2_v"], False, q["Wa"])
    a["L1_post_scale"] = mid_scales(96 ** -0.5 / 8, 96 ** -0.5 / 8, 3 ** -0.5, 1.0, MSG_COUNT)
    a["dst_wide"] = np.concatenate([np.full((1, 1), -1, np.int32), a["dst_row"], np.full((1, 1), -1, np.int32)], 1)
    q = {k[7:]: v for k, v in n.items() if k.startswith("L2_gnn_")}
    def wide(ws, wv):
        m = pre_weights(ws, wv)
        return np.concatenate([m, m[:, NS:NS + 2 * NV]], 1)
    a["L2_pre"] = np.concatenate([wide(q["msrc_ws"], q["msrc_wv"]), wide(q["mdst_ws"], q["mdst_wv"])], 1)
    a["L2_pre_scale"] = half_scales(1.0, 1.0)
    a["L2_pre_b"] = np.zeros((1, 2 * WIDE), np.float32)
    a["L2_pre_b"][0, WIDE:WIDE + NS] = q["mdst_bs"]

    def norm_rows(w0, b0, w1):
        return np.concatenate([w0, np.repeat(w1, 3), b0, np.zeros(3 * NV, np.float32)])[None]
    a["L2_ln1"] = norm_rows(q["ln1_w0"], q["ln1_b0"], q["ln1_w1"])
    a["L2_ln2"] = norm_rows(q["ln2_w0"], q["ln2_b0"], q["ln2_w1"])
    a["L2_rw1"] = np.concatenate([q["rw1"], q["rb1"][None]])
    a["L2_rw2"] = np.concatenate([q["rw2"], q["rb2"][None]])
    r3 = np.concatenate([q["rw3"], q["roff"][None]])
    a["L2_rw3"] = np.concatenate([r3[:, 0:128], r3[:, 160:224], r3[:, 128:160]], 1)
    a["L2_gb"] = np.stack([q["rg1"], q["rbe1"], q["rg2"], q["rbe2"]], 1)
    lin, sc = np.zeros((R_ + 1, 256), np.float32), np.ones((3 * P, 1), np.float32)
    lin[0:NS, 32:160] = q["lin_ws"][0:NS]
    lin[NS:2 * NS, 0:32] = q["lin_wv"][0:NS]
    lin[128:160, 32:160] = q["lin_ws"][NS:]
    sc[128:160] = 3 ** -0.5
    sc[160:256] = 2 ** -0.5
    for k in range(3):
        lin[256 + NV * k:288 + NV * k, 160 + NV * k:192 + NV * k] = q["lin_wv"][NS:NS + NV]
        lin[160 + NV * k:192 + NV * k, 160 + NV * k:192 + NV * k] = q["lin_wv"][NS + NV:]
    lin[R_, 32:160] = q["lin_bs"]
    a["L2_lin"], a["L2_lin_scale"] = lin, np.ascontiguousarray(sc.reshape(3, P).T)
    a["L2_dots"] = q["alpha_dot"].reshape(1, -1)
    def vec_rows(w):
        return kron3_major(w.T).T
    proj = np.zeros((FEAT, FEAT), np.float32)
    proj[0:NS, 0:NS] = q["proj_ws"]
    proj[NS:, NS:] = vec_rows(q["proj_wv"])
    a["L2_proj"] = proj
    a["L2_proj_b"] = np.zeros((1, FEAT), np.float32)
    a["L2_proj_b"][0, 0:NS] = q["proj_bs"]
    f1 = np.zeros((FEAT, 384), np.float32)
    f1[0:NS, 0:192] = q["f1_ws"]
    f1[NS:, 192:] = kron3_major(q["f1_wv"])
    a["L2_f1"] = f1
    a["L2_f1_b"] = np.zeros((1, 384), np.float32)
    a["L2_f1_b"][0, 0:192] = q["f1_bs"]
    f2 = np.zeros((320, FEAT), np.float32)
    f2[0:128, 0:NS] = q["f2_ws"]
    f2[128:, NS:] = vec_rows(q["f2_wv"])
    a["L2_f2"] = f2
    a["L2_f2_b"] = np.zeros((1, FEAT), np.float32)
    a["L2_f2_b"][0, 0:NS] = q["f2_bs"]
    q = {k[7:]: v for k, v in n.items() if k.startswith("L3_gnn_")}
    a["L3_pre"] = pre_weights(q["W_nl0"], q["W_nl1"], q["W_skip0"], q["W_skip1"], True)
    a["L3_pre_scale"] = half_scales(1.0, 1.0)
    a["L3_fc1"], a["L3_fc2"] = q["W_fc1"], weight_columns(q["W_fc2"])
    a["L3_post"] = post_weights(q["W_out_s"], q["W_out_v"], True)
    a["L3_post_scale"] = mid_scales(1 / 32, 1 / 32, 3 ** -0.5, 2 ** -0.5)
    return a


LAYERS = (0, 1, 2, 3)


def kernel(**inputs):
    from concourse import bacc
    from concourse.bass_utils import run_bass_kernel_spmd
    S = Shapes(inputs["x"].shape[0], inputs["src"].shape[0])
    arrays = {k: np.ascontiguousarray(v) for k, v in layout(inputs, S).items()}
    nc = bacc.Bacc("TRN2", target_bir_lowering=False, num_devices=1)
    D = {k: nc.dram_tensor(f"in_{k}", v.shape, mybir.dt.from_np(v.dtype), kind="ExternalInput").ap() for k, v in arrays.items()}
    D["shapes"] = S
    out = nc.dram_tensor("out_x", (S.nodes, FEAT), F32, kind="ExternalOutput").ap()
    build(nc, D, out, S, LAYERS)
    r = run_bass_kernel_spmd(nc, [{f"in_{k}": v for k, v in arrays.items()}], core_ids=[0])
    return r.results[0]["out_x"]
```
